# Optimizing a Trainium2 kernel written in Bass

```python
import numpy as np
import jax
import jax.numpy as jnp

def _softmax(x, axis=-1):
    return jax.nn.softmax(x, axis=axis)

def _gelu(x):
    return jax.nn.gelu(x, approximate=True)

def _silu(x):
    return jax.nn.silu(x)

def _sigmoid(x):
    return jax.nn.sigmoid(x)

def _layernorm(x, axis=-1, eps=1e-05):
    m = jnp.mean(x, axis=axis, keepdims=True)
    v = jnp.var(x, axis=axis, keepdims=True)
    return (x - m) / jnp.sqrt(v + eps)

def _scatter_add(tgt, idx, src, axis=0):
    return tgt.at[idx].add(src)

def _segment_sum(src, seg, n):
    return jax.ops.segment_sum(src, seg, n)
kernel_name = 'mk_macaron_d1_jaxref_r4_01f609'

def setup_inputs(seed: int=0):
    np.random.seed(seed)
    _w = jnp.asarray

    def _L0_attn_setup():
        import jax, jax.numpy as jnp
        import numpy as np
        HEAD_NUM = 16
        NEG_BIG = 1000000.0
        key = jax.random.key(seed)
        ks = jax.random.split(key, 5)
        E = 256
        B, S = (1, 1024)
        x = jax.random.normal(ks[0], (B, S, E), dtype=jnp.float32)
        W1 = jax.random.normal(ks[1], (E, 3 * E), dtype=jnp.float32) * (1.0 / np.sqrt(E))
        b1 = jax.random.normal(ks[2], (3 * E,), dtype=jnp.float32) * 0.02
        Wp = jax.random.normal(ks[3], (E, E), dtype=jnp.float32) * (1.0 / np.sqrt(E))
        bp = jax.random.normal(ks[4], (E,), dtype=jnp.float32) * 0.02
        return {'x': x, 'W1': W1, 'b1': b1, 'Wp': Wp, 'bp': bp}
    _L0_attn_in = _L0_attn_setup()

    def _L0_ffn_setup():
        import jax, jax.numpy as jnp
        import numpy as np
        NUM_EXPERTS = 8
        EXPERT_CAPACITY = 2.0
        key = jax.random.key(seed)
        k1, k2, k3, k4 = jax.random.split(key, 4)
        B, T, C, H, E = (4, 1024, 256, 1024, NUM_EXPERTS)
        x = jax.random.normal(k1, (B, T, C), jnp.float32)
        gate_w = jax.random.normal(k2, (C, E), jnp.float32) * 0.02
        w1 = jax.random.normal(k3, (E, C, H), jnp.float32) * 0.02
        w2 = jax.random.normal(k4, (E, H, C), jnp.float32) * 0.02
        return {'x': x, 'gate_w': gate_w, 'w1': w1, 'w2': w2}
    _L0_ffn_in = _L0_ffn_setup()
    _d = {'L0_attn_x': _L0_attn_in['x'], 'L0_attn_W1': _L0_attn_in['W1'], 'L0_attn_b1': _L0_attn_in['b1'], 'L0_attn_Wp': _L0_attn_in['Wp'], 'L0_attn_bp': _L0_attn_in['bp'], 'L0_ffn_gate_w': _L0_ffn_in['gate_w'], 'L0_ffn_w1': _L0_ffn_in['w1'], 'L0_ffn_w2': _L0_ffn_in['w2']}
    _x0 = _d['L0_attn_x']
    _d['L0_attn_x'] = jax.random.normal(jax.random.fold_in(jax.random.key(seed), 1), (4, 1024, 256), dtype=_x0.dtype)
    del _x0
    return _d

def reference(L0_attn_x, L0_attn_W1, L0_attn_b1, L0_attn_Wp, L0_attn_bp, L0_ffn_gate_w, L0_ffn_w1, L0_ffn_w2):

    def _L0_attn_ref(x, W1, b1, Wp, bp):
        import jax, jax.numpy as jnp
        import numpy as np
        HEAD_NUM = 16
        NEG_BIG = 1000000.0
        B, S, E = x.shape
        H = HEAD_NUM
        d = E // H
        dk = jnp.asarray(d, x.dtype) ** 0.5
        h = x @ W1 + b1
        h = jnp.swapaxes(h.reshape(B, S, H, 3 * d), 1, 2)
        q, k, v = (h[..., :d], h[..., d:2 * d], h[..., 2 * d:])
        w = jnp.einsum('bhqd,bhkd->bhqk', q, k) / dk
        mask = jnp.tril(jnp.ones((S, S), dtype=x.dtype))
        w = jax.nn.softmax(w * mask - (1.0 - mask) * NEG_BIG, axis=-1)
        a = jnp.einsum('bhqk,bhkd->bhqd', w, v)
        a = jnp.swapaxes(a, 1, 2).reshape(B, S, E)
        return a @ Wp + bp

    def _L0_ffn_ref(x, gate_w, w1, w2):
        import jax, jax.numpy as jnp
        import numpy as np
        NUM_EXPERTS = 8
        EXPERT_CAPACITY = 2.0
        B, T, C = x.shape
        E = gate_w.shape[1]
        cap = int(EXPERT_CAPACITY * T / E)
        scores = jnp.einsum('BTC,CE->BTE', x, gate_w)
        probs = jax.nn.softmax(scores, axis=-1)
        probs_et = jnp.transpose(probs, (0, 2, 1))
        top_p, top_idx = jax.lax.top_k(probs_et, cap)
        xin = jnp.take_along_axis(x[:, None, :, :], top_idx[..., None], axis=2)
        h = jax.nn.gelu(jnp.einsum('BElC,ECH->BElH', xin, w1), approximate=False)
        y = jnp.einsum('BElH,EHC->BElC', h, w2)
        y = y * top_p[..., None]
        b_idx = jnp.arange(B)[:, None, None]
        out = jnp.zeros((B, T, C), x.dtype).at[b_idx, top_idx].add(y)
        return out
    x = L0_attn_x
    x = x + 0.5 * _L0_ffn_ref(_layernorm(x, axis=-1), L0_ffn_gate_w, L0_ffn_w1, L0_ffn_w2)
    x = x + _L0_attn_ref(_layernorm(x, axis=-1), L0_attn_W1, L0_attn_b1, L0_attn_Wp, L0_attn_bp)
    x = x + 0.5 * _L0_ffn_ref(_layernorm(x, axis=-1), L0_ffn_gate_w, L0_ffn_w1, L0_ffn_w2)
    return x

_drawn_inputs = setup_inputs


def setup_inputs(seed=0):
    import zlib

    import numpy as np

    out = dict(_drawn_inputs(seed))
    spreads = {}
    factors = {'L0_attn_bp': 2.937}
    for name, (base, spread) in spreads.items():
        noise = np.random.default_rng([zlib.crc32(name.encode()), seed]).standard_normal(out[name].shape)
        drawn = base * np.exp(spread * noise) if base else spread * noise
        out[name] = jnp.asarray(drawn.astype(out[name].dtype))
    for name, factor in factors.items():
        out[name] = (out[name] * factor).astype(out[name].dtype)
    return out
```

```python
from contextlib import ExitStack

import concourse.bass as bass
from concourse import mybir

ALU = mybir.AluOpType
ACT = mybir.ActivationFunctionType
AX = mybir.AxisListType
F32 = mybir.dt.float32
F32R = mybir.dt.float32r
BF16 = mybir.dt.bfloat16
F16 = mybir.dt.float16
I32 = mybir.dt.int32
U32 = mybir.dt.uint32

P = 128
BANK = 512
LN_EPS = 1e-5
PROB_BITS = 30
ds = bass.ds


class Shapes:

    def __init__(self, x, gate_w, w1):
        self.B, self.T, self.C = x.shape
        self.E = gate_w.shape[1]
        self.H = w1.shape[2]
        self.CAP = 2 * self.T // self.E
        self.TT = self.T // P
        self.KC = self.C // P
        self.J = self.H // P
        self.BE = self.B * self.E
        self.ROW = self.C + self.E
        self.SH = self.CAP // P
        self.ST = self.B * self.SH
        self.U = 2 * self.E
        self.Q = self.ST // 2
        assert self.CAP == 2 * P and self.KC == 2 and self.ST == 8 and self.TT == 8 and self.E == 8


class Ring:

    def __init__(self, sem, depth):
        self.sem, self.depth = sem, depth

    def start(self, eng):
        eng.sem_inc(self.sem, self.depth)

    def wait_free(self, eng, k):
        eng.wait_ge(self.sem, k + 1)

    def emptied(self, ins):
        ins.then_inc(self.sem, 1)

    def wait_emptied(self, eng, k):
        eng.wait_ge(self.sem, k + 1 + self.depth)


class Chain:

    def __init__(self, eng, sem, base=0):
        self.eng, self.sem, self.base, self.n = eng, sem, base, 0

    def did(self, ins):
        ins.then_inc(self.sem, 1)
        self.n += 1

    def settle(self):
        self.eng.wait_ge(self.sem, self.base + self.n)

    def pause(self):
        self.settle()
        self.eng.sem_inc(self.sem, 1)
        self.n += 1



class Moments:

    DVE_STEPS = 3

    def __init__(self, s, sb, sem, tag):
        self.s = s
        self.stats = sb(f"stats{tag}", [P, s.TT, 6], F32)
        self.mv = sb(f"mean_var{tag}", [P, s.TT, 2], F32)
        self.ve = sb(f"var_eps{tag}", [P, s.TT], F32)
        self.rstd = sb(f"rstd{tag}", [P, s.TT], F32)
        self.dve = sem(f"norm_dve{tag}")
        self.var_ready = sem(f"var_ready{tag}")
        self.rstd_ready = sem(f"rstd_ready{tag}")


class Gate(Moments):

    DVE_STEPS = Moments.DVE_STEPS + 4

    def __init__(self, s, sb, sem, turn, score, tag, xT=None):
        super().__init__(s, sb, sem, tag)
        self.turn, self.score = turn, score
        self.row = sb(f"row{tag}", [P, s.TT, s.ROW], F32)
        self.xT = xT if xT is not None else sb(f"xT{tag}", [P, s.KC, s.T], F32)[:]
        self.top = sb(f"top{tag}", [P, s.TT], F32)
        self.sub = sb(f"sub{tag}", [P, s.TT, s.E], F32)
        self.ex = sb(f"ex{tag}", [P, s.TT, s.E], F32)
        self.tot = sb(f"tot{tag}", [P, s.TT], F32)
        self.inv = sb(f"inv{tag}", [P, s.TT], F32)
        self.row_ready = sem(f"row_ready{tag}")
        self.turned = sem(f"turned{tag}")
        self.turn_ring = Ring(sem(f"turn_free{tag}"), 2)
        self.score_ready = sem(f"score_ready{tag}")
        self.sub_ready = sem(f"sub_ready{tag}")
        self.ex_ready = sem(f"ex_ready{tag}")
        self.prob_ready = sem(f"prob_ready{tag}")
        self.table_out = sem(f"table_out{tag}")


def gate_stats(g, dve, chain, x):
    s = g.s
    for t in range(s.TT):
        last = dve.bn_stats(g.stats[:, t, :], x[:, t, :])
    chain.did(last)
    chain.pause()
    for t in range(s.TT):
        last = dve.bn_aggr(g.mv[:, t, :], g.stats[:, t, :])
    chain.did(last)
    chain.settle()
    dve.tensor_scalar(g.ve[:], g.mv[:, :, 1], LN_EPS, None, ALU.add).then_inc(g.var_ready, 1)


def gate_rstd(g, pool, b, power):
    pool.wait_ge(g.var_ready, b + 1)
    pool.tensor_tensor(g.rstd[:], g.ve[:], power[:], ALU.pow).then_inc(g.rstd_ready, 1)


def gate_rows(g, dve, b, x):
    s = g.s
    dve.wait_ge(g.rstd_ready, b + 1)
    dve.wait_ge(g.table_out, 16 * (b + 1))
    for t in range(s.TT):
        last = dve.tensor_scalar(g.row[:, t, 0:s.C], x[:, t, :], g.mv[:, t, 0:1], g.rstd[:, t:t + 1],
                                 ALU.subtract, ALU.mult)
    last.then_inc(g.row_ready, 1)


def gate_turn(g, pe, b, ident):
    s = g.s
    pe.wait_ge(g.row_ready, b + 1)
    for n in range(4):
        c, half = n // 2, n % 2
        g.turn_ring.wait_free(pe, 4 * b + n)
        for t in range(4):
            last = pe.transpose(g.turn[:, n % 2, t * P:(t + 1) * P],
                                g.row[:, 4 * half + t, c * P:(c + 1) * P], ident[:])
        last.then_inc(g.turned, 1)


def gate_score(g, pe, b, gate):
    s = g.s
    g.turn_ring.wait_emptied(pe, 4 * b + 3)
    for t in range(s.TT):
        for c in range(s.KC):
            last = pe.matmul(g.score[:, t, :], g.xT[:, c, t * P:(t + 1) * P], gate[:, c, :],
                             start=(c == 0), stop=(c == s.KC - 1))
    last.then_inc(g.score_ready, 1)


def gate_copy(g, act, b):
    act.wait_ge(g.score_ready, b + 1)
    for n in range(4):
        c, half = n // 2, n % 2
        act.wait_ge(g.turned, 4 * b + n + 1)
        g.turn_ring.emptied(act.activation(g.xT[:, c, half * BANK:(half + 1) * BANK],
                                           g.turn[:, n % 2, :], ACT.Copy))


def gate_exp(g, act, b):
    act.wait_ge(g.sub_ready, b + 1)
    act.activation(g.ex[:], g.sub[:], ACT.Exp).then_inc(g.ex_ready, 1)


def gate_softmax_front(g, dve, chain, b):
    s = g.s
    dve.wait_ge(g.score_ready, b + 2)
    chain.did(dve.tensor_reduce(g.top[:], g.score[:], AX.X, ALU.max))
    chain.settle()
    dve.tensor_tensor(g.sub[:], g.score[:], g.top[:].unsqueeze(2).to_broadcast([P, s.TT, s.E]),
                      ALU.subtract).then_inc(g.sub_ready, 1)


def gate_softmax_back(g, dve, chain, b, prob):
    s = g.s
    dve.wait_ge(g.ex_ready, b + 1)
    chain.did(dve.tensor_reduce(g.tot[:], g.ex[:], AX.X, ALU.add))
    chain.settle()
    chain.did(dve.reciprocal(g.inv[:], g.tot[:]))
    chain.settle()
    chain.did(dve.tensor_tensor(g.row[:, :, s.C:s.ROW], g.ex[:],
                                g.inv[:].unsqueeze(2).to_broadcast([P, s.TT, s.E]), ALU.mult))
    chain.settle()
    dve.tensor_copy(prob[:, ds(b * s.TT * s.E, s.TT * s.E)].rearrange("p (t e) -> p t e", t=s.TT),
                    g.row[:, :, s.C:s.ROW]).then_inc(g.prob_ready, 1)


def gate_table(g, sp, b, table):
    s = g.s
    sp.wait_ge(g.prob_ready, b + 1)
    dst = table.rearrange("(b t p) r -> b p t r", b=s.B, p=P)[b]
    sp.dma_start(dst, g.row[:]).then_inc(g.table_out, 16)


def gate_start(g, eng):
    eng.sem_inc(g.table_out, 16)
    eng.sem_inc(g.score_ready, 1)
    g.turn_ring.start(eng)


def norm_block(nc, s, c, x, table, acc, prob):
    with ExitStack() as ctx:
        sb = lambda n, sh, d: ctx.enter_context(nc.sbuf_tensor(n, sh, d))
        sem = c.sem
        turn = ctx.enter_context(nc.psum_tensor("turn_n", [P, 2, BANK], F32))
        score = ctx.enter_context(nc.psum_tensor("score_n", [P, s.TT, s.E], F32))
        g = Gate(s, sb, sem, turn, score, "_n")
        xin = sb("xin", [P, s.TT, s.C], F32)
        x_loaded, acc_init = sem("x_loaded"), sem("acc_init")
        xv = x.rearrange("b (t p) c -> b p t c", p=P)
        block = ctx.enter_context(nc.Block())

        @block.sync
        def _(sp):
            gate_start(g, sp)
            sp.dma_start(xin[:], xv[0]).then_inc(x_loaded, 16)
            sp.dma_start(c.gate[:], c.gate_w.rearrange("(k p) e -> p k e", p=P)).then_inc(c.gate_in, 16)
            sp.dma_start(acc, x.rearrange("b t c -> (b t) c")).then_inc(acc_init, 16)
            with sp.Fori(0, s.B - 1) as b:
                sp.wait_ge(g.row_ready, b + 1)
                sp.dma_start(xin[:], xv[b + 1]).then_inc(x_loaded, 16)
                gate_table(g, sp, b, table)
            gate_table(g, sp, s.B - 1, table)
            sp.wait_ge(acc_init, 16)
            sp.wait_ge(g.table_out, 16 * (s.B + 1))

        @block.gpsimd
        def _(pool):
            make_constants(nc, c, s, pool)
            with pool.Fori(0, s.B) as b:
                gate_rstd(g, pool, b, c.power)

        @block.tensor
        def _(pe):
            pe.wait_ge(c.made, c.MADE)
            pe.wait_ge(c.gate_in, 16)
            with pe.Fori(0, s.B) as b:
                gate_turn(g, pe, b, c.ident)
                gate_score(g, pe, b, c.gate)

        @block.scalar
        def _(act):
            with act.Fori(0, s.B) as b:
                gate_copy(g, act, b)
                gate_exp(g, act, b)

        @block.vector
        def _(dve):
            dve.wait_ge(c.made, c.MADE)
            convert_constants(nc, c, dve)
            with dve.Fori(0, s.B) as b:
                chain = Chain(dve, g.dve, b * g.DVE_STEPS)
                dve.wait_ge(x_loaded, 16 * (b + 1))
                gate_stats(g, dve, chain, xin)
                gate_rows(g, dve, b, xin)
                gate_softmax_front(g, dve, chain, b)
                gate_softmax_back(g, dve, chain, b, prob)
                assert chain.n == g.DVE_STEPS



class Constants:
    def __init__(self, nc, ctx, s, gate_w):
        sb = lambda n, sh, d: ctx.enter_context(nc.sbuf_tensor(n, sh, d))
        self.sem = lambda n: ctx.enter_context(nc.semaphore(n))
        self.gate_w = gate_w
        self.gate = sb("gate", [P, s.KC, s.E], F32)
        self.ident = sb("ident", [P, P], F32)
        self.identb = sb("identb", [P, P], BF16)
        self.ones = sb("ones", [P, P], BF16)
        self.upto = sb("upto", [P, P], BF16)
        self.later = sb("later", [P, P], BF16)
        self.slot_i = sb("slot_i", [P, s.CAP], I32)
        self.slot = sb("slot", [P, s.CAP], F16)
        self.tok_i = sb("tok_i", [P, s.TT], I32)
        self.tok = sb("tok", [P, s.TT], F16)
        self.first_i = sb("first_i", [P, s.B, s.SH], I32)
        self.first = sb("first", [P, s.B, s.SH], F32)
        self.shift = sb("shift", [P, PROB_BITS + 1], I32)
        self.one_i = sb("one_i", [P, PROB_BITS + 1], I32)
        self.bit_i = sb("bit_i", [P, PROB_BITS + 1], I32)
        self.bit_f = sb("bit_f", [P, PROB_BITS + 1], F32)
        self.power = sb("power", [P, s.TT], F32)
        self.blank = self.sem("blank")
        self.made = self.sem("made")
        self.gate_in = self.sem("gate_in")
        self.converted = self.sem("converted")

    MADE = 10


def make_constants(nc, c, s, pool):
    pool.memset(c.ident[:], 0.0).then_inc(c.blank, 1)
    pool.memset(c.identb[:], 0.0).then_inc(c.blank, 1)
    pool.memset(c.upto[:], 1.0).then_inc(c.blank, 1)
    pool.memset(c.later[:], 0.0).then_inc(c.blank, 1)
    pool.memset(c.ones[:], 1.0).then_inc(c.blank, 1)
    pool.memset(c.power[:], -0.5).then_inc(c.made, 1)
    pool.iota(c.shift[:, 0:PROB_BITS], pattern=[[-1, PROB_BITS]], base=PROB_BITS - 1, channel_multiplier=0)
    pool.memset(c.shift[:, PROB_BITS:], 0).then_inc(c.made, 1)
    pool.memset(c.one_i[:], 1).then_inc(c.made, 1)
    pool.wait_ge(c.blank, 5)
    for m in (c.ident, c.identb):
        pool.affine_select(out=m[:], in_=m[:], compare_op=ALU.not_equal, fill=1.0, base=0,
                           pattern=[[-1, P]], channel_multiplier=1).then_inc(c.made, 1)
    pool.affine_select(out=c.upto[:], in_=c.upto[:], compare_op=ALU.is_ge, fill=0.0, base=0,
                       pattern=[[1, P]], channel_multiplier=-1).then_inc(c.made, 1)
    pool.affine_select(out=c.later[:], in_=c.later[:], compare_op=ALU.is_ge, fill=-4e6, base=0,
                       pattern=[[-1, P]], channel_multiplier=1).then_inc(c.made, 1)
    pool.iota(c.slot_i[:], pattern=[[1, s.CAP]], base=1, channel_multiplier=0).then_inc(c.made, 1)
    pool.iota(c.tok_i[:], pattern=[[P, s.TT]], base=0, channel_multiplier=1).then_inc(c.made, 1)
    pool.iota(c.first_i[:], pattern=[[s.T, s.B], [0, s.SH]], base=0, channel_multiplier=0).then_inc(c.made, 1)


def convert_constants(nc, c, dve):
    dve.tensor_tensor(c.bit_i[:], c.one_i[:], c.shift[:], ALU.logical_shift_left).then_inc(c.converted, 1)
    dve.wait_ge(c.converted, 1)
    dve.tensor_copy(c.bit_f[:], c.bit_i[:]).then_inc(c.converted, 1)
    dve.tensor_copy(c.slot[:], c.slot_i[:]).then_inc(c.converted, 1)
    dve.tensor_copy(c.tok[:], c.tok_i[:]).then_inc(c.converted, 1)
    dve.tensor_copy(c.first[:], c.first_i[:]).then_inc(c.converted, 1)



def route_block(nc, s, c, prob, index, tag):
    B, E, TT, BE = s.B, s.E, s.TT, s.BE
    with ExitStack() as ctx:
        sb = lambda n, sh, d: ctx.enter_context(nc.sbuf_tensor(n + tag, sh, d))
        ps = lambda n, sh: ctx.enter_context(nc.psum_tensor(n + tag, sh, F32))
        sem = lambda n: c.sem(n + tag)
        thr = sb("thr", [P, BE], I32)
        trial = sb("trial", [P, BE], I32)
        add = sb("add", [P, BE], I32)
        over = sb("over", [P, B, TT, E], BF16)
        equal = sb("equal", [P, B, TT, E], BF16)
        need = sb("need", [P, BE], F32)
        fits = sb("fits", [P, B, TT, E], BF16)
        taken = sb("taken", [P, B, TT, E], BF16)
        rank = sb("rank", [P, E, B, TT], F32)
        hot = sb("hot", [P, 2, TT, s.CAP], F16)
        count = ps("count", [P, BANK])
        run = ps("run", [P, TT, BE])
        lists = ps("lists", [P, BANK])
        dve_s, tried, counted = sem("route_dve"), sem("tried"), sem("counted")
        hot_ready = sem("hot_ready")
        hot_ring = Ring(sem("hot_free"), 2)
        pv = prob[:].rearrange("p (b t e) -> p b t e", b=B, t=TT)

        def spread(v):
            return v.rearrange("p (b e) -> p b e", b=B).unsqueeze(2).to_broadcast([P, B, TT, E])

        def totals(pe, mask):
            for t in range(TT):
                last = pe.matmul(count[:, 0:BE], c.ones[:], mask[:, :, t, :], start=(t == 0), stop=(t == TT - 1))
            return last

        def running(pe, mask):
            for t in range(TT):
                for before in range(t):
                    pe.matmul(run[:, t, :], c.ones[:], mask[:, :, before, :], start=(before == 0), stop=False)
                last = pe.matmul(run[:, t, :], c.upto[:], mask[:, :, t, :], start=(t == 0), stop=True)
            return last

        block = ctx.enter_context(nc.Block())

        @block.vector
        def _(dve):
            chain = Chain(dve, dve_s)
            dve.memset(thr[:], 0)
            chain.did(dve.memset(trial[:], 1 << (PROB_BITS - 1)))
            chain.settle()
            before, STEPS = chain.n, 3
            with dve.Fori(0, PROB_BITS) as k:
                chain = Chain(dve, dve_s, before + STEPS * k)
                dve.tensor_tensor(over[:], pv, spread(trial[:].bitcast(F32)), ALU.is_ge).then_inc(tried, 1)
                dve.wait_ge(counted, k + 1)
                chain.did(dve.tensor_scalar(add[:], count[:, 0:BE], float(s.CAP), c.bit_f[:, ds(k, 1)],
                                            ALU.is_ge, ALU.mult))
                chain.settle()
                chain.did(dve.scalar_tensor_tensor(trial[:], add[:], c.bit_i[:, ds(k + 1, 1)], thr[:],
                                                   ALU.bitwise_or, ALU.bitwise_or))
                chain.settle()
                chain.did(dve.tensor_tensor(thr[:], thr[:], add[:], ALU.bitwise_or))
                assert chain.n == STEPS
            chain = Chain(dve, dve_s, before + STEPS * PROB_BITS)
            chain.settle()
            dve.tensor_tensor(over[:], pv, spread(thr[:].bitcast(F32)), ALU.is_gt)
            dve.tensor_tensor(equal[:], pv, spread(thr[:].bitcast(F32)), ALU.is_equal).then_inc(tried, 1)
            dve.wait_ge(counted, PROB_BITS + 1)
            chain.did(dve.tensor_scalar(need[:], count[:, 0:BE], -1.0, float(s.CAP), ALU.mult, ALU.add))
            chain.settle()
            chain.did(dve.tensor_tensor(fits[:], run[:].rearrange("p t (b e) -> p b t e", b=B), spread(need[:]), ALU.is_le))
            chain.settle()
            chain.did(dve.tensor_tensor(taken[:], fits[:], equal[:], ALU.mult))
            chain.settle()
            dve.tensor_tensor(fits[:], taken[:], over[:], ALU.add).then_inc(tried, 1)
            dve.wait_ge(counted, PROB_BITS + 2)
            chain.did(dve.tensor_tensor(rank[:].rearrange("p e b t -> p b t e"),
                                        run[:].rearrange("p t (b e) -> p b t e", b=B), fits[:], ALU.mult))
            chain.settle()
            with dve.Fori(0, E) as e:
                for b in range(B):
                    k = e * B + b
                    hot_ring.wait_free(dve, k)
                    for t in range(TT):
                        last = dve.tensor_scalar(hot[:, b % 2, t, :], c.slot[:],
                                                 rank[:].rearrange("p e b t -> p (e b t)")[:, ds(k * TT + t, 1)],
                                                 None, ALU.is_equal)
                    last.then_inc(hot_ready, 1)
            hot_ring.wait_emptied(dve, BE - 1)
            dve.tensor_tensor(index[:].rearrange("p (e k) -> p e k", e=E),
                              lists[:, 0:E * s.ST].rearrange("p (e k) -> p e k", e=E),
                              c.first[:].rearrange("p b h -> p (b h)").unsqueeze(1).to_broadcast([P, E, s.ST]),
                              ALU.add)

        @block.tensor
        def _(pe):
            hot_ring.start(pe)
            with pe.Fori(0, PROB_BITS) as k:
                pe.wait_ge(tried, k + 1)
                totals(pe, over).then_inc(counted, 1)
            pe.wait_ge(tried, PROB_BITS + 1)
            totals(pe, over)
            running(pe, equal).then_inc(counted, 1)
            pe.wait_ge(tried, PROB_BITS + 2)
            running(pe, fits).then_inc(counted, 1)
            with pe.Fori(0, E) as e:
                for b in range(B):
                    pe.wait_ge(hot_ready, e * B + b + 1)
                    for h in range(s.SH):
                        for t in range(TT):
                            last = pe.matmul(lists[:, ds(e * s.ST + b * s.SH + h, 1)],
                                             hot[:, b % 2, t, h * P:(h + 1) * P], c.tok[:, t:t + 1],
                                             start=(t == 0), stop=(t == TT - 1))
                    hot_ring.emptied(last)



def experts_block(nc, s, c, w1, w2, table, acc, index, tag):
    J, KC, Q, U, C, H = s.J, s.KC, s.Q, s.U, s.C, s.H
    W = Q * P
    WP = KC * H // J
    FIRST, LOOP = 2, 4
    LOOPS = (U - 2 * FIRST) // LOOP
    with ExitStack() as ctx:
        sb = lambda n, sh, d: ctx.enter_context(nc.sbuf_tensor(n + tag, sh, d))
        ps = lambda n, sh: ctx.enter_context(nc.psum_tensor(n + tag, sh, F32))
        sem = lambda n: c.sem(n + tag)
        w1_in = sb("w1_in", [P, KC, H], F32)
        w2_in = sb("w2_in", [P, J, C], F32)
        w1_hi, w1_lo = (sb(n, [P, 2, KC, H], F32R) for n in ("w1_hi", "w1_lo"))
        w2_hi, w2_lo = (sb(n, [P, 2, J, C], F32R) for n in ("w2_hi", "w2_lo"))
        rows = sb("rows", [P, 2, Q, s.ROW], F32)
        xT_hi, xT_lo = (sb(n, [P, 2, KC, W], F32R) for n in ("xs_hi", "xs_lo"))
        act_f = sb("act_f", [P, 2, W], F32)
        h_hi, h_lo = (sb(n, [P, 2, J, W], F32R) for n in ("h_hi", "h_lo"))
        gain = sb("gain", [P, 4, Q], F32)
        y = sb("y", [P, 2, Q, C], F32)
        lists = sb("slots", [P, 4, Q], U32)
        turn = ps("turn", [P, KC, BANK])
        up = ps("up", [P, 4, BANK])
        down = ps("down", [P, 2, BANK])

        w1_loaded, w2_loaded = sem("w1_loaded"), sem("w2_loaded")
        w1_hi_ready, w1_ready = sem("w1_hi_ready"), sem("w1_ready")
        w2_hi_ready, w2_ready = sem("w2_hi_ready"), sem("w2_ready")
        list_ready, pool_steps = sem("list_ready"), sem("pool_steps")
        gathered = [sem(f"gathered{k}") for k in range(2)]
        added = [sem(f"added{k}") for k in range(2)]
        turned, xs_hi_ready, gained = sem("turned"), sem("xs_hi_ready"), sem("gained")
        up_done, h_hi_ready, down_done = sem("up_done"), sem("h_hi_ready"), sem("down_done")
        turn_ring = Ring(sem("xs_ready"), KC)
        up_ring = Ring(sem("gelu_done"), 4)
        act_ring = Ring(sem("h_ready"), 2)
        down_ring = Ring(sem("y_ready"), 2)

        def dma_total(u, k):
            return 8 * Q * (u - k % 2) + 16 * Q

        def added_total(u, k):
            return dma_total(u, k) + 16 * Q

        def splits(u, k):
            return (J // 2) * (u - k % 2) + J

        def expert(u, k):
            return u // 2 if isinstance(u, int) else (u - k % 2) // 2

        def piece(weights_in, hi, lo, k, j):
            flat = lambda v: v.rearrange("p a b -> p (a b)")[:, j * WP:(j + 1) * WP]
            return flat(weights_in[:]), flat(hi[:, k]), flat(lo[:, k])

        def steps(eng, body):
            for u in range(FIRST):
                body(u, u)
            with eng.Fori(0, LOOPS) as i:
                for k in range(LOOP):
                    body(LOOP * i + (FIRST + k), (FIRST + k) % LOOP)
            for u in range(U - FIRST, U):
                body(u, u % LOOP)

        def hold(pool, sem, value):
            pool.wait_ge(sem, value)
            pool.sem_inc(pool_steps, 1)

        def known(u):
            return isinstance(u, int)

        def at_least(u, least):
            return u >= least if isinstance(u, int) else least <= FIRST

        def before(u, end):
            return u < end if isinstance(u, int) else True

        block = ctx.enter_context(nc.Block())

        @block.sync
        def _(sp):
            w1_v = w1.rearrange("e (k p) h -> e p k h", p=P)
            w2_v = w2.rearrange("e (j p) n -> e p j n", p=P)
            sp.dma_start(w1_in[:], w1_v[0]).then_inc(w1_loaded, 16)
            sp.dma_start(w2_in[:], w2_v[0]).then_inc(w2_loaded, 16)
            with sp.Fori(0, s.E - 1) as e:
                sp.wait_ge(w1_ready, J * (e + 1))
                sp.dma_start(w1_in[:], w1_v[e + 1]).then_inc(w1_loaded, 16)
                sp.wait_ge(w2_ready, J * (e + 1))
                sp.dma_start(w2_in[:], w2_v[e + 1]).then_inc(w2_loaded, 16)

        @block.gpsimd
        def _(pool):
            down_ring.start(pool)
            act_ring.start(pool)
            up_ring.start(pool)
            turn_ring.start(pool)

            def gather(u, k, reused=True):
                if at_least(u, 2):
                    pool.wait_ge(added[k % 2], added_total(u - 4, k))
                pool.tensor_copy(lists[:, k % 4, :], index[:, ds(u * Q, Q)]).then_inc(list_ready, 1)
                if reused:
                    pool.wait_ge(turned, KC * (u - 1))
                    pool.wait_ge(gained, u - 1)
                hold(pool, list_ready, u + 1)
                for q in range(Q):
                    pool.indirect_dma_start(rows[:, k % 2, q, :], None, table,
                                            bass.IndirectOffsetOnAxis(lists[:, k % 4, q:q + 1], 0)
                                            ).then_inc(gathered[k % 2], 16)

            def add(u, k):
                pool.wait_ge(added[k % 2], added_total(u - 2, k))
                for q in range(Q):
                    hold(pool, down_ring.sem, Q * u + q + 1 + down_ring.depth)
                    pool.indirect_dma_start(acc, bass.IndirectOffsetOnAxis(lists[:, k % 4, q:q + 1], 0),
                                            y[:, k % 2, q, :], None, compute_op=ALU.add
                                            ).then_inc(added[k % 2], 16)

            def body(u, k):
                if before(u, U - 2):
                    gather(u + 2, (k + 2) % LOOP)
                if at_least(u, 1):
                    add(u - 1, (k - 1) % LOOP)

            for k in range(2):
                pool.dma_start(y[:, k, 0, :], acc[0:P, :]).then_inc(added[k], 16 * Q)
                gather(k, k, reused=False)
            steps(pool, body)
            add(U - 1, (U - 1) % LOOP)
            for k in range(2):
                pool.wait_ge(added[k], added_total(U - 2 + k, k))

        @block.tensor
        def _(pe):
            def turn_rows(u, k):
                pe.wait_ge(gathered[k % 2], dma_total(u, k))
                for kc in range(KC):
                    turn_ring.wait_free(pe, KC * u + kc)
                    for q in range(Q):
                        last = pe.transpose(turn[:, kc, q * P:(q + 1) * P],
                                            rows[:, k % 2, q, kc * P:(kc + 1) * P], c.ident[:])
                    last.then_inc(turned, 1)

            def multiply_up(u, k):
                b, eb = k % 2, k // 2
                turn_ring.wait_emptied(pe, KC * u + KC - 1)
                pe.wait_ge(w1_ready, splits(u, k))
                for j in range(J):
                    up_ring.wait_free(pe, J * u + j)
                    terms = [(w, x, kc) for kc in range(KC)
                             for w, x in ((w1_hi, xT_hi), (w1_hi, xT_lo), (w1_lo, xT_hi))]
                    for n, (w, x, kc) in enumerate(terms):
                        last = pe.matmul(up[:, j % 4, :], w[:, eb, kc, j * P:(j + 1) * P], x[:, b, kc, :],
                                         start=(n == 0), stop=(n == len(terms) - 1))
                    last.then_inc(up_done, 1)

            def multiply_down(u, k):
                b, eb = k % 2, k // 2
                act_ring.wait_emptied(pe, J * u + J - 1)
                pe.wait_ge(w2_ready, splits(u, k))
                for q in range(Q):
                    down_ring.wait_free(pe, Q * u + q)
                    terms = [(h, w, j) for j in range(J)
                             for h, w in ((h_hi, w2_hi), (h_hi, w2_lo), (h_lo, w2_hi))]
                    for n, (h, w, j) in enumerate(terms):
                        last = pe.matmul(down[:, q % 2, 0:C], h[:, b, j, q * P:(q + 1) * P], w[:, eb, j, :],
                                         start=(n == 0), stop=(n == len(terms) - 1))
                    last.then_inc(down_done, 1)

            def body(u, k):
                if before(u, U - 1):
                    turn_rows(u + 1, (k + 1) % LOOP)
                multiply_up(u, k)
                if at_least(u, 1):
                    multiply_down(u - 1, (k - 1) % LOOP)

            turn_rows(0, 0)
            steps(pe, body)
            multiply_down(U - 1, (U - 1) % LOOP)

        @block.scalar
        def _(act):
            def rows_hi(u, k, reused=True):
                if reused:
                    act.wait_ge(up_done, J * (u - 1))
                for kc in range(KC):
                    act.wait_ge(turned, KC * u + kc + 1)
                    act.activation(xT_hi[:, k % 2, kc, :], turn[:, kc, :], ACT.Copy).then_inc(xs_hi_ready, 1)

            def w1_piece(e, eb, j):
                act.wait_ge(w1_loaded, 16 * (e + 1))
                whole, hi, _ = piece(w1_in, w1_hi, w1_lo, eb, j)
                act.activation(hi, whole, ACT.Copy).then_inc(w1_hi_ready, 1)

            def w2_piece(e, eb, j):
                act.wait_ge(w2_loaded, 16 * (e + 1))
                whole, hi, _ = piece(w2_in, w2_hi, w2_lo, eb, j)
                act.activation(hi, whole, ACT.Copy).then_inc(w2_hi_ready, 1)

            def body(u, k):
                if before(u, U - 1):
                    rows_hi(u + 1, (k + 1) % LOOP, reused=at_least(u, 1))
                for j in range(J):
                    act.wait_ge(up_done, J * u + j + 1)
                    act_ring.wait_free(act, J * u + j)
                    up_ring.emptied(act.activation(act_f[:, j % 2, :], up[:, j % 4, :], ACT.Gelu))
                    if before(u, U - 2):
                        e = expert(u, k) + 1
                        if k % 2 == 0:
                            w1_piece(e, (k // 2 + 1) % 2, j)
                        else:
                            if j == 0 and at_least(u, 2):
                                act.wait_ge(down_done, Q * (u - 1))
                            w2_piece(e, (k // 2 + 1) % 2, j)

            for j in range(J):
                w1_piece(0, 0, j)
            for j in range(J):
                w2_piece(0, 0, j)
            rows_hi(0, 0, reused=False)
            steps(act, body)

        @block.vector
        def _(dve):
            def rows_lo(u, k, reused=True):
                for kc in range(KC):
                    dve.wait_ge(xs_hi_ready, KC * u + kc + 1)
                    turn_ring.emptied(dve.tensor_tensor(xT_lo[:, k % 2, kc, :], turn[:, kc, :],
                                                        xT_hi[:, k % 2, kc, :].bitcast(F32), ALU.subtract))
                dve.wait_ge(gathered[k % 2], dma_total(u, k))
                if reused:
                    down_ring.wait_emptied(dve, Q * (u - 3) - 1)
                dve.tensor_scalar(gain[:, k, :], rows[:, k % 2, :, ds(C + expert(u, k), 1)].rearrange("p q a -> p (q a)"),
                                  0.5, None, ALU.mult).then_inc(gained, 1)

            def w1_piece(e, eb, j):
                dve.wait_ge(w1_hi_ready, J * e + j + 1)
                whole, hi, lo = piece(w1_in, w1_hi, w1_lo, eb, j)
                dve.tensor_tensor(lo, whole, hi.bitcast(F32), ALU.subtract).then_inc(w1_ready, 1)

            def w2_piece(e, eb, j):
                dve.wait_ge(w2_hi_ready, J * e + j + 1)
                whole, hi, lo = piece(w2_in, w2_hi, w2_lo, eb, j)
                dve.tensor_tensor(lo, whole, hi.bitcast(F32), ALU.subtract).then_inc(w2_ready, 1)

            def scale(u, k):
                dve.wait_ge(gained, u + 1)
                dve.wait_ge(added[k % 2], added_total(u - 2, k))
                for q in range(Q):
                    dve.wait_ge(down_done, Q * u + q + 1)
                    down_ring.emptied(dve.tensor_scalar(y[:, k % 2, q, :], down[:, q % 2, 0:C],
                                                        gain[:, k, q:q + 1], None, ALU.mult))

            def body(u, k):
                if before(u, U - 1):
                    rows_lo(u + 1, (k + 1) % LOOP, reused=not (known(u) and u < 3))
                for j in range(J):
                    if j == 0 and not (known(u) and u < 2):
                        dve.wait_ge(down_done, Q * (u - 1))
                    up_ring.wait_emptied(dve, J * u + j)
                    dve.tensor_copy(h_hi[:, k % 2, j, :], act_f[:, j % 2, :]).then_inc(h_hi_ready, 1)
                    if before(u, U - 2):
                        e = expert(u, k) + 1
                        (w1_piece if k % 2 == 0 else w2_piece)(e, (k // 2 + 1) % 2, j)
                    dve.wait_ge(h_hi_ready, J * u + j + 1)
                    act_ring.emptied(dve.tensor_tensor(h_lo[:, k % 2, j, :], act_f[:, j % 2, :],
                                                       h_hi[:, k % 2, j, :].bitcast(F32), ALU.subtract))
                if at_least(u, 1):
                    scale(u - 1, (k - 1) % LOOP)

            for j in range(J):
                w1_piece(0, 0, j)
            for j in range(J):
                w2_piece(0, 0, j)
            rows_lo(0, 0, reused=False)
            steps(dve, body)
            scale(U - 1, (U - 1) % LOOP)



class Slots:

    def __init__(self, ring, filled, order, b):
        assert len(order) % ring.depth == 0, len(order)
        self.ring, self.filled, self.order, self.base = ring, filled, order, b * len(order)

    def fill(self, pe, what):
        k = self.order.index(what)
        self.ring.wait_free(pe, self.base + k)
        return k % self.ring.depth

    def take(self, eng, what):
        k = self.order.index(what)
        eng.wait_ge(self.filled, self.base + k + 1)
        return k % self.ring.depth

    def wait_emptied(self, eng, what):
        self.ring.wait_emptied(eng, self.base + self.order.index(what))


def attention_block(nc, s, c, x1, W1, b1, Wp, bp, x2, table, prob):
    B, T, C, TT, KC = s.B, s.T, s.C, s.TT, s.KC
    NH, G, D = 16, 4, 16
    HG = NH // G
    PART = 3 * D
    ROWS = 4 * D
    STACKING = 16 * (2 * 4 * G + 1)
    VW = D + 1
    HALF = BANK
    HT = HALF // P
    SCALE = 1.0 / D ** 0.5
    NS = 3
    SETS = [(half, kt) for half in range(2) for kt in range(HT * (half + 1))]
    N = len(SETS)
    MAXES = [(h, qt, k0, min(k0 + BANK, (qt + 1) * P))
             for h in range(G) for qt in range(TT) for k0 in range(0, (qt + 1) * P, BANK)]
    PER_SET = 5

    def maxes(i):
        return MAXES[PER_SET * i:PER_SET * (i + 1)]

    def end_of(half):
        return HT - 1 if half == 0 else N - 1

    def steps():
        for hg in range(HG):
            for i in range(N):
                yield hg, i, ((hg - 1, 1) if i == 2 and hg else (hg, 0) if i == HT + 2 else None)

    TURNS = [(ch, half) for ch in range(KC) for half in range(2)]
    A_ORDER = [("x", n) for n in TURNS]
    for hg in range(HG):
        A_ORDER += [("qk", hg, half) for half in range(2)]
        if hg == 0:
            A_ORDER += [("v", t) for t in range(TT)]
    A_ORDER += [("max", 0) + m for m in MAXES] + [("top", 0)]
    for hg, i, out in steps():
        if hg + 1 < HG:
            A_ORDER += [("max", hg + 1) + m for m in maxes(i)]
            if i == N - 2:
                A_ORDER += [("top", hg + 1)]
        if out:
            A_ORDER += [("out", out)]
    A_ORDER += [("out", (HG - 1, 1))] + [("att", n) for n in TURNS] + [("proj", t) for t in range(TT)] + [("score",)]
    B_ORDER = [(hg, i, h) for hg in range(HG) for i in range(N) for h in range(G)]
    O_ORDER = [("out", (hg, half)) for hg in range(HG) for half in range(2)] + [("row", n) for n in TURNS]

    with ExitStack() as ctx:
        sb = lambda n, sh, d: ctx.enter_context(nc.sbuf_tensor(n + "_a", sh, d))
        ps = lambda n, sh: ctx.enter_context(nc.psum_tensor(n + "_a", sh, F32))
        sem = lambda n: c.sem(n + "_a")
        bankA, bankB, bankO = ps("bankA", [P, 3, BANK]), ps("bankB", [P, 3, BANK]), ps("bankO", [P, 2, BANK])
        gsb = lambda n, sh, d: ctx.enter_context(nc.sbuf_tensor(n, sh, d))
        m1 = Moments(s, gsb, c.sem, "_x1")
        xin = sb("xin", [P, TT, C], F32)
        att = sb("att", [P, TT, C], F32)
        xT_hi, xT_lo = sb("aT_hi", [P, KC, T], F32R), sb("aT_lo", [P, KC, T], F32R)
        wqk_hi, wqk_lo = (sb(n, [P, KC, HG, P], F32R) for n in ("wqk_hi", "wqk_lo"))
        wv_hi, wv_lo = (sb(n, [P, KC, NH, D], F32R) for n in ("wv_hi", "wv_lo"))
        wp_hi, wp_lo = (sb(n, [P, KC, C], F32R) for n in ("wp_hi", "wp_lo"))
        bqk = sb("bqk", [P, HG], F32)
        bv = sb("bv", [P, NH, D], F32)
        bo = sb("bo", [P, C], F32)
        qk_hi, qk_lo = (sb(n, [P, 2, T], F32R) for n in ("qk_hi", "qk_lo"))
        sq, sk = (sb(n, [P, NS, G, T], F32R) for n in ("sq", "sk"))
        val = sb("val", [P, TT, NH * VW + 16], F32)
        ex = sb("expo", [P, 2, G, BANK], F32)
        g = Gate(s, gsb, c.sem, None, None, "_a", xT=ex[:, 0].rearrange("p (k h) q -> p k (h q)", k=KC))
        oT = sb("oT", [P, T], F32)
        tops = sb("tops", [P, G, TT, 2], F32)
        ntop = sb("ntop", [P, G * TT], F32)
        ntopT = sb("ntopT", [G * TT, P], F32R)
        inv = sb("invs", [P, 2, HT, G], F32)

        A_filled, B_filled, O_filled = sem("A_filled"), sem("B_filled"), sem("O_filled")
        ringA, ringB, ringO = Ring(sem("A_free"), 3), Ring(sem("B_free"), 3), Ring(sem("O_free"), 2)
        w_loaded, w_hi_ready, w_ready, b_loaded, filled, padded = (
            sem(n) for n in ("w_loaded", "w_hi_ready", "w_ready", "b_loaded", "filled", "padded"))
        x_loaded, an_ready, hi_ready = (sem(n) for n in ("x_loaded", "an_ready", "hi_ready"))
        stacked, top_in = [sem(f"stacked{k}") for k in range(NS)], [sem(f"top_in{k}") for k in range(NS)]
        ntop_ready, masked, ex_used = (sem(n) for n in ("ntop_ready", "masked", "ex_used"))
        att_dve, att_ready, pool_steps, biased, x2_ready, x2_out = (
            sem(n) for n in ("att_dve", "att_ready", "pool_steps", "biased", "x2_ready", "x2_out"))
        HI_PER = 2 * len(TURNS) + 2 * HG
        DIAG = 2 * HT

        def slots(b):
            return (Slots(ringA, A_filled, A_ORDER, b), Slots(ringB, B_filled, B_ORDER, b),
                    Slots(ringO, O_filled, O_ORDER, b))

        def turns(hg, b):
            return b * len(range(hg % NS, HG, NS)) + hg // NS + 1

        def cols(i):
            half, kt = SETS[i]
            return max(kt - HT * half, 0) * P

        def crosses(i):
            half, kt = SETS[i]
            return kt + 1 if kt >= HT * half else 0

        flat = g.row[:].rearrange("p t r -> p (t r)")
        W1_in = flat[:, 0:KC * PART * NH].rearrange("p (k h r) -> p k h r", k=KC, r=PART)
        Wp_in = flat[:, KC * PART * NH:KC * (PART * NH + C)].rearrange("p (k n) -> p k n", k=KC)
        SPLITS = [(W1_in[:, k, :, 0:2 * D], *(w[:, k].rearrange("p a (g r) -> p (a g) r", g=G) for w in (wqk_hi, wqk_lo)))
                  for k in range(KC)]
        SPLITS += [(W1_in[:, k, :, 2 * D:PART], wv_hi[:, k], wv_lo[:, k]) for k in range(KC)]
        SPLITS += [(Wp_in[:, k], wp_hi[:, k], wp_lo[:, k]) for k in range(KC)]
        block = ctx.enter_context(nc.Block())

        @block.sync
        def _(sp):
            for r in (ringA, ringB, ringO):
                r.start(sp)
            sp.sem_inc(g.table_out, 16)
            sp.sem_inc(x2_out, 16)
            x1_v = x1.rearrange("(b t p) c -> b p t c", b=B, p=P)
            x2_v = x2.rearrange("(b t p) c -> b p t c", b=B, p=P)
            sp.dma_start(xin[:], x1_v[0]).then_inc(x_loaded, 16)
            sp.dma_start(W1_in.rearrange("p k h r -> p k (h r)"), W1.rearrange("(k p) n -> p k n", p=P)).then_inc(w_loaded, 16)
            sp.dma_start(Wp_in, Wp.rearrange("(k p) n -> p k n", p=P)).then_inc(w_loaded, 16)
            with nc.allow_non_contiguous_dma(reason="biases, a few hundred bytes each"):
                for h in range(NH):
                    sp.dma_start(bqk[32 * (h % G):32 * (h % G) + 2 * D, h // G:h // G + 1],
                                 b1[PART * h:PART * h + 2 * D].unsqueeze(1)).then_inc(b_loaded, 16)
                sp.dma_start(bv[:], b1.rearrange("(h r) -> h r", h=NH)[:, 2 * D:PART].unsqueeze(0).to_broadcast([P, NH, D])
                             ).then_inc(b_loaded, 16)
                sp.dma_start(bo[:], bp.unsqueeze(0).to_broadcast([P, C])).then_inc(b_loaded, 16)
            sp.wait_ge(filled, 2)
            sp.wait_ge(padded, 1)

            def stack(hg, b, A):
                k, q = hg % NS, hg % 2
                A.wait_emptied(sp, ("qk", hg, 1))
                if hg >= NS:
                    sp.wait_ge(ex_used, N * (HG * b + hg - NS + 1))
                sp.dma_start(sq[ROWS:ROWS + 1, k, :, :].bitcast(F32), sk[ROWS + 1:ROWS + 2, k, :, :].bitcast(F32)).then_inc(stacked[k], 16)
                for h in range(G):
                    lo, mid, up = 32 * h, 32 * h + D, 32 * h + 2 * D
                    for n, part in enumerate((qk_hi, qk_lo, qk_hi, qk_lo)):
                        sp.dma_start(sq[n * D:(n + 1) * D, k, h, :].bitcast(F32), part[lo:mid, q, :].bitcast(F32)).then_inc(stacked[k], 16)
                    for n, part in enumerate((qk_hi, qk_hi, qk_lo, qk_lo)):
                        sp.dma_start(sk[n * D:(n + 1) * D, k, h, :].bitcast(F32), part[mid:up, q, :].bitcast(F32)).then_inc(stacked[k], 16)

            def top_rows(hg, A):
                k = hg % NS
                A.wait_emptied(sp, ("top", hg))
                sp.dma_start(sq[ROWS:ROWS + 1, k, :, :].bitcast(F32).rearrange("p g (t q) -> p (g t) q", q=P),
                             ntopT[:].bitcast(F32)).then_inc(top_in[k], 16)

            with sp.Fori(0, B) as b:
                A, _, _ = slots(b)
                for hg in range(NS):
                    stack(hg, b, A)
                for hg in range(HG):
                    top_rows(hg, A)
                    if hg >= 1 and hg + NS - 1 < HG:
                        stack(hg + NS - 1, b, A)
                sp.wait_ge(x2_ready, TT * (b + 1))
                sp.dma_start(x2_v[b], att[:]).then_inc(x2_out, 16)
                sp.dma_start(xin[:], x1_v[(b + 1) % B]).then_inc(x_loaded, 16)
                gate_table(g, sp, b, table)
            sp.wait_ge(x2_out, 16 * (B + 1))
            sp.wait_ge(g.table_out, 16 * (B + 1))
            sp.wait_ge(x_loaded, 16 * (B + 1))

        @block.gpsimd
        def _(pool):
            pool.memset(sk[ROWS:P, :, :, :].bitcast(F32), 0.0).then_inc(filled, 1)
            pool.wait_ge(filled, 1)
            pool.memset(sk[ROWS:ROWS + 1, :, :, :].bitcast(F32), 1.0).then_inc(filled, 1)
            pool.wait_ge(filled, 2)
            pool.wait_ge(b_loaded, 16 * (NH + 2))
            with pool.Fori(0, B) as b:
                _, Bs, _ = slots(b)
                gate_rstd(m1, pool, b, c.power)
                pool.wait_ge(an_ready, b + 1)
                pool.tensor_tensor(xin[:], xin[:], bo[:].unsqueeze(1).to_broadcast([P, TT, C]), ALU.add).then_inc(biased, 1)
                for hg in range(HG):
                    for i in range(N):
                        if crosses(i):
                            Bs.wait_emptied(pool, (hg, i, G - 1))
                            pool.sem_inc(pool_steps, 1)
                            pool.affine_select(out=ex[:, i % 2, :, 0:P], in_=ex[:, i % 2, :, 0:P], compare_op=ALU.is_ge,
                                               fill=0.0, base=0, pattern=[[0, G], [1, P]],
                                               channel_multiplier=-1).then_inc(masked, 1)
                gate_rstd(g, pool, b, c.power)

        @block.tensor
        def _(pe):
            def split3(out, lhs, rhs, n, last):
                pe.matmul(out, lhs[0], rhs[0], start=(n == 0), stop=False)
                pe.matmul(out, lhs[0], rhs[1], start=False, stop=False)
                return pe.matmul(out, lhs[1], rhs[0], start=False, stop=last)

            def turn(slots, bank, src, name):
                for n in TURNS:
                    ch, half = n
                    k = slots.fill(pe, (name, n))
                    for t in range(HT):
                        last = pe.transpose(bank[:, k, t * P:(t + 1) * P],
                                            src[:, HT * half + t, ch * P:(ch + 1) * P], c.ident[:])
                    last.then_inc(slots.filled, 1)

            def project_qk(A, hg):
                for half in range(2):
                    k = A.fill(pe, ("qk", hg, half))
                    for ch in range(KC):
                        cut = slice(half * HALF, (half + 1) * HALF)
                        last = split3(bankA[:, k, :], (wqk_hi[:, ch, hg, :], wqk_lo[:, ch, hg, :]),
                                      (xT_hi[:, ch, cut], xT_lo[:, ch, cut]), ch, ch == KC - 1)
                    last.then_inc(A_filled, 1)

            def project_rows(A, name, w_hi, w_lo):
                for t in range(TT):
                    k = A.fill(pe, (name, t))
                    for ch in range(KC):
                        cut = slice(t * P, (t + 1) * P)
                        last = split3(bankA[:, k, 0:C], (xT_hi[:, ch, cut], xT_lo[:, ch, cut]),
                                      (w_hi[:, ch], w_lo[:, ch]), ch, ch == KC - 1)
                    last.then_inc(A_filled, 1)

            def scores_for_max(A, hg, m):
                h, qt, k0, k1 = m
                a = A.fill(pe, ("max", hg) + m)
                crossing = k1 == (qt + 1) * P
                last = pe.matmul(bankA[:, a, 0:k1 - k0], sq[:, hg % NS, h, qt * P:(qt + 1) * P],
                                 sk[:, hg % NS, h, k0:k1], start=True, stop=not crossing)
                if crossing:
                    last = pe.matmul(bankA[:, a, k1 - k0 - P:k1 - k0], c.identb[:], c.later[:], start=False, stop=True)
                last.then_inc(A_filled, 1)

            def turn_tops(A, b, hg):
                pe.wait_ge(ntop_ready, HG * b + hg + 1)
                a = A.fill(pe, ("top", hg))
                pe.transpose(bankA[0:G * TT, a, 0:P], ntop[:], c.ident[:]).then_inc(A_filled, 1)

            def scores(Bs, hg, i, h):
                half, kt = SETS[i]
                q0 = half * HALF + cols(i)
                k = Bs.fill(pe, (hg, i, h))
                pe.matmul(bankB[:, k, 0:HALF - cols(i)], sk[:, hg % NS, h, kt * P:(kt + 1) * P],
                          sq[:, hg % NS, h, q0:(half + 1) * HALF], start=True, stop=True).then_inc(B_filled, 1)

            def weigh(Bs, Os, b, hg, i):
                half, kt = SETS[i]
                Bs.wait_emptied(pe, (hg, i, G - 1))
                if crosses(i):
                    pe.wait_ge(masked, DIAG * (HG * b + hg) + crosses(i))
                out = ("out", (hg, half))
                k = Os.fill(pe, out) if kt == 0 else O_ORDER.index(out) % 2
                for h in range(G):
                    v0 = VW * (hg * G + h)
                    last = pe.matmul(bankO[32 * h:32 * (h + 1), k, cols(i):HALF], val[:, kt, v0:v0 + 32],
                                     ex[:, i % 2, h, 0:HALF - cols(i)], start=(kt == 0), stop=(i == end_of(half)))
                last.then_inc(ex_used, 1)
                if i == end_of(half):
                    pe.wait_ge(ex_used, N * (HG * b + hg) + i + 1)
                    pe.sem_inc(O_filled, 1)

            def turn_sums(A, Os, out):
                Os.wait_emptied(pe, ("out", out))
                a = A.fill(pe, ("out", out))
                for t in range(HT):
                    q0 = out[1] * HALF + t * P
                    last = pe.transpose(bankA[:, a, t * P:(t + 1) * P], oT[:, q0:q0 + P], c.ident[:])
                last.then_inc(A_filled, 1)

            pe.wait_ge(w_ready, len(SPLITS))
            pe.wait_ge(filled, 2)
            pe.wait_ge(padded, 3)
            with pe.Fori(0, B) as b:
                A, Bs, Os = slots(b)
                pe.wait_ge(an_ready, b + 1)
                turn(A, bankA, att, "x")
                A.wait_emptied(pe, ("x", TURNS[-1]))
                for hg in range(HG):
                    project_qk(A, hg)
                    if hg == 0:
                        project_rows(A, "v", wv_hi, wv_lo)
                pe.wait_ge(stacked[0], STACKING * turns(0, b))
                for m in MAXES:
                    scores_for_max(A, 0, m)
                turn_tops(A, b, 0)
                before = None
                for hg, i, out in steps():
                    more = maxes(i) if hg + 1 < HG else []
                    if i == 0:
                        pe.wait_ge(top_in[hg % NS], 16 * turns(hg, b))
                        if more:
                            pe.wait_ge(stacked[(hg + 1) % NS], STACKING * turns(hg + 1, b))
                    for h in range(G):
                        scores(Bs, hg, i, h)
                        for m in more[h:h + 1] if h < G - 1 else more[h:]:
                            scores_for_max(A, hg + 1, m)
                    if before:
                        weigh(Bs, Os, b, *before)
                    before = (hg, i)
                    if hg + 1 < HG and i == N - 2:
                        turn_tops(A, b, hg + 1)
                    if out:
                        turn_sums(A, Os, out)
                weigh(Bs, Os, b, *before)
                turn_sums(A, Os, (HG - 1, 1))
                pe.wait_ge(att_ready, b + 1)
                turn(A, bankA, att, "att")
                A.wait_emptied(pe, ("att", TURNS[-1]))
                project_rows(A, "proj", wp_hi, wp_lo)
                pe.wait_ge(g.row_ready, b + 1)
                turn(Os, bankO, g.row, "row")
                Os.wait_emptied(pe, ("row", TURNS[-1]))
                a = A.fill(pe, ("score",))
                for t in range(TT):
                    for ch in range(KC):
                        last = pe.matmul(bankA[:, a, t * s.E:(t + 1) * s.E], g.xT[:, ch, t * P:(t + 1) * P],
                                         c.gate[:, ch, :], start=(ch == 0), stop=(ch == KC - 1))
                last.then_inc(A_filled, 1)

        @block.scalar
        def _(act):
            def high(A, what, out, func=ACT.Copy, **bias):
                k = A.take(act, what)
                act.activation(out, bankA[:, k, :], func, **bias).then_inc(hi_ready, 1)

            act.wait_ge(w_loaded, 32)
            for whole, hi, _ in SPLITS:
                act.activation(hi, whole, ACT.Copy).then_inc(w_hi_ready, 1)
            act.wait_ge(b_loaded, 16 * (NH + 2))
            with act.Fori(0, B) as b:
                A, Bs, Os = slots(b)

                def copy_sums(out):
                    k = Os.take(act, ("out", out))
                    hg, half = out
                    if hg:
                        A.wait_emptied(act, ("out", (hg - 1, half)))
                    Os.ring.emptied(act.activation(oT[:, half * HALF:(half + 1) * HALF], bankO[:, k, :], ACT.Copy))

                for n in TURNS:
                    high(A, ("x", n), xT_hi[:, n[0], n[1] * HALF:(n[1] + 1) * HALF])
                for hg in range(HG):
                    if hg >= 2:
                        act.wait_ge(stacked[(hg - 2) % NS], STACKING * turns(hg - 2, b))
                    for half in range(2):
                        high(A, ("qk", hg, half), qk_hi[:, hg % 2, half * HALF:(half + 1) * HALF], ACT.Identity,
                             bias=bqk[:, hg:hg + 1])
                for hg, i, _ in steps():
                    n = hg * N + i
                    for h in range(G):
                        k = Bs.take(act, (hg, i, h))
                        if h == 0:
                            if n >= 2:
                                act.wait_ge(ex_used, N * HG * b + n - 1)
                        Bs.ring.emptied(act.activation(ex[:, i % 2, h, 0:HALF - cols(i)], bankB[:, k, 0:HALF - cols(i)],
                                                       ACT.Exp, scale=SCALE))
                    if i == HT:
                        copy_sums((hg, 0))
                    if i == 0 and hg:
                        copy_sums((hg - 1, 1))
                copy_sums((HG - 1, 1))
                for n in TURNS:
                    high(A, ("att", n), xT_hi[:, n[0], n[1] * HALF:(n[1] + 1) * HALF])
                for n in TURNS:
                    k = Os.take(act, ("row", n))
                    Os.ring.emptied(act.activation(g.xT[:, n[0], n[1] * HALF:(n[1] + 1) * HALF], bankO[:, k, :], ACT.Copy))
                A.wait_emptied(act, ("score",))
                act.activation(g.ex[:], g.sub[:], ACT.Exp).then_inc(g.ex_ready, 1)

        @block.vector
        def _(dve):
            for n, (whole, hi, lo) in enumerate(SPLITS):
                dve.wait_ge(w_hi_ready, n + 1)
                dve.tensor_tensor(lo, whole, hi.bitcast(F32), ALU.subtract).then_inc(w_ready, 1)
            dve.memset(sq[ROWS:P, :, :, :].bitcast(F32), 0.0).then_inc(padded, 1)
            dve.memset(tops[:], -3e38).then_inc(padded, 1)
            dve.memset(val[:], 1.0).then_inc(padded, 1)
            dve.wait_ge(padded, 3)
            dve.wait_ge(w_ready, len(SPLITS))
            with dve.Fori(0, B) as b:
                A, _, _ = slots(b)
                norm = Chain(dve, m1.dve, Moments.DVE_STEPS * b)
                gate = Chain(dve, g.dve, Gate.DVE_STEPS * b)
                HEAD_STEPS = 2 * HG
                heads = Chain(dve, att_dve, HEAD_STEPS * b)

                def rest(nth, what, out, hi, bias=None):
                    k = A.take(dve, what)
                    dve.wait_ge(hi_ready, HI_PER * b + nth + 1)
                    ringA.emptied(dve.tensor_tensor(out, bankA[:, k, :], hi.bitcast(F32), ALU.subtract) if bias is None else
                                  dve.scalar_tensor_tensor(out, bankA[:, k, :], bias, hi.bitcast(F32), ALU.add, ALU.subtract))

                def rest_turned(first, name):
                    for n, (ch, half) in enumerate(TURNS):
                        cut = slice(half * HALF, (half + 1) * HALF)
                        rest(first + n, (name, (ch, half)), xT_lo[:, ch, cut], xT_hi[:, ch, cut])

                def largest(hg, m):
                    h, qt, k0, k1 = m
                    k = A.take(dve, ("max", hg) + m)
                    ringA.emptied(dve.tensor_reduce(tops[:, h, qt, k0 // BANK:k0 // BANK + 1], bankA[:, k, 0:k1 - k0],
                                                    AX.X, ALU.max))

                def negate_tops(hg):
                    A.wait_emptied(dve, ("max", hg) + MAXES[-1])
                    dve.tensor_reduce(ntop[:].rearrange("p (g t) -> p g t", g=G), tops[:], AX.X, ALU.max,
                                      negate=True).then_inc(ntop_ready, 1)

                def copy_tops(hg):
                    k = A.take(dve, ("top", hg))
                    if hg >= 1:
                        dve.wait_ge(top_in[(hg - 1) % NS], 16 * turns(hg - 1, b))
                    ins = dve.tensor_copy(ntopT[:], bankA[0:G * TT, k, 0:P])
                    ringA.emptied(ins)

                def divide(out):
                    hg, half = out
                    k = A.take(dve, ("out", out))
                    sums = bankA[:, k, :].rearrange("p (t g d) -> p t g d", t=HT, g=G)
                    heads.did(dve.reciprocal(inv[:, half].unsqueeze(3), sums[:, :, :, D:D + 1]))
                    heads.settle()
                    to = att[:, HT * half:HT * (half + 1), hg * G * D:(hg + 1) * G * D]
                    ringA.emptied(dve.tensor_tensor(to.rearrange("p t (g d) -> p t g d", g=G), sums[:, :, :, 0:D],
                                                    inv[:, half].unsqueeze(3).to_broadcast([P, HT, G, D]), ALU.mult))

                dve.wait_ge(x_loaded, 16 * (b + 1))
                gate_stats(m1, dve, norm, xin)
                dve.wait_ge(m1.rstd_ready, b + 1)
                dve.wait_ge(x2_out, 16 * (b + 1))
                for t in range(TT):
                    last = dve.tensor_scalar(att[:, t, :], xin[:, t, :], m1.mv[:, t, 0:1], m1.rstd[:, t:t + 1],
                                             ALU.subtract, ALU.mult)
                last.then_inc(an_ready, 1)
                rest_turned(0, "x")
                nth = len(TURNS)
                for hg in range(HG):
                    for half in range(2):
                        cut = slice(half * HALF, (half + 1) * HALF)
                        rest(nth, ("qk", hg, half), qk_lo[:, hg % 2, cut], qk_hi[:, hg % 2, cut], bqk[:, hg:hg + 1])
                        nth += 1
                    if hg == 0:
                        for t in range(TT):
                            k = A.take(dve, ("v", t))
                            ringA.emptied(dve.tensor_tensor(
                                val[:, t, 0:NH * VW].rearrange("p (h w) -> p h w", w=VW)[:, :, 0:D],
                                bankA[:, k, 0:C].rearrange("p (h d) -> p h d", d=D), bv[:], ALU.add))
                for m in MAXES:
                    largest(0, m)
                negate_tops(0)
                copy_tops(0)
                for hg, i, out in steps():
                    if hg + 1 < HG:
                        for m in maxes(i):
                            largest(hg + 1, m)
                        if PER_SET * i < len(MAXES) <= PER_SET * (i + 1):
                            negate_tops(hg + 1)
                        if i == N - 2:
                            copy_tops(hg + 1)
                    if out:
                        divide(out)
                divide((HG - 1, 1))
                A.wait_emptied(dve, ("out", (HG - 1, 1)))
                dve.sem_inc(att_ready, 1)
                rest_turned(nth, "att")
                dve.wait_ge(biased, b + 1)
                for t in range(TT):
                    k = A.take(dve, ("proj", t))
                    ins = dve.tensor_tensor(att[:, t, :], bankA[:, k, 0:C], xin[:, t, :], ALU.add)
                    ringA.emptied(ins)
                A.wait_emptied(dve, ("proj", TT - 1))
                dve.sem_inc(x2_ready, TT)
                gate_stats(g, dve, gate, att)
                gate_rows(g, dve, b, att)
                k = A.take(dve, ("score",))
                score = bankA[:, k, 0:TT * s.E].rearrange("p (t e) -> p t e", e=s.E)
                gate.did(dve.tensor_reduce(g.top[:], score, AX.X, ALU.max))
                gate.settle()
                ringA.emptied(dve.tensor_tensor(g.sub[:], score, g.top[:].unsqueeze(2).to_broadcast([P, TT, s.E]),
                                                ALU.subtract))
                gate_softmax_back(g, dve, gate, b, prob)
                assert (norm.n, gate.n, heads.n) == (Moments.DVE_STEPS, Gate.DVE_STEPS, HEAD_STEPS)



def macaron_layer(nc, x, W1, b1, Wp, bp, gate_w, w1, w2, out):
    s = Shapes(x, gate_w, w1)
    with ExitStack() as ctx:
        c = Constants(nc, ctx, s, gate_w)
        prob = ctx.enter_context(nc.sbuf_tensor("prob", [P, s.BE * s.TT], F32))
        index = ctx.enter_context(nc.sbuf_tensor("index", [P, s.E * s.ST], U32))
        table = nc.dram_tensor("table", (s.B * s.T, s.ROW), F32).ap()
        x1 = nc.dram_tensor("x1", (s.B * s.T, s.C), F32).ap()
        x2 = out.rearrange("b t c -> (b t) c")
        norm_block(nc, s, c, x, table, x1, prob)
        route_block(nc, s, c, prob, index, "_1")
        experts_block(nc, s, c, w1, w2, table, x1, index, "_1")
        attention_block(nc, s, c, x1, W1, b1, Wp, bp, x2, table, prob)
        route_block(nc, s, c, prob, index, "_2")
        experts_block(nc, s, c, w1, w2, table, x2, index, "_2")


_INS = ["L0_attn_x", "L0_attn_W1", "L0_attn_b1", "L0_attn_Wp", "L0_attn_bp", "L0_ffn_gate_w", "L0_ffn_w1", "L0_ffn_w2"]
_OUTS = [((4, 1024, 256), "float32")]


def kernel(**inputs):
    import numpy as _np
    import concourse.bacc as _bacc
    from concourse import mybir as _mybir
    from concourse.bass_utils import run_bass_kernel_spmd as _run

    nc = _bacc.Bacc("TRN2", target_bir_lowering=False, num_devices=1)
    arrays, args = {}, []
    for name in _INS:
        a = _np.ascontiguousarray(inputs[name])
        arrays[f"in_{name}_dram"] = a
        args.append(nc.dram_tensor(f"in_{name}_dram", a.shape, _mybir.dt.from_np(a.dtype), kind="ExternalInput").ap())
    for i, (shape, dtype) in enumerate(_OUTS):
        dt = _mybir.dt.from_np(_np.dtype(dtype))
        args.append(nc.dram_tensor(f"out_{i}_dram", shape, dt, kind="ExternalOutput").ap())
    macaron_layer(nc, *args)
    r = _run(nc, [arrays], core_ids=[0])
    got = tuple(r.results[0][f"out_{i}_dram"] for i in range(len(_OUTS)))
    return got[0]
```

```python
from contextlib import ExitStack

import concourse.bass as bass
from concourse import mybir

ALU = mybir.AluOpType
ACT = mybir.ActivationFunctionType
AX = mybir.AxisListType
F32 = mybir.dt.float32
F32R = mybir.dt.float32r
BF16 = mybir.dt.bfloat16
F16 = mybir.dt.float16
I32 = mybir.dt.int32
U32 = mybir.dt.uint32

P = 128
BANK = 512
LN_EPS = 1e-5
PROB_BITS = 30
ds = bass.ds


class Shapes:

    def __init__(self, x, gate_w, w1):
        self.B, self.T, self.C = x.shape
        self.E = gate_w.shape[1]
        self.H = w1.shape[2]
        self.CAP = 2 * self.T // self.E
        self.TT = self.T // P
        self.KC = self.C // P
        self.J = self.H // P
        self.BE = self.B * self.E
        self.ROW = self.C + self.E
        self.SH = self.CAP // P
        self.ST = self.B * self.SH
        self.U = 2 * self.E
        self.Q = self.ST // 2
        assert self.CAP == 2 * P and self.KC == 2 and self.ST == 8 and self.TT == 8 and self.E == 8


class Ring:

    def __init__(self, sem, depth):
        self.sem, self.depth = sem, depth

    def start(self, eng):
        eng.sem_inc(self.sem, self.depth)

    def wait_free(self, eng, k):
        eng.wait_ge(self.sem, k + 1)

    def emptied(self, ins):
        ins.then_inc(self.sem, 1)

    def wait_emptied(self, eng, k):
        eng.wait_ge(self.sem, k + 1 + self.depth)


class Chain:

    def __init__(self, eng, sem, base=0):
        self.eng, self.sem, self.base, self.n = eng, sem, base, 0

    def did(self, ins):
        ins.then_inc(self.sem, 1)
        self.n += 1

    def settle(self):
        self.eng.wait_ge(self.sem, self.base + self.n)

    def pause(self):
        self.settle()
        self.eng.sem_inc(self.sem, 1)
        self.n += 1



class Moments:

    DVE_STEPS = 3

    def __init__(self, s, sb, sem, tag):
        self.s = s
        self.stats = sb(f"stats{tag}", [P, s.TT, 6], F32)
        self.mv = sb(f"mean_var{tag}", [P, s.TT, 2], F32)
        self.ve = sb(f"var_eps{tag}", [P, s.TT], F32)
        self.rstd = sb(f"rstd{tag}", [P, s.TT], F32)
        self.dve = sem(f"norm_dve{tag}")
        self.var_ready = sem(f"var_ready{tag}")
        self.rstd_ready = sem(f"rstd_ready{tag}")


class Gate(Moments):

    DVE_STEPS = Moments.DVE_STEPS + 4

    def __init__(self, s, sb, sem, turn, score, tag, xT=None):
        super().__init__(s, sb, sem, tag)
        self.turn, self.score = turn, score
        self.row = sb(f"row{tag}", [P, s.TT, s.ROW], F32)
        self.xT = xT if xT is not None else sb(f"xT{tag}", [P, s.KC, s.T], F32)[:]
        self.top = sb(f"top{tag}", [P, s.TT], F32)
        self.sub = sb(f"sub{tag}", [P, s.TT, s.E], F32)
        self.ex = sb(f"ex{tag}", [P, s.TT, s.E], F32)
        self.tot = sb(f"tot{tag}", [P, s.TT], F32)
        self.inv = sb(f"inv{tag}", [P, s.TT], F32)
        self.row_ready = sem(f"row_ready{tag}")
        self.turned = sem(f"turned{tag}")
        self.turn_ring = Ring(sem(f"turn_free{tag}"), 2)
        self.score_ready = sem(f"score_ready{tag}")
        self.sub_ready = sem(f"sub_ready{tag}")
        self.ex_ready = sem(f"ex_ready{tag}")
        self.prob_ready = sem(f"prob_ready{tag}")
        self.table_out = sem(f"table_out{tag}")


def gate_stats(g, dve, chain, x):
    s = g.s
    for t in range(s.TT):
        last = dve.bn_stats(g.stats[:, t, :], x[:, t, :])
    chain.did(last)
    chain.pause()
    for t in range(s.TT):
        last = dve.bn_aggr(g.mv[:, t, :], g.stats[:, t, :])
    chain.did(last)
    chain.settle()
    dve.tensor_scalar(g.ve[:], g.mv[:, :, 1], LN_EPS, None, ALU.add).then_inc(g.var_ready, 1)


def gate_rstd(g, pool, b, power):
    pool.wait_ge(g.var_ready, b + 1)
    pool.tensor_tensor(g.rstd[:], g.ve[:], power[:], ALU.pow).then_inc(g.rstd_ready, 1)


def gate_rows(g, dve, b, x):
    s = g.s
    dve.wait_ge(g.rstd_ready, b + 1)
    dve.wait_ge(g.table_out, 16 * (b + 1))
    for t in range(s.TT):
        last = dve.tensor_scalar(g.row[:, t, 0:s.C], x[:, t, :], g.mv[:, t, 0:1], g.rstd[:, t:t + 1],
                                 ALU.subtract, ALU.mult)
    last.then_inc(g.row_ready, 1)


def gate_turn(g, pe, b, ident):
    s = g.s
    pe.wait_ge(g.row_ready, b + 1)
    for n in range(4):
        c, half = n // 2, n % 2
        g.turn_ring.wait_free(pe, 4 * b + n)
        for t in range(4):
            last = pe.transpose(g.turn[:, n % 2, t * P:(t + 1) * P],
                                g.row[:, 4 * half + t, c * P:(c + 1) * P], ident[:])
        last.then_inc(g.turned, 1)


def gate_score(g, pe, b, gate):
    s = g.s
    g.turn_ring.wait_emptied(pe, 4 * b + 3)
    for t in range(s.TT):
        for c in range(s.KC):
            last = pe.matmul(g.score[:, t, :], g.xT[:, c, t * P:(t + 1) * P], gate[:, c, :],
                             start=(c == 0), stop=(c == s.KC - 1))
    last.then_inc(g.score_ready, 1)


def gate_copy(g, act, b):
    act.wait_ge(g.score_ready, b + 1)
    for n in range(4):
        c, half = n // 2, n % 2
        act.wait_ge(g.turned, 4 * b + n + 1)
        g.turn_ring.emptied(act.activation(g.xT[:, c, half * BANK:(half + 1) * BANK],
                                           g.turn[:, n % 2, :], ACT.Copy))


def gate_exp(g, act, b):
    act.wait_ge(g.sub_ready, b + 1)
    act.activation(g.ex[:], g.sub[:], ACT.Exp).then_inc(g.ex_ready, 1)


def gate_softmax_front(g, dve, chain, b):
    s = g.s
    dve.wait_ge(g.score_ready, b + 2)
    chain.did(dve.tensor_reduce(g.top[:], g.score[:], AX.X, ALU.max))
    chain.settle()
    dve.tensor_tensor(g.sub[:], g.score[:], g.top[:].unsqueeze(2).to_broadcast([P, s.TT, s.E]),
                      ALU.subtract).then_inc(g.sub_ready, 1)


def gate_softmax_back(g, dve, chain, b, prob):
    s = g.s
    dve.wait_ge(g.ex_ready, b + 1)
    chain.did(dve.tensor_reduce(g.tot[:], g.ex[:], AX.X, ALU.add))
    chain.settle()
    chain.did(dve.reciprocal(g.inv[:], g.tot[:]))
    chain.settle()
    chain.did(dve.tensor_tensor(g.row[:, :, s.C:s.ROW], g.ex[:],
                                g.inv[:].unsqueeze(2).to_broadcast([P, s.TT, s.E]), ALU.mult))
    chain.settle()
    dve.tensor_copy(prob[:, ds(b * s.TT * s.E, s.TT * s.E)].rearrange("p (t e) -> p t e", t=s.TT),
                    g.row[:, :, s.C:s.ROW]).then_inc(g.prob_ready, 1)


def gate_table(g, sp, b, table):
    s = g.s
    sp.wait_ge(g.prob_ready, b + 1)
    dst = table.rearrange("(b t p) r -> b p t r", b=s.B, p=P)[b]
    sp.dma_start(dst, g.row[:]).then_inc(g.table_out, 16)


def gate_start(g, eng):
    eng.sem_inc(g.table_out, 16)
    eng.sem_inc(g.score_ready, 1)
    g.turn_ring.start(eng)


def norm_block(nc, s, c, x, table, acc, prob):
    with ExitStack() as ctx:
        sb = lambda n, sh, d: ctx.enter_context(nc.sbuf_tensor(n, sh, d))
        sem = c.sem
        turn = ctx.enter_context(nc.psum_tensor("turn_n", [P, 2, BANK], F32))
        score = ctx.enter_context(nc.psum_tensor("score_n", [P, s.TT, s.E], F32))
        g = Gate(s, sb, sem, turn, score, "_n")
        xin = sb("xin", [P, s.TT, s.C], F32)
        x_loaded, acc_init = sem("x_loaded"), sem("acc_init")
        xv = x.rearrange("b (t p) c -> b p t c", p=P)
        block = ctx.enter_context(nc.Block())

        @block.sync
        def _(sp):
            gate_start(g, sp)
            sp.dma_start(xin[:], xv[0]).then_inc(x_loaded, 16)
            sp.dma_start(c.gate[:], c.gate_w.rearrange("(k p) e -> p k e", p=P)).then_inc(c.gate_in, 16)
            sp.dma_start(acc, x.rearrange("b t c -> (b t) c")).then_inc(acc_init, 16)
            with sp.Fori(0, s.B - 1) as b:
                sp.wait_ge(g.row_ready, b + 1)
                sp.dma_start(xin[:], xv[b + 1]).then_inc(x_loaded, 16)
                gate_table(g, sp, b, table)
            gate_table(g, sp, s.B - 1, table)
            sp.wait_ge(acc_init, 16)
            sp.wait_ge(g.table_out, 16 * (s.B + 1))

        @block.gpsimd
        def _(pool):
            make_constants(nc, c, s, pool)
            with pool.Fori(0, s.B) as b:
                gate_rstd(g, pool, b, c.power)

        @block.tensor
        def _(pe):
            pe.wait_ge(c.made, c.MADE)
            pe.wait_ge(c.gate_in, 16)
            with pe.Fori(0, s.B) as b:
                gate_turn(g, pe, b, c.ident)
                gate_score(g, pe, b, c.gate)

        @block.scalar
        def _(act):
            with act.Fori(0, s.B) as b:
                gate_copy(g, act, b)
                gate_exp(g, act, b)

        @block.vector
        def _(dve):
            dve.wait_ge(c.made, c.MADE)
            convert_constants(nc, c, dve)
            with dve.Fori(0, s.B) as b:
                chain = Chain(dve, g.dve, b * g.DVE_STEPS)
                dve.wait_ge(x_loaded, 16 * (b + 1))
                gate_stats(g, dve, chain, xin)
                gate_rows(g, dve, b, xin)
                gate_softmax_front(g, dve, chain, b)
                gate_softmax_back(g, dve, chain, b, prob)
                assert chain.n == g.DVE_STEPS



class Constants:
    def __init__(self, nc, ctx, s, gate_w):
        sb = lambda n, sh, d: ctx.enter_context(nc.sbuf_tensor(n, sh, d))
        self.sem = lambda n: ctx.enter_context(nc.semaphore(n))
        self.gate_w = gate_w
        self.gate = sb("gate", [P, s.KC, s.E], F32)
        self.ident = sb("ident", [P, P], F32)
        self.identb = sb("identb", [P, P], BF16)
        self.ones = sb("ones", [P, P], BF16)
        self.upto = sb("upto", [P, P], BF16)
        self.later = sb("later", [P, P], BF16)
        self.slot_i = sb("slot_i", [P, s.CAP], I32)
        self.slot = sb("slot", [P, s.CAP], F16)
        self.tok_i = sb("tok_i", [P, s.TT], I32)
        self.tok = sb("tok", [P, s.TT], F16)
        self.first_i = sb("first_i", [P, s.B, s.SH], I32)
        self.first = sb("first", [P, s.B, s.SH], F32)
        self.shift = sb("shift", [P, PROB_BITS + 1], I32)
        self.one_i = sb("one_i", [P, PROB_BITS + 1], I32)
        self.bit_i = sb("bit_i", [P, PROB_BITS + 1], I32)
        self.bit_f = sb("bit_f", [P, PROB_BITS + 1], F32)
        self.power = sb("power", [P, s.TT], F32)
        self.blank = self.sem("blank")
        self.made = self.sem("made")
        self.gate_in = self.sem("gate_in")
        self.converted = self.sem("converted")

    MADE = 10


def make_constants(nc, c, s, pool):
    pool.memset(c.ident[:], 0.0).then_inc(c.blank, 1)
    pool.memset(c.identb[:], 0.0).then_inc(c.blank, 1)
    pool.memset(c.upto[:], 1.0).then_inc(c.blank, 1)
    pool.memset(c.later[:], 0.0).then_inc(c.blank, 1)
    pool.memset(c.ones[:], 1.0).then_inc(c.blank, 1)
    pool.memset(c.power[:], -0.5).then_inc(c.made, 1)
    pool.iota(c.shift[:, 0:PROB_BITS], pattern=[[-1, PROB_BITS]], base=PROB_BITS - 1, channel_multiplier=0)
    pool.memset(c.shift[:, PROB_BITS:], 0).then_inc(c.made, 1)
    pool.memset(c.one_i[:], 1).then_inc(c.made, 1)
    pool.wait_ge(c.blank, 5)
    for m in (c.ident, c.identb):
        pool.affine_select(out=m[:], in_=m[:], compare_op=ALU.not_equal, fill=1.0, base=0,
                           pattern=[[-1, P]], channel_multiplier=1).then_inc(c.made, 1)
    pool.affine_select(out=c.upto[:], in_=c.upto[:], compare_op=ALU.is_ge, fill=0.0, base=0,
                       pattern=[[1, P]], channel_multiplier=-1).then_inc(c.made, 1)
    pool.affine_select(out=c.later[:], in_=c.later[:], compare_op=ALU.is_ge, fill=-4e6, base=0,
                       pattern=[[-1, P]], channel_multiplier=1).then_inc(c.made, 1)
    pool.iota(c.slot_i[:], pattern=[[1, s.CAP]], base=1, channel_multiplier=0).then_inc(c.made, 1)
    pool.iota(c.tok_i[:], pattern=[[P, s.TT]], base=0, channel_multiplier=1).then_inc(c.made, 1)
    pool.iota(c.first_i[:], pattern=[[s.T, s.B], [0, s.SH]], base=0, channel_multiplier=0).then_inc(c.made, 1)


def convert_constants(nc, c, dve):
    dve.tensor_tensor(c.bit_i[:], c.one_i[:], c.shift[:], ALU.logical_shift_left).then_inc(c.converted, 1)
    dve.wait_ge(c.converted, 1)
    dve.tensor_copy(c.bit_f[:], c.bit_i[:]).then_inc(c.converted, 1)
    dve.tensor_copy(c.slot[:], c.slot_i[:]).then_inc(c.converted, 1)
    dve.tensor_copy(c.tok[:], c.tok_i[:]).then_inc(c.converted, 1)
    dve.tensor_copy(c.first[:], c.first_i[:]).then_inc(c.converted, 1)



def route_block(nc, s, c, prob, index, tag):
    B, E, TT, BE = s.B, s.E, s.TT, s.BE
    with ExitStack() as ctx:
        sb = lambda n, sh, d: ctx.enter_context(nc.sbuf_tensor(n + tag, sh, d))
        ps = lambda n, sh: ctx.enter_context(nc.psum_tensor(n + tag, sh, F32))
        sem = lambda n: c.sem(n + tag)
        thr = sb("thr", [P, BE], I32)
        trial = sb("trial", [P, BE], I32)
        add = sb("add", [P, BE], I32)
        over = sb("over", [P, B, TT, E], BF16)
        equal = sb("equal", [P, B, TT, E], BF16)
        need = sb("need", [P, BE], F32)
        fits = sb("fits", [P, B, TT, E], BF16)
        taken = sb("taken", [P, B, TT, E], BF16)
        rank = sb("rank", [P, E, B, TT], F32)
        hot = sb("hot", [P, 2, TT, s.CAP], F16)
        count = ps("count", [P, BANK])
        run = ps("run", [P, TT, BE])
        lists = ps("lists", [P, BANK])
        dve_s, tried, counted = sem("route_dve"), sem("tried"), sem("counted")
        hot_ready = sem("hot_ready")
        hot_ring = Ring(sem("hot_free"), 2)
        pv = prob[:].rearrange("p (b t e) -> p b t e", b=B, t=TT)

        def spread(v):
            return v.rearrange("p (b e) -> p b e", b=B).unsqueeze(2).to_broadcast([P, B, TT, E])

        def totals(pe, mask):
            for t in range(TT):
                last = pe.matmul(count[:, 0:BE], c.ones[:], mask[:, :, t, :], start=(t == 0), stop=(t == TT - 1))
            return last

        def running(pe, mask):
            for t in range(TT):
                for before in range(t):
                    pe.matmul(run[:, t, :], c.ones[:], mask[:, :, before, :], start=(before == 0), stop=False)
                last = pe.matmul(run[:, t, :], c.upto[:], mask[:, :, t, :], start=(t == 0), stop=True)
            return last

        block = ctx.enter_context(nc.Block())

        @block.vector
        def _(dve):
            chain = Chain(dve, dve_s)
            dve.memset(thr[:], 0)
            chain.did(dve.memset(trial[:], 1 << (PROB_BITS - 1)))
            chain.settle()
            before, STEPS = chain.n, 3
            with dve.Fori(0, PROB_BITS) as k:
                chain = Chain(dve, dve_s, before + STEPS * k)
                dve.tensor_tensor(over[:], pv, spread(trial[:].bitcast(F32)), ALU.is_ge).then_inc(tried, 1)
                dve.wait_ge(counted, k + 1)
                chain.did(dve.tensor_scalar(add[:], count[:, 0:BE], float(s.CAP), c.bit_f[:, ds(k, 1)],
                                            ALU.is_ge, ALU.mult))
                chain.settle()
                chain.did(dve.scalar_tensor_tensor(trial[:], add[:], c.bit_i[:, ds(k + 1, 1)], thr[:],
                                                   ALU.bitwise_or, ALU.bitwise_or))
                chain.settle()
                chain.did(dve.tensor_tensor(thr[:], thr[:], add[:], ALU.bitwise_or))
                assert chain.n == STEPS
            chain = Chain(dve, dve_s, before + STEPS * PROB_BITS)
            chain.settle()
            dve.tensor_tensor(over[:], pv, spread(thr[:].bitcast(F32)), ALU.is_gt)
            dve.tensor_tensor(equal[:], pv, spread(thr[:].bitcast(F32)), ALU.is_equal).then_inc(tried, 1)
            dve.wait_ge(counted, PROB_BITS + 1)
            chain.did(dve.tensor_scalar(need[:], count[:, 0:BE], -1.0, float(s.CAP), ALU.mult, ALU.add))
            chain.settle()
            chain.did(dve.tensor_tensor(fits[:], run[:].rearrange("p t (b e) -> p b t e", b=B), spread(need[:]), ALU.is_le))
            chain.settle()
            chain.did(dve.tensor_tensor(taken[:], fits[:], equal[:], ALU.mult))
            chain.settle()
            dve.tensor_tensor(fits[:], taken[:], over[:], ALU.add).then_inc(tried, 1)
            dve.wait_ge(counted, PROB_BITS + 2)
            chain.did(dve.tensor_tensor(rank[:].rearrange("p e b t -> p b t e"),
                                        run[:].rearrange("p t (b e) -> p b t e", b=B), fits[:], ALU.mult))
            chain.settle()
            with dve.Fori(0, E) as e:
                for b in range(B):
                    k = e * B + b
                    hot_ring.wait_free(dve, k)
                    for t in range(TT):
                        last = dve.tensor_scalar(hot[:, b % 2, t, :], c.slot[:],
                                                 rank[:].rearrange("p e b t -> p (e b t)")[:, ds(k * TT + t, 1)],
                                                 None, ALU.is_equal)
                    last.then_inc(hot_ready, 1)
            hot_ring.wait_emptied(dve, BE - 1)
            dve.tensor_tensor(index[:].rearrange("p (e k) -> p e k", e=E),
                              lists[:, 0:E * s.ST].rearrange("p (e k) -> p e k", e=E),
                              c.first[:].rearrange("p b h -> p (b h)").unsqueeze(1).to_broadcast([P, E, s.ST]),
                              ALU.add)

        @block.tensor
        def _(pe):
            hot_ring.start(pe)
            with pe.Fori(0, PROB_BITS) as k:
                pe.wait_ge(tried, k + 1)
                totals(pe, over).then_inc(counted, 1)
            pe.wait_ge(tried, PROB_BITS + 1)
            totals(pe, over)
            running(pe, equal).then_inc(counted, 1)
            pe.wait_ge(tried, PROB_BITS + 2)
            running(pe, fits).then_inc(counted, 1)
            with pe.Fori(0, E) as e:
                for b in range(B):
                    pe.wait_ge(hot_ready, e * B + b + 1)
                    for h in range(s.SH):
                        for t in range(TT):
                            last = pe.matmul(lists[:, ds(e * s.ST + b * s.SH + h, 1)],
                                             hot[:, b % 2, t, h * P:(h + 1) * P], c.tok[:, t:t + 1],
                                             start=(t == 0), stop=(t == TT - 1))
                    hot_ring.emptied(last)



def experts_block(nc, s, c, w1, w2, table, acc, index, tag):
    J, KC, Q, U, C, H = s.J, s.KC, s.Q, s.U, s.C, s.H
    W = Q * P
    WP = KC * H // J
    FIRST, LOOP = 2, 4
    LOOPS = (U - 2 * FIRST) // LOOP
    with ExitStack() as ctx:
        sb = lambda n, sh, d: ctx.enter_context(nc.sbuf_tensor(n + tag, sh, d))
        ps = lambda n, sh: ctx.enter_context(nc.psum_tensor(n + tag, sh, F32))
        sem = lambda n: c.sem(n + tag)
        w1_in = sb("w1_in", [P, KC, H], F32)
        w2_in = sb("w2_in", [P, J, C], F32)
        w1_hi, w1_lo = (sb(n, [P, 2, KC, H], F32R) for n in ("w1_hi", "w1_lo"))
        w2_hi, w2_lo = (sb(n, [P, 2, J, C], F32R) for n in ("w2_hi", "w2_lo"))
        rows = sb("rows", [P, 2, Q, s.ROW], F32)
        xT_hi, xT_lo = (sb(n, [P, 2, KC, W], F32R) for n in ("xs_hi", "xs_lo"))
        act_f = sb("act_f", [P, 2, W], F32)
        h_hi, h_lo = (sb(n, [P, 2, J, W], F32R) for n in ("h_hi", "h_lo"))
        gain = sb("gain", [P, 4, Q], F32)
        y = sb("y", [P, 2, Q, C], F32)
        lists = sb("slots", [P, 4, Q], U32)
        turn = ps("turn", [P, KC, BANK])
        up = ps("up", [P, 4, BANK])
        down = ps("down", [P, 2, BANK])

        w1_loaded, w2_loaded = sem("w1_loaded"), sem("w2_loaded")
        w1_hi_ready, w1_ready = sem("w1_hi_ready"), sem("w1_ready")
        w2_hi_ready, w2_ready = sem("w2_hi_ready"), sem("w2_ready")
        list_ready, pool_steps = sem("list_ready"), sem("pool_steps")
        gathered = [sem(f"gathered{k}") for k in range(2)]
        added = [sem(f"added{k}") for k in range(2)]
        turned, xs_hi_ready, gained = sem("turned"), sem("xs_hi_ready"), sem("gained")
        up_done, h_hi_ready, down_done = sem("up_done"), sem("h_hi_ready"), sem("down_done")
        turn_ring = Ring(sem("xs_ready"), KC)
        up_ring = Ring(sem("gelu_done"), 4)
        act_ring = Ring(sem("h_ready"), 2)
        down_ring = Ring(sem("y_ready"), 2)

        def dma_total(u, k):
            return 8 * Q * (u - k % 2) + 16 * Q

        def added_total(u, k):
            return dma_total(u, k) + 16 * Q

        def splits(u, k):
            return (J // 2) * (u - k % 2) + J

        def expert(u, k):
            return u // 2 if isinstance(u, int) else (u - k % 2) // 2

        def piece(weights_in, hi, lo, k, j):
            flat = lambda v: v.rearrange("p a b -> p (a b)")[:, j * WP:(j + 1) * WP]
            return flat(weights_in[:]), flat(hi[:, k]), flat(lo[:, k])

        def steps(eng, body):
            for u in range(FIRST):
                body(u, u)
            with eng.Fori(0, LOOPS) as i:
                for k in range(LOOP):
                    body(LOOP * i + (FIRST + k), (FIRST + k) % LOOP)
            for u in range(U - FIRST, U):
                body(u, u % LOOP)

        def hold(pool, sem, value):
            pool.wait_ge(sem, value)
            pool.sem_inc(pool_steps, 1)

        def known(u):
            return isinstance(u, int)

        def at_least(u, least):
            return u >= least if isinstance(u, int) else least <= FIRST

        def before(u, end):
            return u < end if isinstance(u, int) else True

        block = ctx.enter_context(nc.Block())

        @block.sync
        def _(sp):
            w1_v = w1.rearrange("e (k p) h -> e p k h", p=P)
            w2_v = w2.rearrange("e (j p) n -> e p j n", p=P)
            sp.dma_start(w1_in[:], w1_v[0]).then_inc(w1_loaded, 16)
            sp.dma_start(w2_in[:], w2_v[0]).then_inc(w2_loaded, 16)
            with sp.Fori(0, s.E - 1) as e:
                sp.wait_ge(w1_ready, J * (e + 1))
                sp.dma_start(w1_in[:], w1_v[e + 1]).then_inc(w1_loaded, 16)
                sp.wait_ge(w2_ready, J * (e + 1))
                sp.dma_start(w2_in[:], w2_v[e + 1]).then_inc(w2_loaded, 16)

        @block.gpsimd
        def _(pool):
            down_ring.start(pool)
            act_ring.start(pool)
            up_ring.start(pool)
            turn_ring.start(pool)

            def gather(u, k, reused=True):
                if at_least(u, 2):
                    pool.wait_ge(added[k % 2], added_total(u - 4, k))
                pool.tensor_copy(lists[:, k % 4, :], index[:, ds(u * Q, Q)]).then_inc(list_ready, 1)
                if reused:
                    pool.wait_ge(turned, KC * (u - 1))
                    pool.wait_ge(gained, u - 1)
                hold(pool, list_ready, u + 1)
                for q in range(Q):
                    pool.indirect_dma_start(rows[:, k % 2, q, :], None, table,
                                            bass.IndirectOffsetOnAxis(lists[:, k % 4, q:q + 1], 0)
                                            ).then_inc(gathered[k % 2], 16)

            def add(u, k):
                pool.wait_ge(added[k % 2], added_total(u - 2, k))
                for q in range(Q):
                    hold(pool, down_ring.sem, Q * u + q + 1 + down_ring.depth)
                    pool.indirect_dma_start(acc, bass.IndirectOffsetOnAxis(lists[:, k % 4, q:q + 1], 0),
                                            y[:, k % 2, q, :], None, compute_op=ALU.add
                                            ).then_inc(added[k % 2], 16)

            def body(u, k):
                if before(u, U - 2):
                    gather(u + 2, (k + 2) % LOOP)
                if at_least(u, 1):
                    add(u - 1, (k - 1) % LOOP)

            for k in range(2):
                pool.dma_start(y[:, k, 0, :], acc[0:P, :]).then_inc(added[k], 16 * Q)
                gather(k, k, reused=False)
            steps(pool, body)
            add(U - 1, (U - 1) % LOOP)
            for k in range(2):
                pool.wait_ge(added[k], added_total(U - 2 + k, k))

        @block.tensor
        def _(pe):
            def turn_rows(u, k):
                pe.wait_ge(gathered[k % 2], dma_total(u, k))
                for kc in range(KC):
                    turn_ring.wait_free(pe, KC * u + kc)
                    for q in range(Q):
                        last = pe.transpose(turn[:, kc, q * P:(q + 1) * P],
                                            rows[:, k % 2, q, kc * P:(kc + 1) * P], c.ident[:])
                    last.then_inc(turned, 1)

            def multiply_up(u, k):
                b, eb = k % 2, k // 2
                turn_ring.wait_emptied(pe, KC * u + KC - 1)
                pe.wait_ge(w1_ready, splits(u, k))
                for j in range(J):
                    up_ring.wait_free(pe, J * u + j)
                    terms = [(w, x, kc) for kc in range(KC)
                             for w, x in ((w1_hi, xT_hi), (w1_hi, xT_lo), (w1_lo, xT_hi))]
                    for n, (w, x, kc) in enumerate(terms):
                        last = pe.matmul(up[:, j % 4, :], w[:, eb, kc, j * P:(j + 1) * P], x[:, b, kc, :],
                                         start=(n == 0), stop=(n == len(terms) - 1))
                    last.then_inc(up_done, 1)

            def multiply_down(u, k):
                b, eb = k % 2, k // 2
                act_ring.wait_emptied(pe, J * u + J - 1)
                pe.wait_ge(w2_ready, splits(u, k))
                for q in range(Q):
                    down_ring.wait_free(pe, Q * u + q)
                    terms = [(h, w, j) for j in range(J)
                             for h, w in ((h_hi, w2_hi), (h_hi, w2_lo), (h_lo, w2_hi))]
                    for n, (h, w, j) in enumerate(terms):
                        last = pe.matmul(down[:, q % 2, 0:C], h[:, b, j, q * P:(q + 1) * P], w[:, eb, j, :],
                                         start=(n == 0), stop=(n == len(terms) - 1))
                    last.then_inc(down_done, 1)

            def body(u, k):
                if before(u, U - 1):
                    turn_rows(u + 1, (k + 1) % LOOP)
                multiply_up(u, k)
                if at_least(u, 1):
                    multiply_down(u - 1, (k - 1) % LOOP)

            turn_rows(0, 0)
            steps(pe, body)
            multiply_down(U - 1, (U - 1) % LOOP)

        @block.scalar
        def _(act):
            def rows_hi(u, k, reused=True):
                if reused:
                    act.wait_ge(up_done, J * (u - 1))
                for kc in range(KC):
                    act.wait_ge(turned, KC * u + kc + 1)
                    act.activation(xT_hi[:, k % 2, kc, :], turn[:, kc, :], ACT.Copy).then_inc(xs_hi_ready, 1)

            def w1_piece(e, eb, j):
                act.wait_ge(w1_loaded, 16 * (e + 1))
                whole, hi, _ = piece(w1_in, w1_hi, w1_lo, eb, j)
                act.activation(hi, whole, ACT.Copy).then_inc(w1_hi_ready, 1)

            def w2_piece(e, eb, j):
                act.wait_ge(w2_loaded, 16 * (e + 1))
                whole, hi, _ = piece(w2_in, w2_hi, w2_lo, eb, j)
                act.activation(hi, whole, ACT.Copy).then_inc(w2_hi_ready, 1)

            def body(u, k):
                if before(u, U - 1):
                    rows_hi(u + 1, (k + 1) % LOOP, reused=at_least(u, 1))
                for j in range(J):
                    act.wait_ge(up_done, J * u + j + 1)
                    act_ring.wait_free(act, J * u + j)
                    up_ring.emptied(act.activation(act_f[:, j % 2, :], up[:, j % 4, :], ACT.Gelu))
                    if before(u, U - 2):
                        e = expert(u, k) + 1
                        if k % 2 == 0:
                            w1_piece(e, (k // 2 + 1) % 2, j)
                        else:
                            if j == 0 and at_least(u, 2):
                                act.wait_ge(down_done, Q * (u - 1))
                            w2_piece(e, (k // 2 + 1) % 2, j)

            for j in range(J):
                w1_piece(0, 0, j)
            for j in range(J):
                w2_piece(0, 0, j)
            rows_hi(0, 0, reused=False)
            steps(act, body)

        @block.vector
        def _(dve):
            def rows_lo(u, k, reused=True):
                for kc in range(KC):
                    dve.wait_ge(xs_hi_ready, KC * u + kc + 1)
                    turn_ring.emptied(dve.tensor_tensor(xT_lo[:, k % 2, kc, :], turn[:, kc, :],
                                                        xT_hi[:, k % 2, kc, :].bitcast(F32), ALU.subtract))
                dve.wait_ge(gathered[k % 2], dma_total(u, k))
                if reused:
                    down_ring.wait_emptied(dve, Q * (u - 3) - 1)
                dve.tensor_scalar(gain[:, k, :], rows[:, k % 2, :, ds(C + expert(u, k), 1)].rearrange("p q a -> p (q a)"),
                                  0.5, None, ALU.mult).then_inc(gained, 1)

            def w1_piece(e, eb, j):
                dve.wait_ge(w1_hi_ready, J * e + j + 1)
                whole, hi, lo = piece(w1_in, w1_hi, w1_lo, eb, j)
                dve.tensor_tensor(lo, whole, hi.bitcast(F32), ALU.subtract).then_inc(w1_ready, 1)

            def w2_piece(e, eb, j):
                dve.wait_ge(w2_hi_ready, J * e + j + 1)
                whole, hi, lo = piece(w2_in, w2_hi, w2_lo, eb, j)
                dve.tensor_tensor(lo, whole, hi.bitcast(F32), ALU.subtract).then_inc(w2_ready, 1)

            def scale(u, k):
                dve.wait_ge(gained, u + 1)
                dve.wait_ge(added[k % 2], added_total(u - 2, k))
                for q in range(Q):
                    dve.wait_ge(down_done, Q * u + q + 1)
                    down_ring.emptied(dve.tensor_scalar(y[:, k % 2, q, :], down[:, q % 2, 0:C],
                                                        gain[:, k, q:q + 1], None, ALU.mult))

            def body(u, k):
                if before(u, U - 1):
                    rows_lo(u + 1, (k + 1) % LOOP, reused=not (known(u) and u < 3))
                for j in range(J):
                    if j == 0 and not (known(u) and u < 2):
                        dve.wait_ge(down_done, Q * (u - 1))
                    up_ring.wait_emptied(dve, J * u + j)
                    dve.tensor_copy(h_hi[:, k % 2, j, :], act_f[:, j % 2, :]).then_inc(h_hi_ready, 1)
                    if before(u, U - 2):
                        e = expert(u, k) + 1
                        (w1_piece if k % 2 == 0 else w2_piece)(e, (k // 2 + 1) % 2, j)
                    dve.wait_ge(h_hi_ready, J * u + j + 1)
                    act_ring.emptied(dve.tensor_tensor(h_lo[:, k % 2, j, :], act_f[:, j % 2, :],
                                                       h_hi[:, k % 2, j, :].bitcast(F32), ALU.subtract))
                if at_least(u, 1):
                    scale(u - 1, (k - 1) % LOOP)

            for j in range(J):
                w1_piece(0, 0, j)
            for j in range(J):
                w2_piece(0, 0, j)
            rows_lo(0, 0, reused=False)
            steps(dve, body)
            scale(U - 1, (U - 1) % LOOP)



class Segment:

    FILLS = ("x", "qk", "v", "max", "top", "out", "att", "proj", "row", "gate")
    HIGHS = ("x", "qk", "att")

    def __init__(self, steps, before=None):
        self.steps = list(steps)
        fills = [s for s in self.steps if s[0] in self.FILLS]
        highs = [s for s in fills if s[0] in self.HIGHS]
        self.fills, self.highs = len(fills), len(highs)
        self.fill_first = before.fills if before else 0
        self.high_first = before.highs if before else 0
        self.fill_place = {s: k for k, s in enumerate(fills)}
        self.high_place = {s: k for k, s in enumerate(highs)}
        assert len(self.fill_place) == len(fills)


class Banks:

    def __init__(self, seg, ring, filled, highs, per_batch, b):
        self.seg, self.ring, self.filled, self.highs = seg, ring, filled, highs
        assert per_batch[0] % ring.depth == 0, per_batch
        again = (per_batch[0] * b, per_batch[1] * b) if seg.fill_first else (0, 0)
        self.first, self.high_first = seg.fill_first + again[0], seg.high_first + again[1]

    def bank(self, step):
        return (self.seg.fill_first + self.seg.fill_place[step]) % self.ring.depth

    def fill(self, pe, step):
        self.ring.wait_free(pe, self.first + self.seg.fill_place[step])
        return self.bank(step)

    def take(self, eng, step):
        eng.wait_ge(self.filled, self.first + self.seg.fill_place[step] + 1)
        return self.bank(step)

    def wait_emptied(self, eng, step):
        self.ring.wait_emptied(eng, self.first + self.seg.fill_place[step])

    def wait_high(self, eng, step):
        eng.wait_ge(self.highs, self.high_first + self.seg.high_place[step] + 1)


def attention_block(nc, s, c, x1, W1, b1, Wp, bp, x2, table, prob):
    B, T, C, TT, KC = s.B, s.T, s.C, s.TT, s.KC
    NH, G, D = 16, 4, 16
    HG = NH // G
    PART = 3 * D
    ROWS = 4 * D
    STACKING = 16 * 4
    SPILLING = 16 * 5
    VW = D + 1
    HALF = BANK
    HT = HALF // P
    SCALE = 1.0 / D ** 0.5
    NS = 2
    SETS = [(half, kt) for half in range(2) for kt in range(HT * (half + 1))]
    N = len(SETS)
    LAST = (HT - 1, N - 1)
    def products(tiles):
        return [(h, qt, k0, min(k0 + BANK, (qt + 1) * P)) for h in range(G) for qt in tiles for k0 in range(0, (qt + 1) * P, BANK)]
    EARLY, LATE = products(range(HT)), products(range(HT, TT))
    SHARES = [EARLY[0:5], EARLY[5:10], EARLY[10:]] + [LATE[n:n + 5] for n in range(0, len(LATE), 5)]
    assert len(SHARES) == N - 2
    TURNS = [(ch, half) for ch in range(KC) for half in range(2)]
    PAIRS = TT // 2

    def group(g, first=False, ahead=True, nxt=True, tail=False):
        for i in range(N):
            share = SHARES[i] if ahead and i < len(SHARES) else []
            for h in range(G):
                yield "scores", g, i, h
                for m in share[h:h + 1] if h < G - 1 else share[h:]:
                    yield ("max", g + 1) + m
            if i:
                yield "weigh", g, i - 1
            elif not first:
                yield "weigh", g - 1, N - 1
            if i == 1 and not first:
                yield "sums", g - 1, 1
            if i == 2 and not first:
                yield "out", g - 1, 1
            if i == HT + 1:
                yield "sums", g, 0
            if i == HT + 2:
                yield "out", g, 0
            if nxt and i in (3, 4):
                yield "qk", g + 2, i - 3
            if nxt and i == 4:
                yield "spill", g + 2
            if nxt and i == 8:
                yield "stack", g + 2, 0
            if ahead and i == 0 and not first:
                yield "stack", g + 1, 1
            if ahead and i == N - 2:
                yield "top", g + 1
            yield "beside", g, i

    def once(steps, beside):
        for s in steps:
            if s[0] == "beside":
                yield from beside.get(s[1:], [])
            else:
                yield s

    X = [("x", ch, half) for ch, half in TURNS]
    VALUES = [("v", n) for n in range(PAIRS)]
    ATT = [("att", ch, half) for ch, half in TURNS]
    PROJ = [("proj", t) for t in range(TT)]
    ROW = [("row", ch, half) for ch, half in TURNS]
    RESIDUAL = {(1, 1): [("residual",)], (2, 0): [("bias",)]}
    NEXT = {(1, 0): [("load",)], (1, 5): [("stats",)], (1, 6): [("norm",)], (1, 8): X[:2], (1, 9): X[2:],
            (3, 6): VALUES[0:1], (3, 8): VALUES[1:2], (3, 10): VALUES[2:3], (4, 0): VALUES[3:]}
    TAIL = {(4, 4): ATT, (4, 5): PROJ[:4], (4, 6): PROJ[4:] + [("send",)], (4, 7): [("gate_stats",)],
            (4, 8): [("rows",)], (4, 9): ROW, (4, 11): [("gate",)]}
    HEAD = Segment([("load",), ("stats",), ("norm",)] + X + [("qk", 4, 0), ("qk", 4, 1), ("spill", 4)]
                   + [("stack", 4, 0), ("stack", 4, 1)] + VALUES + [("qk", 5, 0), ("qk", 5, 1), ("spill", 5)]
                   + [("stack", 5, 0), ("stack", 5, 1)] + [("max", 4) + m for m in EARLY + LATE] + [("top", 4)]
                   + list(once(group(4, first=True), {})))
    LOOP = Segment(once([s for g in (1, 2, 3, 4) for s in group(g)], {**RESIDUAL, **NEXT, **TAIL}), HEAD)
    END = Segment(list(once([s for g in (1, 2, 3) for s in group(g, ahead=g < 3, nxt=g < 2)], RESIDUAL))
                  + [("weigh", 3, N - 1), ("sums", 3, 1), ("out", 3, 1)] + ATT + PROJ
                  + [("send",), ("gate_stats",), ("rows",)] + ROW + [("gate",)], HEAD)

    with ExitStack() as ctx:
        sb = lambda n, sh, d: ctx.enter_context(nc.sbuf_tensor(n + "_a", sh, d))
        ps = lambda n, sh: ctx.enter_context(nc.psum_tensor(n + "_a", sh, F32))
        sem = lambda n: c.sem(n + "_a")
        bankA, bankB, bankO = ps("bankA", [P, 3, BANK]), ps("bankB", [P, 3, BANK]), ps("bankO", [P, 2, BANK])
        gsb = lambda n, sh, d: ctx.enter_context(nc.sbuf_tensor(n, sh, d))
        m1 = Moments(s, gsb, c.sem, "_x1")
        g_ = Gate(s, gsb, c.sem, None, None, "_a")
        xin = sb("xin", [P, TT, C], F32)
        xres = sb("xres", [P, TT, C], F32)
        att = sb("att", [P, TT, C], F32)
        xT_hi, xT_lo = sb("aT_hi", [P, KC, T], F32R), sb("aT_lo", [P, KC, T], F32R)
        rT_hi, rT_lo = sb("rT_hi", [P, KC, T], F32R), sb("rT_lo", [P, KC, T], F32R)
        wqk_hi, wqk_lo = (sb(n, [P, KC, HG, P], F32R) for n in ("wqk_hi", "wqk_lo"))
        wv_hi, wv_lo = (sb(n, [P, KC, NH, D], F32R) for n in ("wv_hi", "wv_lo"))
        wp_hi, wp_lo = (sb(n, [P, KC, C], F32R) for n in ("wp_hi", "wp_lo"))
        bqk = sb("bqk", [P, HG], F32)
        bv = sb("bv", [P, NH, D], F32)
        bo = sb("bo", [P, C], F32)
        qk_hi, qk_lo = (sb(n, [P, T], F32R) for n in ("qk_hi", "qk_lo"))
        sq, sk = (sb(n, [P, NS, G, T], F32R) for n in ("sq", "sk"))
        val = sb("val", [P, TT, NH * VW + 16], F32)
        ex = sb("expo", [P, 2, G, BANK], F32)
        oT = sb("oT", [P, T], F32)
        tops = sb("tops", [P, G, TT, 2], F32)
        ntop = sb("ntop", [P, G * TT], F32)
        ntopT = sb("ntopT", [G * TT, P], F32R)
        inv = sb("invs", [P, 2, HT, G], F32)
        q_rows = nc.dram_tensor("q_rows", (NS, 2 * D + 1, G, T), F32).ap()
        k_rows = nc.dram_tensor("k_rows", (NS, 3 * D, G, T), F32).ap()

        A_filled, B_filled, O_filled = sem("A_filled"), sem("B_filled"), sem("O_filled")
        ringA, ringB, ringO = Ring(sem("A_free"), 3), Ring(sem("B_free"), 3), Ring(sem("O_free"), 2)
        w_loaded, w_hi_ready, w_ready, b_loaded, filled, padded, zero_out = (
            sem(n) for n in ("w_loaded", "w_hi_ready", "w_ready", "b_loaded", "filled", "padded", "zero_out"))
        x_loaded, res_loaded, an_ready, hi_ready = (sem(n) for n in ("x_loaded", "res_loaded", "an_ready", "hi_ready"))
        stacked = [[sem(f"stacked{k}{half}") for half in range(2)] for k in range(NS)]
        spilled, top_in = sem("spilled"), [sem(f"top_in{k}") for k in range(NS)]
        ntop_ready, masked, ex_used = (sem(n) for n in ("ntop_ready", "masked", "ex_used"))
        att_dve, sp_steps, pool_steps, biased, x2_ready, x2_out = (
            sem(n) for n in ("att_dve", "sp_steps", "pool_steps", "biased", "x2_ready", "x2_out"))
        DIAG = 2 * HT
        x1_v = x1.rearrange("(b t p) c -> b p t c", b=B, p=P)
        x2_v = x2.rearrange("(b t p) c -> b p t c", b=B, p=P)

        def banks(seg, b):
            return Banks(seg, ringA, A_filled, hi_ready, (LOOP.fills, LOOP.highs), b)

        def nth(g, b):
            return HG * b + g

        def turn_of(g, b):
            return (HG // NS) * b + g // NS + 1

        def cols(i):
            half, kt = SETS[i]
            return max(kt - HT * half, 0) * P

        def crosses(i):
            half, kt = SETS[i]
            return kt + 1 if kt >= HT * half else 0

        def score_bank(g, b, i, h):
            return G * (N * nth(g, b) + i) + h

        def bank_of(i, h):
            assert (HG * G * N) % 3 == 0 and (G * N) % 3 == 0
            return (G * i + h) % 3

        flat = g_.row[:].rearrange("p t r -> p (t r)")
        W1_in = flat[:, 0:KC * PART * NH].rearrange("p (k h r) -> p k h r", k=KC, r=PART)
        Wp_in = flat[:, KC * PART * NH:KC * (PART * NH + C)].rearrange("p (k n) -> p k n", k=KC)
        SPLITS = [(W1_in[:, k, :, part * D:(part + 1) * D].rearrange("p (a g) r -> p a g r", g=G),
                   *(w[:, k, :, part * G * D:(part + 1) * G * D].rearrange("p a (g r) -> p a g r", g=G)
                     for w in (wqk_hi, wqk_lo)))
                  for k in range(KC) for part in range(2)]
        SPLITS += [(W1_in[:, k, :, 2 * D:PART], wv_hi[:, k], wv_lo[:, k]) for k in range(KC)]
        SPLITS += [(Wp_in[:, k], wp_hi[:, k], wp_lo[:, k]) for k in range(KC)]
        BIASES = 2 * HG + 2
        block = ctx.enter_context(nc.Block())

        @block.sync
        def _(sp):
            def walk(seg, b):
                A = banks(seg, b)
                for step in seg.steps:
                    kind, a = step[0], step[1:]
                    if kind == "load":
                        sp.dma_start(xin[:], x1_v[b + 1]).then_inc(x_loaded, 16)
                    elif kind == "residual":
                        sp.wait_ge(x2_out, 16 * (b + 1))
                        sp.sem_inc(sp_steps, 1)
                        sp.dma_start(xres[:], x1_v[b]).then_inc(res_loaded, 16)
                    elif kind == "spill":
                        g, k = a[0], a[0] % NS
                        A.wait_emptied(sp, ("qk", g, 1))
                        sp.sem_inc(sp_steps, 1)
                        if seg is not HEAD or g > 5:
                            for half in range(2):
                                sp.wait_ge(stacked[k][half], STACKING * turn_of(g - 2, b))
                                sp.sem_inc(sp_steps, 1)
                        for row, rows, part, first in ((0, q_rows, qk_hi, 0), (D, q_rows, qk_lo, 0), (0, k_rows, qk_hi, G * D),
                                                       (D, k_rows, qk_lo, G * D), (2 * D, k_rows, qk_hi, G * D)):
                            sp.dma_start(rows[k, row:row + D].rearrange("r h t -> h r t"),
                                         part[first:first + G * D, :].bitcast(F32)).then_inc(spilled, 16)
                    elif kind == "stack":
                        g, half = a
                        k, cut = g % NS, slice(half * HALF, (half + 1) * HALF)
                        sp.wait_ge(spilled, SPILLING * (nth(g, b) + 1))
                        sp.sem_inc(sp_steps, 1)
                        if (seg is not HEAD) or g > 5:
                            sp.wait_ge(ex_used, N * nth(g - 2, b) + (2 * HT if half == 0 else N))
                        for row, stack, rows, first, n in ((0, sq, q_rows, 0, 2 * D), (2 * D, sq, q_rows, 0, 2 * D + 1),
                                                           (0, sk, k_rows, 0, 2 * D), (2 * D, sk, k_rows, D, 2 * D)):
                            sp.dma_start(stack[row:row + n, k, :, cut].bitcast(F32),
                                         rows[k, first:first + n, :, cut]).then_inc(stacked[k][half], 16)
                    elif kind == "top":
                        g, k = a[0], a[0] % NS
                        A.wait_emptied(sp, step)
                        sp.dma_start(sq[ROWS:ROWS + 1, k, :, :].bitcast(F32).rearrange("p g (t q) -> p (g t) q", q=P),
                                     ntopT[:].bitcast(F32)).then_inc(top_in[k], 16)
                    elif kind == "send":
                        sp.wait_ge(x2_ready, b + 1)
                        sp.dma_start(x2_v[b], xres[:]).then_inc(x2_out, 16)
                    elif kind == "gate":
                        gate_table(g_, sp, b, table)

            for r in (ringA, ringB, ringO):
                r.start(sp)
            sp.sem_inc(g_.table_out, 16)
            sp.sem_inc(x2_out, 16)
            sp.dma_start(W1_in.rearrange("p k h r -> p k (h r)"), W1.rearrange("(k p) n -> p k n", p=P)).then_inc(w_loaded, 16)
            sp.dma_start(Wp_in, Wp.rearrange("(k p) n -> p k n", p=P)).then_inc(w_loaded, 16)
            with nc.allow_non_contiguous_dma(reason="biases, a few hundred bytes each"):
                for a in range(HG):
                    for part in range(2):
                        sp.dma_start(bqk[part * G * D:(part + 1) * G * D, a:a + 1],
                                     b1.rearrange("(a g s r) -> a s g r", a=HG, g=G, r=D)[a, part].unsqueeze(2)).then_inc(b_loaded, 16)
                sp.dma_start(bv[:], b1.rearrange("(h r) -> h r", h=NH)[:, 2 * D:PART].unsqueeze(0).to_broadcast([P, NH, D])
                             ).then_inc(b_loaded, 16)
                sp.dma_start(bo[:], bp.unsqueeze(0).to_broadcast([P, C])).then_inc(b_loaded, 16)
            sp.wait_ge(filled, 2)
            sp.wait_ge(padded, 1)
            for k in range(NS):
                sp.dma_start(q_rows[k, 2 * D:2 * D + 1], sq[ROWS:ROWS + 1, k, :, :].bitcast(F32)).then_inc(zero_out, 16)
            sp.wait_ge(zero_out, 16 * NS)
            walk(HEAD, -1)
            with sp.Fori(0, B - 1) as b:
                walk(LOOP, b)
            walk(END, B - 1)
            sp.wait_ge(x2_out, 16 * (B + 1))
            sp.wait_ge(g_.table_out, 16 * (B + 1))

        @block.gpsimd
        def _(pool):
            def walk(seg, b):
                for step in seg.steps:
                    kind, a = step[0], step[1:]
                    if kind == "stats":
                        gate_rstd(m1, pool, b + 1, c.power)
                    elif kind == "gate_stats":
                        gate_rstd(g_, pool, b, c.power)
                    elif kind == "bias":
                        pool.wait_ge(res_loaded, 16 * (b + 1))
                        pool.tensor_tensor(xres[:], xres[:], bo[:].unsqueeze(1).to_broadcast([P, TT, C]), ALU.add).then_inc(biased, 1)
                    elif kind == "weigh" and crosses(a[1]):
                        g, i = a
                        ringB.wait_emptied(pool, score_bank(g, b, i, G - 1))
                        pool.sem_inc(pool_steps, 1)
                        pool.affine_select(out=ex[:, i % 2, :, 0:P], in_=ex[:, i % 2, :, 0:P], compare_op=ALU.is_ge,
                                           fill=0.0, base=0, pattern=[[0, G], [1, P]],
                                           channel_multiplier=-1).then_inc(masked, 1)

            pool.memset(sk[ROWS:P, :, :, :].bitcast(F32), 0.0).then_inc(filled, 1)
            pool.wait_ge(filled, 1)
            pool.memset(sk[ROWS:ROWS + 1, :, :, :].bitcast(F32), 1.0).then_inc(filled, 1)
            pool.wait_ge(filled, 2)
            pool.wait_ge(b_loaded, 16 * BIASES)
            walk(HEAD, -1)
            with pool.Fori(0, B - 1) as b:
                walk(LOOP, b)
            walk(END, B - 1)

        @block.tensor
        def _(pe):
            def split3(out, lhs, rhs, n, last):
                pe.matmul(out, lhs[0], rhs[0], start=(n == 0), stop=False)
                pe.matmul(out, lhs[0], rhs[1], start=False, stop=False)
                return pe.matmul(out, lhs[1], rhs[0], start=False, stop=last)

            def rows_by(bank, xs, ws, t):
                for ch in range(KC):
                    cut = slice(t * P, (t + 1) * P)
                    last = split3(bank, (xs[0][:, ch, cut], xs[1][:, ch, cut]), (ws[0][:, ch], ws[1][:, ch]), ch, ch == KC - 1)
                return last

            def walk(seg, b):
                A = banks(seg, b)
                for step in seg.steps:
                    kind, a = step[0], step[1:]
                    if kind in ("x", "att", "row"):
                        src = {"x": xin, "att": att, "row": g_.row}[kind]
                        ch, half = a
                        if a == TURNS[0]:
                            if kind == "x":
                                pe.wait_ge(an_ready, b + 2)
                            elif kind == "att":
                                A.wait_emptied(pe, ("out", 3, 1))
                            else:
                                pe.wait_ge(g_.row_ready, b + 1)
                        k = A.fill(pe, step)
                        for t in range(HT):
                            last = pe.transpose(bankA[:, k, t * P:(t + 1) * P],
                                                src[:, HT * half + t, ch * P:(ch + 1) * P], c.ident[:])
                        last.then_inc(A_filled, 1)
                    elif kind == "qk":
                        g, half = a
                        if seg is HEAD and g == 4:
                            A.wait_emptied(pe, X[-1])
                        k = A.fill(pe, step)
                        for ch in range(KC):
                            cut = slice(half * HALF, (half + 1) * HALF)
                            last = split3(bankA[:, k, :], (wqk_hi[:, ch, g % HG, :], wqk_lo[:, ch, g % HG, :]),
                                          (xT_hi[:, ch, cut], xT_lo[:, ch, cut]), ch, ch == KC - 1)
                        last.then_inc(A_filled, 1)
                    elif kind == "v":
                        k = A.fill(pe, step)
                        for n in range(2):
                            last = rows_by(bankA[:, k, n * C:(n + 1) * C], (xT_hi, xT_lo), (wv_hi, wv_lo), 2 * a[0] + n)
                        last.then_inc(A_filled, 1)
                    elif kind == "proj":
                        if a[0] == 0:
                            A.wait_emptied(pe, ATT[-1])
                        k = A.fill(pe, step)
                        rows_by(bankA[:, k, 0:C], (rT_hi, rT_lo), (wp_hi, wp_lo), a[0]).then_inc(A_filled, 1)
                    elif kind == "max":
                        g, h, qt, k0, k1 = a
                        for half, first in ((0, EARLY[0]), (1, LATE[0])):
                            if a[1:] == first:
                                pe.wait_ge(stacked[g % NS][half], STACKING * turn_of(g, b))
                        k = A.fill(pe, step)
                        crossing = k1 == (qt + 1) * P
                        last = pe.matmul(bankA[:, k, 0:k1 - k0], sq[:, g % NS, h, qt * P:(qt + 1) * P],
                                         sk[:, g % NS, h, k0:k1], start=True, stop=not crossing)
                        if crossing:
                            last = pe.matmul(bankA[:, k, k1 - k0 - P:k1 - k0], c.identb[:], c.later[:], start=False, stop=True)
                        last.then_inc(A_filled, 1)
                    elif kind == "top":
                        pe.wait_ge(ntop_ready, nth(a[0], b) + 1)
                        k = A.fill(pe, step)
                        pe.transpose(bankA[0:G * TT, k, 0:P], ntop[:], c.ident[:]).then_inc(A_filled, 1)
                    elif kind == "scores":
                        g, i, h = a
                        if i == 0 and h == 0:
                            pe.wait_ge(top_in[g % NS], 16 * turn_of(g, b))
                        half, kt = SETS[i]
                        q0 = half * HALF + cols(i)
                        ringB.wait_free(pe, score_bank(g, b, i, h))
                        pe.matmul(bankB[:, bank_of(i, h), 0:HALF - cols(i)], sk[:, g % NS, h, kt * P:(kt + 1) * P],
                                  sq[:, g % NS, h, q0:(half + 1) * HALF], start=True, stop=True).then_inc(B_filled, 1)
                    elif kind == "weigh":
                        g, i = a
                        half, kt = SETS[i]
                        ringB.wait_emptied(pe, score_bank(g, b, i, G - 1))
                        if crosses(i):
                            pe.wait_ge(masked, DIAG * nth(g, b) + crosses(i))
                        if kt == 0:
                            ringO.wait_free(pe, 2 * nth(g, b) + half)
                        for h in range(G):
                            v0 = VW * (g % HG * G + h)
                            last = pe.matmul(bankO[32 * h:32 * (h + 1), half, cols(i):HALF], val[:, kt, v0:v0 + 32],
                                             ex[:, i % 2, h, 0:HALF - cols(i)], start=(kt == 0), stop=(i == LAST[half]))
                        last.then_inc(ex_used, 1)
                    elif kind == "out":
                        g, half = a
                        ringO.wait_emptied(pe, 2 * nth(g, b) + half)
                        k = A.fill(pe, step)
                        for t in range(HT):
                            q0 = half * HALF + t * P
                            last = pe.transpose(bankA[:, k, t * P:(t + 1) * P], oT[:, q0:q0 + P], c.ident[:])
                        last.then_inc(A_filled, 1)
                    elif kind == "gate":
                        A.wait_emptied(pe, ROW[-1])
                        k = A.fill(pe, step)
                        for t in range(TT):
                            for ch in range(KC):
                                last = pe.matmul(bankA[:, k, t * s.E:(t + 1) * s.E], g_.xT[:, ch, t * P:(t + 1) * P],
                                                 c.gate[:, ch, :], start=(ch == 0), stop=(ch == KC - 1))
                        last.then_inc(A_filled, 1)

            pe.wait_ge(w_ready, len(SPLITS))
            pe.wait_ge(filled, 2)
            pe.wait_ge(padded, 3)
            walk(HEAD, -1)
            with pe.Fori(0, B - 1) as b:
                walk(LOOP, b)
            walk(END, B - 1)

        @block.scalar
        def _(act):
            def walk(seg, b):
                A = banks(seg, b)
                for step in seg.steps:
                    kind, a = step[0], step[1:]
                    if kind in ("x", "att"):
                        k = A.take(act, step)
                        ch, half = a
                        to = xT_hi if kind == "x" else rT_hi
                        act.activation(to[:, ch, half * HALF:(half + 1) * HALF], bankA[:, k, :], ACT.Copy).then_inc(hi_ready, 1)
                    elif kind == "qk":
                        g, half = a
                        k = A.take(act, step)
                        if half == 0 and not (seg is HEAD and g == 4):
                            act.wait_ge(spilled, SPILLING * nth(g, b))
                        act.activation(qk_hi[:, half * HALF:(half + 1) * HALF], bankA[:, k, :], ACT.Identity,
                                       bias=bqk[:, g % HG:g % HG + 1]).then_inc(hi_ready, 1)
                    elif kind == "scores":
                        g, i, h = a
                        act.wait_ge(B_filled, score_bank(g, b, i, h) + 1)
                        if h == 0 and not (seg is HEAD and i < 2):
                            act.wait_ge(ex_used, N * nth(g, b) + i - 1)
                        ringB.emptied(act.activation(ex[:, i % 2, h, 0:HALF - cols(i)],
                                                     bankB[:, bank_of(i, h), 0:HALF - cols(i)], ACT.Exp, scale=SCALE))
                    elif kind == "sums":
                        g, half = a
                        act.wait_ge(ex_used, N * nth(g, b) + LAST[half] + 1)
                        ringO.emptied(act.activation(oT[:, half * HALF:(half + 1) * HALF], bankO[:, half, :], ACT.Copy))
                    elif kind == "gate":
                        A.wait_emptied(act, step)
                        act.activation(g_.ex[:], g_.sub[:], ACT.Exp).then_inc(g_.ex_ready, 1)

            act.wait_ge(w_loaded, 32)
            for whole, hi, _ in SPLITS:
                act.activation(hi, whole, ACT.Copy).then_inc(w_hi_ready, 1)
            act.wait_ge(b_loaded, 16 * BIASES)
            walk(HEAD, -1)
            with act.Fori(0, B - 1) as b:
                walk(LOOP, b)
            walk(END, B - 1)

        @block.vector
        def _(dve):
            def walk(seg, b):
                A = banks(seg, b)
                norm = Chain(dve, m1.dve, Moments.DVE_STEPS * (b + 1))
                gate = Chain(dve, g_.dve, Gate.DVE_STEPS * b)
                for step in seg.steps:
                    kind, a = step[0], step[1:]
                    if kind == "stats":
                        dve.wait_ge(x_loaded, 16 * (b + 2))
                        gate_stats(m1, dve, norm, xin)
                    elif kind == "norm":
                        dve.wait_ge(m1.rstd_ready, b + 2)
                        for t in range(TT):
                            last = dve.tensor_scalar(xin[:, t, :], xin[:, t, :], m1.mv[:, t, 0:1], m1.rstd[:, t:t + 1],
                                                     ALU.subtract, ALU.mult)
                        last.then_inc(an_ready, 1)
                    elif kind in ("x", "att"):
                        ch, half = a
                        hi, lo = (xT_hi, xT_lo) if kind == "x" else (rT_hi, rT_lo)
                        cut = slice(half * HALF, (half + 1) * HALF)
                        A.wait_high(dve, step)
                        ringA.emptied(dve.tensor_tensor(lo[:, ch, cut], bankA[:, A.bank(step), :], hi[:, ch, cut].bitcast(F32),
                                                        ALU.subtract))
                    elif kind == "qk":
                        g, half = a
                        cut = slice(half * HALF, (half + 1) * HALF)
                        A.wait_high(dve, step)
                        ringA.emptied(dve.scalar_tensor_tensor(qk_lo[:, cut], bankA[:, A.bank(step), :], bqk[:, g % HG:g % HG + 1],
                                                               qk_hi[:, cut].bitcast(F32), ALU.add, ALU.subtract))
                    elif kind == "v":
                        k = A.take(dve, step)
                        ringA.emptied(dve.tensor_tensor(
                            val[:, 2 * a[0]:2 * a[0] + 2, 0:NH * VW].rearrange("p n (h w) -> p n h w", w=VW)[:, :, :, 0:D],
                            bankA[:, k, :].rearrange("p (n h d) -> p n h d", n=2, d=D),
                            bv[:].unsqueeze(1).to_broadcast([P, 2, NH, D]), ALU.add))
                    elif kind == "max":
                        g, h, qt, k0, k1 = a
                        k = A.take(dve, step)
                        ringA.emptied(dve.tensor_reduce(tops[:, h, qt, k0 // BANK:k0 // BANK + 1], bankA[:, k, 0:k1 - k0],
                                                        AX.X, ALU.max))
                        if a[1:] == LATE[-1]:
                            A.wait_emptied(dve, step)
                            dve.tensor_reduce(ntop[:].rearrange("p (g t) -> p g t", g=G), tops[:], AX.X, ALU.max,
                                              negate=True).then_inc(ntop_ready, 1)
                    elif kind == "top":
                        k = A.take(dve, step)
                        g = a[0]
                        if not (seg is HEAD and g == 4):
                            dve.wait_ge(top_in[(g - 1) % NS], 16 * turn_of(g - 1, b))
                        ringA.emptied(dve.tensor_copy(ntopT[:], bankA[0:G * TT, k, 0:P]))
                    elif kind == "out":
                        g, half = a
                        k = A.take(dve, step)
                        sums = bankA[:, k, :].rearrange("p (t g d) -> p t g d", t=HT, g=G)
                        dve.reciprocal(inv[:, half].unsqueeze(3), sums[:, :, :, D:D + 1]).then_inc(att_dve, 1)
                        dve.wait_ge(att_dve, 2 * nth(g, b) + half + 1)
                        to = att[:, HT * half:HT * (half + 1), g % HG * G * D:(g % HG + 1) * G * D]
                        ringA.emptied(dve.tensor_tensor(to.rearrange("p t (g d) -> p t g d", g=G), sums[:, :, :, 0:D],
                                                        inv[:, half].unsqueeze(3).to_broadcast([P, HT, G, D]), ALU.mult))
                    elif kind == "proj":
                        if a[0] == 0:
                            dve.wait_ge(biased, b + 1)
                        k = A.take(dve, step)
                        ringA.emptied(dve.tensor_tensor(xres[:, a[0], :], bankA[:, k, 0:C], xres[:, a[0], :], ALU.add))
                    elif kind == "send":
                        A.wait_emptied(dve, PROJ[-1])
                        dve.sem_inc(x2_ready, 1)
                    elif kind == "gate_stats":
                        gate_stats(g_, dve, gate, xres)
                    elif kind == "rows":
                        gate_rows(g_, dve, b, xres)
                    elif kind == "row":
                        k = A.take(dve, step)
                        ringA.emptied(dve.tensor_copy(g_.xT[:, a[0], a[1] * HALF:(a[1] + 1) * HALF], bankA[:, k, :]))
                    elif kind == "gate":
                        k = A.take(dve, step)
                        score = bankA[:, k, 0:TT * s.E].rearrange("p (t e) -> p t e", e=s.E)
                        gate.did(dve.tensor_reduce(g_.top[:], score, AX.X, ALU.max))
                        gate.settle()
                        ringA.emptied(dve.tensor_tensor(g_.sub[:], score, g_.top[:].unsqueeze(2).to_broadcast([P, TT, s.E]),
                                                        ALU.subtract))
                        gate_softmax_back(g_, dve, gate, b, prob)
                assert norm.n in (0, Moments.DVE_STEPS) and gate.n in (0, Gate.DVE_STEPS)

            for n, (whole, hi, lo) in enumerate(SPLITS):
                dve.wait_ge(w_hi_ready, n + 1)
                dve.tensor_tensor(lo, whole, hi.bitcast(F32), ALU.subtract).then_inc(w_ready, 1)
            dve.memset(sq[ROWS:P, :, :, :].bitcast(F32), 0.0).then_inc(padded, 1)
            dve.memset(tops[:], -3e38).then_inc(padded, 1)
            dve.memset(val[:], 1.0).then_inc(padded, 1)
            dve.wait_ge(padded, 3)
            dve.wait_ge(w_ready, len(SPLITS))
            walk(HEAD, -1)
            with dve.Fori(0, B - 1) as b:
                walk(LOOP, b)
            walk(END, B - 1)



def macaron_layer(nc, x, W1, b1, Wp, bp, gate_w, w1, w2, out):
    s = Shapes(x, gate_w, w1)
    with ExitStack() as ctx:
        c = Constants(nc, ctx, s, gate_w)
        prob = ctx.enter_context(nc.sbuf_tensor("prob", [P, s.BE * s.TT], F32))
        index = ctx.enter_context(nc.sbuf_tensor("index", [P, s.E * s.ST], U32))
        table = nc.dram_tensor("table", (s.B * s.T, s.ROW), F32).ap()
        x1 = nc.dram_tensor("x1", (s.B * s.T, s.C), F32).ap()
        x2 = out.rearrange("b t c -> (b t) c")
        norm_block(nc, s, c, x, table, x1, prob)
        route_block(nc, s, c, prob, index, "_1")
        experts_block(nc, s, c, w1, w2, table, x1, index, "_1")
        attention_block(nc, s, c, x1, W1, b1, Wp, bp, x2, table, prob)
        route_block(nc, s, c, prob, index, "_2")
        experts_block(nc, s, c, w1, w2, table, x2, index, "_2")


_INS = ["L0_attn_x", "L0_attn_W1", "L0_attn_b1", "L0_attn_Wp", "L0_attn_bp", "L0_ffn_gate_w", "L0_ffn_w1", "L0_ffn_w2"]
_OUTS = [((4, 1024, 256), "float32")]


def kernel(**inputs):
    import numpy as _np
    import concourse.bacc as _bacc
    from concourse import mybir as _mybir
    from concourse.bass_utils import run_bass_kernel_spmd as _run

    nc = _bacc.Bacc("TRN2", target_bir_lowering=False, num_devices=1)
    arrays, args = {}, []
    for name in _INS:
        a = _np.ascontiguousarray(inputs[name])
        arrays[f"in_{name}_dram"] = a
        args.append(nc.dram_tensor(f"in_{name}_dram", a.shape, _mybir.dt.from_np(a.dtype), kind="ExternalInput").ap())
    for i, (shape, dtype) in enumerate(_OUTS):
        dt = _mybir.dt.from_np(_np.dtype(dtype))
        args.append(nc.dram_tensor(f"out_{i}_dram", shape, dt, kind="ExternalOutput").ap())
    macaron_layer(nc, *args)
    r = _run(nc, [arrays], core_ids=[0])
    got = tuple(r.results[0][f"out_{i}_dram"] for i in range(len(_OUTS)))
    return got[0]
```

```python
from contextlib import ExitStack

import concourse.bass as bass
from concourse import mybir

ALU = mybir.AluOpType
ACT = mybir.ActivationFunctionType
AX = mybir.AxisListType
F32 = mybir.dt.float32
F32R = mybir.dt.float32r
BF16 = mybir.dt.bfloat16
F16 = mybir.dt.float16
I32 = mybir.dt.int32
U32 = mybir.dt.uint32

P = 128
PAD = 32
BANK = 512
LN_EPS = 1e-5
DIGITS = 15
TOGETHER = 5
ds = bass.ds


class Shapes:

    def __init__(self, x, gate_w, w1):
        self.B, self.T, self.C = x.shape
        self.E = gate_w.shape[1]
        self.H = w1.shape[2]
        self.CAP = 2 * self.T // self.E
        self.TT = self.T // P
        self.KC = self.C // P
        self.J = self.H // P
        self.BE = self.B * self.E
        self.ROW = self.C + self.E
        self.SH = self.CAP // P
        self.ST = self.B * self.SH
        self.U = 2 * self.E
        self.Q = self.ST // 2
        assert self.CAP == 2 * P and self.KC == 2 and self.ST == 8 and self.TT == 8 and self.E == 8


class Ring:

    def __init__(self, sem, depth):
        self.sem, self.depth = sem, depth

    def start(self, eng):
        eng.sem_inc(self.sem, self.depth)

    def wait_free(self, eng, k):
        eng.wait_ge(self.sem, k + 1)

    def emptied(self, ins):
        ins.then_inc(self.sem, 1)

    def wait_emptied(self, eng, k):
        eng.wait_ge(self.sem, k + 1 + self.depth)


class Chain:

    def __init__(self, eng, sem, base=0):
        self.eng, self.sem, self.base, self.n = eng, sem, base, 0

    def did(self, ins):
        ins.then_inc(self.sem, 1)
        self.n += 1

    def settle(self):
        self.eng.wait_ge(self.sem, self.base + self.n)

    def pause(self):
        self.settle()
        self.eng.sem_inc(self.sem, 1)
        self.n += 1



class Moments:

    DVE_STEPS = 3

    def __init__(self, s, sb, sem, tag):
        self.s = s
        self.stats = sb(f"stats{tag}", [P, s.TT, 6], F32)
        self.mv = sb(f"mean_var{tag}", [P, s.TT, 2], F32)
        self.ve = sb(f"var_eps{tag}", [P, s.TT], F32)
        self.rstd = sb(f"rstd{tag}", [P, s.TT], F32)
        self.dve = sem(f"norm_dve{tag}")
        self.var_ready = sem(f"var_ready{tag}")
        self.rstd_ready = sem(f"rstd_ready{tag}")


class Gate(Moments):

    DVE_STEPS = Moments.DVE_STEPS + 4

    def __init__(self, s, sb, sem, turn, score, tag, like=None):
        super().__init__(s, sb, sem, tag)
        self.turn, self.score = turn, score
        self.row = sb(f"row{tag}", [P, s.TT, s.ROW], F32)
        self.xT = sb(f"xT{tag}", [P, s.KC, s.T], F32)
        self.top = sb(f"top{tag}", [P, s.TT], F32)
        self.sub = sb(f"sub{tag}", [P, s.TT, s.E], F32)
        self.ex = sb(f"ex{tag}", [P, s.TT, s.E], F32)
        self.tot = sb(f"tot{tag}", [P, s.TT], F32)
        self.inv = sb(f"inv{tag}", [P, s.TT], F32)
        self.wide = sb(f"wide{tag}", [P, 2 * P], F32)
        self.row_ready = sem(f"row_ready{tag}")
        self.turned = sem(f"turned{tag}")
        self.turn_ring = Ring(sem(f"turn_free{tag}"), turn.shape[1] if turn is not None else 1)
        own = lambda name, shared: sem(f"{name}{tag}") if like is None else shared
        self.wide_ready = own("wide_ready", like and like.wide_ready)
        self.wide_copied = own("wide_copied", like and like.wide_copied)
        self.score_ready = own("score_ready", like and like.score_ready)
        self.sub_ready = own("sub_ready", like and like.sub_ready)
        self.ex_ready = sem(f"ex_ready{tag}")
        self.prob_ready = sem(f"prob_ready{tag}")
        self.table_out = sem(f"table_out{tag}")


def gate_stats(g, dve, chain, x):
    s = g.s
    for t in range(s.TT):
        last = dve.bn_stats(g.stats[:, t, :], x[:, t, :])
    chain.did(last)
    chain.pause()
    for t in range(s.TT):
        last = dve.bn_aggr(g.mv[:, t, :], g.stats[:, t, :])
    chain.did(last)
    chain.settle()
    dve.tensor_scalar(g.ve[:], g.mv[:, :, 1], LN_EPS, None, ALU.add).then_inc(g.var_ready, 1)


def gate_rstd(g, pool, b, power):
    pool.wait_ge(g.var_ready, b + 1)
    pool.tensor_tensor(g.rstd[:], g.ve[:], power[:], ALU.pow).then_inc(g.rstd_ready, 1)


def gate_rows(g, dve, b, x):
    s = g.s
    dve.wait_ge(g.rstd_ready, b + 1)
    dve.wait_ge(g.table_out, 16 * (b + 1))
    for t in range(s.TT):
        last = dve.tensor_scalar(g.row[:, t, 0:s.C], x[:, t, :], g.mv[:, t, 0:1], g.rstd[:, t:t + 1],
                                 ALU.subtract, ALU.mult)
    last.then_inc(g.row_ready, 1)


def gate_turn(g, pe, n, ident):
    c, half = n // 2, n % 2
    pe.wait_ge(g.row_ready, 1)
    g.turn_ring.wait_free(pe, n)
    for t in range(4):
        last = pe.transpose(g.turn[:, n % g.turn_ring.depth, t * P:(t + 1) * P],
                            g.row[:, 4 * half + t, c * P:(c + 1) * P], ident[:])
    last.then_inc(g.turned, 1)


def gate_score(g, pe, gate, wide):
    s = g.s
    for c in range(s.KC):
        for quarter in range(4):
            last = pe.matmul(wide[quarter * PAD:(quarter + 1) * PAD, :], gate[:, c, :],
                             g.xT[:, c, quarter * 2 * P:(quarter + 1) * 2 * P], start=(c == 0), stop=(c == s.KC - 1))
    last.then_inc(g.wide_ready, 1)


def gate_score_copy(g, dve, nth, wide):
    dve.wait_ge(g.wide_ready, nth + 1)
    dve.tensor_copy(g.wide[:], wide).then_inc(g.wide_copied, 1)


def gate_score_turn(g, pe, nth, score, ident):
    pe.wait_ge(g.wide_copied, nth + 1)
    for n in range(2):
        last = pe.transpose(score[:, n * P:(n + 1) * P], g.wide[:, n * P:(n + 1) * P], ident[:])
    return last


def by_tile(g, score):
    return score.rearrange("p (n q e) -> p q n e", n=2, q=4)[:, :, :, 0:g.s.E]


def gate_copy(g, act, n):
    c, half = n // 2, n % 2
    act.wait_ge(g.turned, n + 1)
    g.turn_ring.emptied(act.activation(g.xT[:, c, half * BANK:(half + 1) * BANK],
                                       g.turn[:, n % g.turn_ring.depth, :], ACT.Copy))


def gate_exp(g, act, b):
    act.wait_ge(g.sub_ready, b + 1)
    act.activation(g.ex[:], g.sub[:], ACT.Exp).then_inc(g.ex_ready, 1)


def gate_softmax_front(g, dve, chain, score):
    s = g.s
    split = lambda v: v.rearrange("p (q n) -> p q n", n=2)
    chain.did(dve.tensor_reduce(split(g.top[:]), by_tile(g, score), AX.X, ALU.max))
    chain.settle()
    return dve.tensor_tensor(g.sub[:].rearrange("p (q n) e -> p q n e", n=2), by_tile(g, score),
                             split(g.top[:]).unsqueeze(3).to_broadcast([P, 4, 2, s.E]), ALU.subtract)


def gate_softmax_back(g, dve, chain, nth, prob, b):
    s = g.s
    dve.wait_ge(g.ex_ready, nth + 1)
    chain.did(dve.tensor_reduce(g.tot[:], g.ex[:], AX.X, ALU.add))
    chain.settle()
    chain.did(dve.reciprocal(g.inv[:], g.tot[:]))
    chain.settle()
    chain.did(dve.tensor_tensor(g.row[:, :, s.C:s.ROW], g.ex[:],
                                g.inv[:].unsqueeze(2).to_broadcast([P, s.TT, s.E]), ALU.mult))
    chain.settle()
    dve.tensor_copy(prob[:, ds(b * s.TT * s.E, s.TT * s.E)].rearrange("p (t e) -> p t e", t=s.TT),
                    g.row[:, :, s.C:s.ROW]).then_inc(g.prob_ready, 1)


def gate_table(g, sp, nth, table, b):
    s = g.s
    sp.wait_ge(g.prob_ready, nth + 1)
    dst = table.rearrange("(b t p) r -> b p t r", b=s.B, p=P)[b]
    sp.dma_start(dst, g.row[:]).then_inc(g.table_out, 16)


def gate_start(g, eng):
    eng.sem_inc(g.table_out, 16)
    g.turn_ring.start(eng)


def norm_block(nc, s, c, x, table, acc, prob):
    with ExitStack() as ctx:
        sb = lambda n, sh, d: ctx.enter_context(nc.sbuf_tensor(n, sh, d))
        ps = lambda n, sh: ctx.enter_context(nc.psum_tensor(n, sh, F32))
        xin = [sb(f"xin{b}", [P, s.TT, s.C], F32) for b in range(s.B)]
        gates = []
        for b in range(s.B):
            gates.append(Gate(s, sb, c.sem, ps(f"turn_n{b}", [P, 1, BANK]), ps(f"score_n{b}", [P, 2 * P]), f"_n{b}",
                              like=gates[0] if gates else None))
        x_loaded = [c.sem(f"x_loaded{b}") for b in range(s.B)]
        c.patterns(s, sb)
        batches = list(enumerate(gates))
        pairs = [gates[b:b + 2] for b in range(0, s.B, 2)]
        block = ctx.enter_context(nc.Block())

        @block.sync
        def _(sp):
            for b, g in batches:
                gate_start(g, sp)
                sp.dma_start(xin[b][:], x.rearrange("b (t p) c -> b p t c", p=P)[b]).then_inc(x_loaded[b], 16)
            sp.wait_ge(c.gate_blank, 1)
            sp.dma_start(c.gate[:, :, 0:s.E], c.gate_w.rearrange("(k p) e -> p k e", p=P)).then_inc(c.gate_in, 16)
            sp.dma_start(acc, x.rearrange("b t c -> (b t) c")).then_inc(c.acc_init, 16)
            for b, g in batches:
                gate_table(g, sp, 0, table, b)
            for b, g in batches:
                sp.wait_ge(g.table_out, 32)

        @block.gpsimd
        def _(pool):
            make_constants(nc, c, s, pool)
            for b, g in batches:
                gate_rstd(g, pool, 0, c.power)
            make_more_constants(nc, c, s, pool)

        @block.tensor
        def _(pe):
            pe.wait_ge(c.first_made, 2)
            pe.wait_ge(c.gate_in, 16)
            for pair in pairs:
                for n in range(4):
                    for g in pair:
                        gate_turn(g, pe, n, c.ident)
            for b, g in batches:
                g.turn_ring.wait_emptied(pe, 3)
                gate_score(g, pe, c.gate, g.turn[:, 0, 0:2 * P])
            for b, g in batches:
                gate_score_turn(g, pe, b, g.score[:], c.ident).then_inc(g.score_ready, 1)

        @block.scalar
        def _(act):
            for pair in pairs:
                for n in range(4):
                    for g in pair:
                        gate_copy(g, act, n)
            for b, g in batches:
                gate_exp(g, act, b)

        @block.vector
        def _(dve):
            chains = [Chain(dve, g.dve) for g in gates]
            for b, g in batches:
                dve.wait_ge(x_loaded[b], 16)
                gate_stats(g, dve, chains[b], xin[b])
                if b:
                    gate_rows(gates[b - 1], dve, 0, xin[b - 1])
            gate_rows(gates[-1], dve, 0, xin[-1])
            dve.wait_ge(c.made, c.MADE)
            convert_constants(nc, c, dve)
            for b, g in batches:
                gate_score_copy(g, dve, b, g.turn[:, 0, 0:2 * P])
            for b, g in batches:
                dve.wait_ge(g.score_ready, b + 1)
                gate_softmax_front(g, dve, chains[b], g.score[:]).then_inc(g.sub_ready, 1)
            for b, g in batches:
                gate_softmax_back(g, dve, chains[b], 0, prob, b)



class Constants:
    def __init__(self, nc, ctx, s, gate_w):
        sb = lambda n, sh, d: ctx.enter_context(nc.sbuf_tensor(n, sh, d))
        self.sem = lambda n: ctx.enter_context(nc.semaphore(n))
        self.gate_w = gate_w
        self.gate = sb("gate", [P, s.KC, PAD], F32)
        self.ident = sb("ident", [P, P], F32)
        self.identb = sb("identb", [P, P], BF16)
        self.ones = sb("ones", [P, P], BF16)
        self.upto = sb("upto", [P, P], BF16)
        self.later = sb("later", [P, P], BF16)
        self.slot = sb("slot", [P, s.CAP], F16)
        self.tok = sb("tok", [P, s.TT], F16)
        self.first = sb("first", [P, s.B, s.SH], F32)
        self.digit_i = sb("digit_i", [P, DIGITS + 2, 3], I32)
        self.digit_f = sb("digit_f", [P, DIGITS + 2], F32)
        self.power = sb("power", [P, s.TT], F32)
        self.blank = self.sem("blank")
        self.made = self.sem("made")
        self.first_made = self.sem("first_made")
        self.gate_blank = self.sem("gate_blank")
        self.gate_in = self.sem("gate_in")
        self.converted = self.sem("converted")
        self.acc_init = self.sem("acc_init")

    MADE = 8

    def patterns(self, s, sb):
        self.slot_i = sb("slot_i", [P, s.CAP], I32)
        self.tok_i = sb("tok_i", [P, s.TT], I32)
        self.first_i = sb("first_i", [P, s.B, s.SH], I32)
        self.shift = sb("shift", [P, DIGITS + 2, 3], I32)
        self.value = sb("value", [P, DIGITS + 2, 3], I32)


def make_constants(nc, c, s, pool):
    pool.memset(c.gate[:], 0.0).then_inc(c.gate_blank, 1)
    pool.memset(c.power[:], -0.5).then_inc(c.first_made, 1)
    pool.memset(c.ident[:], 0.0).then_inc(c.blank, 1)
    pool.wait_ge(c.blank, 1)
    pool.affine_select(out=c.ident[:], in_=c.ident[:], compare_op=ALU.not_equal, fill=1.0, base=0,
                       pattern=[[-1, P]], channel_multiplier=1).then_inc(c.first_made, 1)
    pool.wait_ge(c.first_made, 2)


def make_more_constants(nc, c, s, pool):
    pool.memset(c.identb[:], 0.0).then_inc(c.blank, 1)
    pool.memset(c.upto[:], 1.0).then_inc(c.blank, 1)
    pool.memset(c.later[:], 0.0).then_inc(c.blank, 1)
    pool.memset(c.ones[:], 1.0).then_inc(c.blank, 1)
    pool.iota(c.shift[:, 0:DIGITS, :], pattern=[[-2, DIGITS], [0, 3]], base=2 * (DIGITS - 1), channel_multiplier=0)
    pool.memset(c.shift[:, DIGITS:, :], 0).then_inc(c.made, 1)
    pool.iota(c.value[:], pattern=[[0, DIGITS + 2], [1, 3]], base=1, channel_multiplier=0).then_inc(c.made, 1)
    pool.wait_ge(c.blank, 5)
    pool.affine_select(out=c.identb[:], in_=c.identb[:], compare_op=ALU.not_equal, fill=1.0, base=0,
                       pattern=[[-1, P]], channel_multiplier=1).then_inc(c.made, 1)
    pool.affine_select(out=c.upto[:], in_=c.upto[:], compare_op=ALU.is_ge, fill=0.0, base=0,
                       pattern=[[1, P]], channel_multiplier=-1).then_inc(c.made, 1)
    pool.affine_select(out=c.later[:], in_=c.later[:], compare_op=ALU.is_ge, fill=-4e6, base=0,
                       pattern=[[-1, P]], channel_multiplier=1).then_inc(c.made, 1)
    pool.iota(c.slot_i[:], pattern=[[1, s.CAP]], base=1, channel_multiplier=0).then_inc(c.made, 1)
    pool.iota(c.tok_i[:], pattern=[[P, s.TT]], base=0, channel_multiplier=1).then_inc(c.made, 1)
    pool.iota(c.first_i[:], pattern=[[s.T, s.B], [0, s.SH]], base=0, channel_multiplier=0).then_inc(c.made, 1)


def convert_constants(nc, c, dve):
    dve.tensor_tensor(c.digit_i[:], c.value[:], c.shift[:], ALU.logical_shift_left).then_inc(c.converted, 1)
    dve.wait_ge(c.converted, 1)
    dve.tensor_copy(c.digit_f[:], c.digit_i[:, :, 0]).then_inc(c.converted, 1)
    dve.tensor_copy(c.slot[:], c.slot_i[:]).then_inc(c.converted, 1)
    dve.tensor_copy(c.tok[:], c.tok_i[:]).then_inc(c.converted, 1)
    dve.tensor_copy(c.first[:], c.first_i[:]).then_inc(c.converted, 1)



class Route:

    def __init__(self, nc, s, c, sb, sem, count, run, lists, prob, index):
        self.nc, self.s, self.c, self.prob, self.index = nc, s, c, prob, index
        B, E, TT, BE = s.B, s.E, s.TT, s.BE
        self.thr = sb("thr", [P, BE], I32)
        self.base = sb("base", [P, 3, BE], I32)
        self.trial = sb("trial", [P, 3, BE], I32)
        self.kept = sb("kept", [P, 3, BE], F32)
        self.add = sb("add", [P, BE], I32)
        self.tries = sb("tries", [P, 3, B, TT, E], BF16)
        self.over = sb("over", [P, B, TT, E], BF16)
        self.equal = sb("equal", [P, B, TT, E], BF16)
        self.need = sb("need", [P, BE], F32)
        self.fits = sb("fits", [P, B, TT, E], BF16)
        self.taken = sb("taken", [P, B, TT, E], BF16)
        self.rank = sb("rank", [P, E, B, TT], F32)
        self.hot = sb("hot", [P, 2, TT, s.CAP], F16)
        self.count, self.run, self.lists = count, run, lists
        self.dve, self.tried, self.counted = sem("route_dve"), sem("tried"), sem("counted")
        self.hot_ready, self.listed, self.index_ready = sem("hot_ready"), sem("listed"), sem("index_ready")


def route_search(r, dve):
    s, c = r.s, r.c
    B, TT, E = s.B, s.TT, s.E
    pv = r.prob[:].rearrange("p (b t e) -> p b t e", b=B, t=TT)

    def spread(v):
        return v.rearrange("p (b e) -> p b e", b=B).unsqueeze(2).to_broadcast([P, B, TT, E])

    def compare():
        for m in range(3):
            dve.tensor_tensor(r.tries[:, m], pv, spread(r.trial[:, m, :].bitcast(F32)), ALU.is_ge).then_inc(r.tried, 1)

    def prepare(n):
        steps = c.digit_i[:].rearrange("p d m -> p (d m)")[:, ds(3 * n, 3)]
        chain.did(dve.tensor_tensor(r.base[:], r.thr[:].unsqueeze(1).to_broadcast([P, 3, s.BE]),
                                    steps.unsqueeze(2).to_broadcast([P, 3, s.BE]), ALU.bitwise_or))

    def propose():
        chain.did(dve.tensor_tensor(r.trial[:], r.base[:], r.add[:].unsqueeze(1).to_broadcast([P, 3, s.BE]), ALU.bitwise_or))
        chain.settle()

    chain = Chain(dve, r.dve)
    dve.memset(r.add[:], 0)
    chain.did(dve.memset(r.thr[:], 0))
    chain.settle()
    prepare(0)
    chain.settle()
    propose()
    compare()
    prepare(1)
    ahead, STEPS = chain.n, 5
    with dve.Fori(0, DIGITS // TOGETHER) as i:
        for n in (TOGETHER * i + k for k in range(TOGETHER)):
            chain = Chain(dve, r.dve, ahead + STEPS * n)
            dve.wait_ge(r.counted, n + 1)
            chain.did(dve.tensor_scalar(r.kept[:], r.count, float(s.CAP), c.digit_f[:, ds(n, 1)], ALU.is_ge, ALU.mult))
            chain.settle()
            with r.nc.allow_low_precision(reason="sums of at most three equal powers of two, exact"):
                chain.did(dve.tensor_reduce(r.add[:], r.kept[:].rearrange("p m k -> p k m"), AX.X, ALU.add))
            chain.settle()
            propose()
            compare()
            chain.did(dve.tensor_tensor(r.thr[:], r.thr[:], r.add[:], ALU.bitwise_or))
            chain.settle()
            prepare(n + 2)
            assert chain.n == STEPS
    chain = Chain(dve, r.dve, ahead + STEPS * DIGITS)
    chain.settle()
    dve.wait_ge(r.tried, 3 * (DIGITS + 1))
    dve.tensor_tensor(r.over[:], pv, spread(r.thr[:].bitcast(F32)), ALU.is_gt)
    dve.tensor_tensor(r.equal[:], pv, spread(r.thr[:].bitcast(F32)), ALU.is_equal).then_inc(r.tried, 1)
    dve.wait_ge(r.counted, DIGITS + 1)
    chain.did(dve.tensor_scalar(r.need[:], r.count[:, 0, :], -1.0, float(s.CAP), ALU.mult, ALU.add))
    chain.settle()
    chain.did(dve.tensor_tensor(r.fits[:], r.run.rearrange("p t (b e) -> p b t e", b=B), spread(r.need[:]), ALU.is_le))
    chain.settle()
    chain.did(dve.tensor_tensor(r.taken[:], r.fits[:], r.equal[:], ALU.mult))
    chain.settle()
    dve.tensor_tensor(r.fits[:], r.taken[:], r.over[:], ALU.add).then_inc(r.tried, 1)
    dve.wait_ge(r.counted, DIGITS + 2)
    chain.did(dve.tensor_tensor(r.rank[:].rearrange("p e b t -> p b t e"),
                                r.run.rearrange("p t (b e) -> p b t e", b=B), r.fits[:], ALU.mult))
    chain.settle()


def route_count(r, pe):
    s, c = r.s, r.c

    def totals(out, mask):
        for t in range(s.TT):
            last = pe.matmul(out, c.ones[:], mask(t), start=(t == 0), stop=(t == s.TT - 1))
        return last

    def running(mask):
        for t in range(s.TT):
            for before in range(t):
                pe.matmul(r.run[:, t, :], c.ones[:], mask[:, :, before, :], start=(before == 0), stop=False)
            last = pe.matmul(r.run[:, t, :], c.upto[:], mask[:, :, t, :], start=(t == 0), stop=True)
        return last

    with pe.Fori(0, DIGITS // TOGETHER) as i:
        for n in (TOGETHER * i + k for k in range(TOGETHER)):
            for m in range(3):
                pe.wait_ge(r.tried, 3 * n + m + 1)
                last = totals(r.count[:, m, :], lambda t: r.tries[:, m, :, t, :])
            last.then_inc(r.counted, 1)
    pe.wait_ge(r.tried, 3 * (DIGITS + 1) + 1)
    totals(r.count[:, 0, :], lambda t: r.over[:, :, t, :])
    running(r.equal).then_inc(r.counted, 1)
    pe.wait_ge(r.tried, 3 * (DIGITS + 1) + 2)
    running(r.fits).then_inc(r.counted, 1)


def route_hot(r, dve, u, first, last):
    s = r.s
    for n in range(first, last):
        ins = dve.tensor_scalar(r.hot[:, n // s.TT, n % s.TT, :], r.c.slot[:],
                                r.rank[:].rearrange("p e b t -> p (e b t)")[:, ds(2 * s.TT * u + n, 1)], None, ALU.is_equal)
    if last == 2 * s.TT:
        ins.then_inc(r.hot_ready, 1)


def route_list(r, pe, u, first=False):
    s = r.s
    if not first:
        pe.wait_ge(r.index_ready, u)
    pe.wait_ge(r.hot_ready, u + 1)
    for b in range(2):
        for h in range(s.SH):
            for t in range(s.TT):
                last = pe.matmul(r.lists[:, b * s.SH + h:b * s.SH + h + 1], r.hot[:, b, t, h * P:(h + 1) * P],
                                 r.c.tok[:, t:t + 1], start=(t == 0), stop=(t == s.TT - 1))
    last.then_inc(r.listed, 1)


def route_index(r, dve, u, half):
    s = r.s
    dve.wait_ge(r.listed, u + 1)
    first = r.c.first[:].rearrange("p b h -> p (b h)")[:, half * s.Q:(half + 1) * s.Q]
    dve.tensor_tensor(r.index[:, ds(u * s.Q, s.Q)], r.lists, first, ALU.add).then_inc(r.index_ready, 1)



def experts_block(nc, s, c, w1, w2, table, acc, prob, index, tag):
    J, KC, Q, U, C, H = s.J, s.KC, s.Q, s.U, s.C, s.H
    W = Q * P
    WP = KC * H // J
    FIRST, LOOP = 2, 4
    LOOPS = (U - 2 * FIRST) // LOOP
    TURN_AT = 5
    HOT = 4
    with ExitStack() as ctx:
        sb = lambda n, sh, d: ctx.enter_context(nc.sbuf_tensor(n + tag, sh, d))
        ps = lambda n, sh: ctx.enter_context(nc.psum_tensor(n + tag, sh, F32))
        sem = lambda n: c.sem(n + tag)
        w1_in = sb("w1_in", [P, KC, H], F32)
        w2_in = sb("w2_in", [P, J, C], F32)
        w1_hi, w1_lo = (sb(n, [P, 2, KC, H], F32R) for n in ("w1_hi", "w1_lo"))
        w2_hi, w2_lo = (sb(n, [P, 2, J, C], F32R) for n in ("w2_hi", "w2_lo"))
        rows = sb("rows", [P, 2, Q, s.ROW], F32)
        xT_hi, xT_lo = (sb(n, [P, 2, KC, W], F32R) for n in ("xs_hi", "xs_lo"))
        act_f = sb("act_f", [P, 2, W], F32)
        h_hi, h_lo = (sb(n, [P, 2, J, W], F32R) for n in ("h_hi", "h_lo"))
        gain = sb("gain", [P, 4, Q], F32)
        y = sb("y", [P, 2, Q, C], F32)
        lists = sb("slots", [P, 4, Q], U32)
        turn = ps("turn", [P, KC, BANK])
        up = ps("up", [P, 2, BANK])
        down = ps("down", [P, 2, BANK])
        chosen = ps("chosen", [P, BANK])
        r = Route(nc, s, c, sb, sem, turn[:, 0, 0:3 * s.BE].rearrange("p (m k) -> p m k", m=3),
                  up[:, 0, 0:s.TT * s.BE].rearrange("p (t k) -> p t k", t=s.TT),
                  chosen[:, 0:Q], prob, index)

        w1_loaded, w2_loaded = sem("w1_loaded"), sem("w2_loaded")
        w1_hi_ready, w1_ready = sem("w1_hi_ready"), sem("w1_ready")
        w2_hi_ready, w2_ready = sem("w2_hi_ready"), sem("w2_ready")
        list_ready, pool_steps = sem("list_ready"), sem("pool_steps")
        gathered = [sem(f"gathered{k}") for k in range(2)]
        added = [sem(f"added{k}") for k in range(2)]
        turned, xs_hi_ready, gained = sem("turned"), sem("xs_hi_ready"), sem("gained")
        up_done, h_hi_ready, down_done = sem("up_done"), sem("h_hi_ready"), sem("down_done")
        turn_ring = Ring(sem("xs_ready"), KC)
        up_ring = Ring(sem("gelu_done"), 2)
        act_ring = Ring(sem("h_ready"), 2)
        down_ring = Ring(sem("y_ready"), 2)

        def dma_total(u, k):
            return 8 * Q * (u - k % 2) + 16 * Q

        def added_total(u, k):
            return dma_total(u, k) + 16 * Q

        def splits(u, k):
            return (J // 2) * (u - k % 2) + J

        def expert(u, k):
            return u // 2 if isinstance(u, int) else (u - k % 2) // 2

        def piece(weights_in, hi, lo, k, j):
            flat = lambda v: v.rearrange("p a b -> p (a b)")[:, j * WP:(j + 1) * WP]
            return flat(weights_in[:]), flat(hi[:, k]), flat(lo[:, k])

        def steps(eng, body):
            for u in range(FIRST):
                body(u, u)
            with eng.Fori(0, LOOPS) as i:
                for k in range(LOOP):
                    body(LOOP * i + (FIRST + k), (FIRST + k) % LOOP)
            for u in range(U - FIRST, U):
                body(u, u % LOOP)

        def hold(pool, sem, value):
            pool.wait_ge(sem, value)
            pool.sem_inc(pool_steps, 1)

        def known(u):
            return isinstance(u, int)

        def at_least(u, least):
            return u >= least if isinstance(u, int) else least <= FIRST

        def before(u, end):
            return u < end if isinstance(u, int) else True

        block = ctx.enter_context(nc.Block())

        @block.sync
        def _(sp):
            w1_v = w1.rearrange("e (k p) h -> e p k h", p=P)
            w2_v = w2.rearrange("e (j p) n -> e p j n", p=P)
            sp.dma_start(w1_in[:], w1_v[0]).then_inc(w1_loaded, 16)
            sp.dma_start(w2_in[:], w2_v[0]).then_inc(w2_loaded, 16)
            with sp.Fori(0, s.E - 1) as e:
                sp.wait_ge(w1_ready, J * (e + 1))
                sp.dma_start(w1_in[:], w1_v[e + 1]).then_inc(w1_loaded, 16)
                sp.wait_ge(w2_ready, J * (e + 1))
                sp.dma_start(w2_in[:], w2_v[e + 1]).then_inc(w2_loaded, 16)

        @block.gpsimd
        def _(pool):
            down_ring.start(pool)
            act_ring.start(pool)
            up_ring.start(pool)
            turn_ring.start(pool)

            def gather(u, k, reused=True):
                if at_least(u, 2):
                    pool.wait_ge(added[k % 2], added_total(u - 4, k))
                if at_least(u, 2):
                    pool.sem_inc(pool_steps, 1)
                pool.wait_ge(r.index_ready, u + 1)
                pool.tensor_copy(lists[:, k % 4, :], index[:, ds(u * Q, Q)]).then_inc(list_ready, 1)
                if reused:
                    pool.wait_ge(turned, KC * (u - 1))
                    pool.wait_ge(gained, u - 1)
                hold(pool, list_ready, u + 1)
                for q in range(Q):
                    pool.indirect_dma_start(rows[:, k % 2, q, :], None, table,
                                            bass.IndirectOffsetOnAxis(lists[:, k % 4, q:q + 1], 0)
                                            ).then_inc(gathered[k % 2], 16)

            def add(u, k):
                pool.wait_ge(added[k % 2], added_total(u - 2, k))
                for q in range(Q):
                    hold(pool, down_ring.sem, Q * u + q + 1 + down_ring.depth)
                    pool.indirect_dma_start(acc, bass.IndirectOffsetOnAxis(lists[:, k % 4, q:q + 1], 0),
                                            y[:, k % 2, q, :], None, compute_op=ALU.add
                                            ).then_inc(added[k % 2], 16)

            def body(u, k):
                if at_least(u, 1):
                    add(u - 1, (k - 1) % LOOP)
                if before(u, U - 2):
                    gather(u + 2, (k + 2) % LOOP)

            pool.wait_ge(c.acc_init, 16)
            for k in range(2):
                pool.dma_start(y[:, k, 0, :], acc[0:P, :]).then_inc(added[k], 16 * Q)
                gather(k, k, reused=False)
            steps(pool, body)
            add(U - 1, (U - 1) % LOOP)
            for k in range(2):
                pool.wait_ge(added[k], added_total(U - 2 + k, k))

        @block.tensor
        def _(pe):
            def turn_rows(u, k):
                pe.wait_ge(gathered[k % 2], dma_total(u, k))
                for kc in range(KC):
                    turn_ring.wait_free(pe, KC * u + kc)
                    for q in range(Q):
                        last = pe.transpose(turn[:, kc, q * P:(q + 1) * P],
                                            rows[:, k % 2, q, kc * P:(kc + 1) * P], c.ident[:])
                    last.then_inc(turned, 1)

            def multiply_up(u, k, j):
                b, eb = k % 2, k // 2
                if j == 0:
                    turn_ring.wait_emptied(pe, KC * u + KC - 1)
                    pe.wait_ge(w1_ready, splits(u, k))
                up_ring.wait_free(pe, J * u + j)
                terms = [(w, x, kc) for kc in range(KC)
                         for w, x in ((w1_hi, xT_hi), (w1_hi, xT_lo), (w1_lo, xT_hi))]
                for n, (w, x, kc) in enumerate(terms):
                    last = pe.matmul(up[:, j % 2, :], w[:, eb, kc, j * P:(j + 1) * P], x[:, b, kc, :],
                                     start=(n == 0), stop=(n == len(terms) - 1))
                last.then_inc(up_done, 1)

            def multiply_down(u, k, step):
                b, eb = k % 2, k // 2
                q, part = step // 2, step % 2
                if step == 0:
                    act_ring.wait_emptied(pe, J * u + J - 1)
                    pe.wait_ge(w2_ready, splits(u, k))
                if part == 0:
                    down_ring.wait_free(pe, Q * u + q)
                terms = [(h, w, j) for j in range(J)
                         for h, w in ((h_hi, w2_hi), (h_hi, w2_lo), (h_lo, w2_hi))]
                half = len(terms) // 2
                for n in range(part * half, (part + 1) * half):
                    h, w, j = terms[n]
                    last = pe.matmul(down[:, q % 2, 0:C], h[:, b, j, q * P:(q + 1) * P], w[:, eb, j, :],
                                     start=(n == 0), stop=(n == len(terms) - 1))
                if part == 1:
                    last.then_inc(down_done, 1)

            def body(u, k):
                for j in range(J):
                    multiply_up(u, k, j)
                    if at_least(u, 1):
                        multiply_down(u - 1, (k - 1) % LOOP, j)
                    if j == TURN_AT and before(u, U - 1):
                        turn_rows(u + 1, (k + 1) % LOOP)
                    if j == J - 2 and before(u, U - 2):
                        route_list(r, pe, u + 2)

            route_count(r, pe)
            route_list(r, pe, 0, first=True)
            route_list(r, pe, 1)
            turn_rows(0, 0)
            steps(pe, body)
            for step in range(2 * Q):
                multiply_down(U - 1, (U - 1) % LOOP, step)

        @block.scalar
        def _(act):
            def rows_hi(u, k, reused=True):
                if reused:
                    act.wait_ge(up_done, J * (u - 1))
                for kc in range(KC):
                    act.wait_ge(turned, KC * u + kc + 1)
                    act.activation(xT_hi[:, k % 2, kc, :], turn[:, kc, :], ACT.Copy).then_inc(xs_hi_ready, 1)

            def w1_piece(e, eb, j):
                act.wait_ge(w1_loaded, 16 * (e + 1))
                whole, hi, _ = piece(w1_in, w1_hi, w1_lo, eb, j)
                act.activation(hi, whole, ACT.Copy).then_inc(w1_hi_ready, 1)

            def w2_piece(e, eb, j):
                act.wait_ge(w2_loaded, 16 * (e + 1))
                whole, hi, _ = piece(w2_in, w2_hi, w2_lo, eb, j)
                act.activation(hi, whole, ACT.Copy).then_inc(w2_hi_ready, 1)

            def body(u, k):
                for j in range(J):
                    act.wait_ge(up_done, J * u + j + 1)
                    act_ring.wait_free(act, J * u + j)
                    up_ring.emptied(act.activation(act_f[:, j % 2, :], up[:, j % 2, :], ACT.Gelu))
                    if before(u, U - 2):
                        e = expert(u, k) + 1
                        if k % 2 == 0:
                            w1_piece(e, (k // 2 + 1) % 2, j)
                        else:
                            if j == 0 and at_least(u, 2):
                                act.wait_ge(down_done, Q * (u - 1))
                            w2_piece(e, (k // 2 + 1) % 2, j)
                    if j == TURN_AT and before(u, U - 1):
                        rows_hi(u + 1, (k + 1) % LOOP, reused=at_least(u, 1))

            for j in range(J):
                w1_piece(0, 0, j)
            for j in range(J):
                w2_piece(0, 0, j)
            rows_hi(0, 0, reused=False)
            steps(act, body)

        @block.vector
        def _(dve):
            def rows_lo(u, k, reused=True):
                for kc in range(KC):
                    dve.wait_ge(xs_hi_ready, KC * u + kc + 1)
                    turn_ring.emptied(dve.tensor_tensor(xT_lo[:, k % 2, kc, :], turn[:, kc, :],
                                                        xT_hi[:, k % 2, kc, :].bitcast(F32), ALU.subtract))
                dve.wait_ge(gathered[k % 2], dma_total(u, k))
                if reused:
                    down_ring.wait_emptied(dve, Q * (u - 3) - 1)
                dve.tensor_scalar(gain[:, k, :], rows[:, k % 2, :, ds(C + expert(u, k), 1)].rearrange("p q a -> p (q a)"),
                                  0.5, None, ALU.mult).then_inc(gained, 1)

            def w1_piece(e, eb, j):
                dve.wait_ge(w1_hi_ready, J * e + j + 1)
                whole, hi, lo = piece(w1_in, w1_hi, w1_lo, eb, j)
                dve.tensor_tensor(lo, whole, hi.bitcast(F32), ALU.subtract).then_inc(w1_ready, 1)

            def w2_piece(e, eb, j):
                dve.wait_ge(w2_hi_ready, J * e + j + 1)
                whole, hi, lo = piece(w2_in, w2_hi, w2_lo, eb, j)
                dve.tensor_tensor(lo, whole, hi.bitcast(F32), ALU.subtract).then_inc(w2_ready, 1)

            def scale(u, k, q):
                if q == 0:
                    dve.wait_ge(gained, u + 1)
                    dve.wait_ge(added[k % 2], added_total(u - 2, k))
                dve.wait_ge(down_done, Q * u + q + 1)
                down_ring.emptied(dve.tensor_scalar(y[:, k % 2, q, :], down[:, q % 2, 0:C],
                                                    gain[:, k, q:q + 1], None, ALU.mult))

            def body(u, k):
                for j in range(J):
                    if j == 0 and not (known(u) and u < 2):
                        dve.wait_ge(down_done, Q * (u - 1))
                    up_ring.wait_emptied(dve, J * u + j)
                    dve.tensor_copy(h_hi[:, k % 2, j, :], act_f[:, j % 2, :]).then_inc(h_hi_ready, 1)
                    if before(u, U - 2):
                        if HOT * j < 2 * s.TT:
                            route_hot(r, dve, u + 2, HOT * j, min(HOT * (j + 1), 2 * s.TT))
                        e = expert(u, k) + 1
                        (w1_piece if k % 2 == 0 else w2_piece)(e, (k // 2 + 1) % 2, j)
                    dve.wait_ge(h_hi_ready, J * u + j + 1)
                    act_ring.emptied(dve.tensor_tensor(h_lo[:, k % 2, j, :], act_f[:, j % 2, :],
                                                       h_hi[:, k % 2, j, :].bitcast(F32), ALU.subtract))
                    if at_least(u, 1) and j >= 2 and j % 2 == 0:
                        scale(u - 1, (k - 1) % LOOP, j // 2 - 1)
                    if j == TURN_AT and before(u, U - 1):
                        rows_lo(u + 1, (k + 1) % LOOP, reused=not (known(u) and u < 3))
                if before(u, U - 2):
                    route_index(r, dve, u + 2, k % 2)
                if at_least(u, 1):
                    scale(u - 1, (k - 1) % LOOP, Q - 1)

            route_search(r, dve)
            route_hot(r, dve, 0, 0, 2 * s.TT)
            for j in range(J):
                w1_piece(0, 0, j)
            route_index(r, dve, 0, 0)
            route_hot(r, dve, 1, 0, 2 * s.TT)
            for j in range(J):
                w2_piece(0, 0, j)
            route_index(r, dve, 1, 1)
            rows_lo(0, 0, reused=False)
            steps(dve, body)
            for q in range(Q):
                scale(U - 1, (U - 1) % LOOP, q)



class Segment:

    FILLS = ("x", "qk", "v", "max", "top", "out", "att", "proj", "row", "gate")
    HIGHS = ("x", "qk", "att")

    def __init__(self, steps, before=None):
        self.steps = list(steps)
        fills = [s for s in self.steps if s[0] in self.FILLS]
        highs = [s for s in fills if s[0] in self.HIGHS]
        self.fills, self.highs = len(fills), len(highs)
        self.fill_first = before.fills if before else 0
        self.high_first = before.highs if before else 0
        self.fill_place = {s: k for k, s in enumerate(fills)}
        self.high_place = {s: k for k, s in enumerate(highs)}
        assert len(self.fill_place) == len(fills)


class Banks:

    def __init__(self, seg, ring, filled, highs, per_batch, b):
        self.seg, self.ring, self.filled, self.highs = seg, ring, filled, highs
        assert per_batch[0] % ring.depth == 0, per_batch
        again = (per_batch[0] * b, per_batch[1] * b) if seg.fill_first else (0, 0)
        self.first, self.high_first = seg.fill_first + again[0], seg.high_first + again[1]

    def bank(self, step):
        return (self.seg.fill_first + self.seg.fill_place[step]) % self.ring.depth

    def fill(self, pe, step):
        self.ring.wait_free(pe, self.first + self.seg.fill_place[step])
        return self.bank(step)

    def take(self, eng, step):
        eng.wait_ge(self.filled, self.first + self.seg.fill_place[step] + 1)
        return self.bank(step)

    def wait_emptied(self, eng, step):
        self.ring.wait_emptied(eng, self.first + self.seg.fill_place[step])

    def wait_high(self, eng, step):
        eng.wait_ge(self.highs, self.high_first + self.seg.high_place[step] + 1)


def attention_block(nc, s, c, x1, W1, b1, Wp, bp, x2, table, prob):
    B, T, C, TT, KC = s.B, s.T, s.C, s.TT, s.KC
    NH, G, D = 16, 4, 16
    HG = NH // G
    PART = 3 * D
    ROWS = 4 * D
    STACKING = 16 * 4
    SPILLING = 16 * 5
    VW = D + 1
    HALF = BANK
    HT = HALF // P
    SCALE = 1.0 / D ** 0.5
    NS = 2
    NX = 3
    SETS = [(half, kt) for half in range(2) for kt in range(HT * (half + 1))]
    N = len(SETS)
    LAST = (HT - 1, N - 1)
    def products(tiles):
        return [(h, qt, k0, min(k0 + BANK, (qt + 1) * P)) for h in range(G) for qt in tiles for k0 in range(0, (qt + 1) * P, BANK)]
    EARLY, LATE = products(range(HT)), products(range(HT, TT))
    SIZES = [G * (HALF - max(kt - HT * half, 0) * P + 3 * HALF) for half, kt in SETS[:N - 2]]

    def spread_over(products, sizes):
        ends = [round(len(products) * sum(sizes[:n]) / sum(sizes)) for n in range(len(sizes) + 1)]
        return [products[ends[n]:ends[n + 1]] for n in range(len(sizes))]

    SHARES = spread_over(EARLY, SIZES[:3]) + spread_over(LATE, SIZES[3:])
    assert len(SHARES) == N - 2
    WEIGH_AT = G - 1
    TURNS = [(ch, half) for ch in range(KC) for half in range(2)]
    PAIRS = TT // 2

    def group(g, first=False, ahead=True, nxt=True, tail=False):
        for i in range(N):
            share = SHARES[i] if ahead and i < len(SHARES) else []
            for h in range(G):
                yield "scores", g, i, h
                if h == WEIGH_AT:
                    if i:
                        yield "weigh", g, i - 1
                    elif not first:
                        yield "weigh", g - 1, N - 1
                for m in share[len(share) * h // G:len(share) * (h + 1) // G]:
                    yield ("max", g + 1) + m
            if i == 0 and not first:
                yield "sums", g - 1, 1
            if i == 2 and not first:
                yield "out", g - 1, 1
            if i == HT:
                yield "sums", g, 0
            if i == HT + 2:
                yield "out", g, 0
            if nxt and i in (3, 4):
                yield "qk", g + 2, i - 3
            if nxt and i == 4:
                yield "spill", g + 2
            if nxt and i == 8:
                yield "stack", g + 2, 0
            if ahead and i == 0 and not first:
                yield "stack", g + 1, 1
            if ahead and i == N - 2:
                yield "top", g + 1
            yield "beside", g, i

    def once(steps, beside):
        for s in steps:
            if s[0] == "beside":
                yield from beside.get(s[1:], [])
            else:
                yield s

    X = [("x", ch, half) for ch, half in TURNS]
    VALUES = [("v", n) for n in range(PAIRS)]
    ATT = [("att", ch, half) for ch, half in TURNS]
    PROJ = [("proj", t) for t in range(TT)]
    ROW = [("row", ch, half) for ch, half in TURNS]
    RESIDUAL = {(1, 1): [("residual",)], (2, 0): [("bias",)]}
    NEXT = {(1, 0): [("load",)], (1, 5): [("stats",)], (1, 6): [("norm",)], (1, 8): X[:2], (1, 9): X[2:],
            (3, 6): VALUES[0:1], (3, 8): VALUES[1:2], (3, 10): VALUES[2:3], (4, 0): VALUES[3:]}
    TAIL = {(4, 4): ATT, (4, 5): PROJ[:4], (4, 6): PROJ[4:] + [("send",)], (4, 7): [("gate_stats",)],
            (4, 8): [("rows",)], (4, 9): ROW, (4, 11): [("gate",)]}
    HEAD = Segment([("load",), ("weights",), ("stats",), ("split",), ("norm",)] + X + [("ready",), ("qk", 4, 0), ("qk", 4, 1), ("spill", 4)]
                   + [("stack", 4, 0), ("stack", 4, 1)] + VALUES + [("qk", 5, 0), ("qk", 5, 1), ("spill", 5)]
                   + [("stack", 5, 0), ("stack", 5, 1)] + [("max", 4) + m for m in EARLY + LATE] + [("top", 4)]
                   + list(once(group(4, first=True), {})))
    LOOP = Segment(once([s for g in (1, 2, 3, 4) for s in group(g)], {**RESIDUAL, **NEXT, **TAIL}), HEAD)
    END = Segment(list(once([s for g in (1, 2, 3) for s in group(g, ahead=g < 3, nxt=g < 2)], RESIDUAL))
                  + [("weigh", 3, N - 1), ("sums", 3, 1), ("out", 3, 1)] + ATT + PROJ
                  + [("send",), ("gate_stats",), ("rows",)] + ROW + [("gate",)], HEAD)

    with ExitStack() as ctx:
        sb = lambda n, sh, d: ctx.enter_context(nc.sbuf_tensor(n + "_a", sh, d))
        ps = lambda n, sh: ctx.enter_context(nc.psum_tensor(n + "_a", sh, F32))
        sem = lambda n: c.sem(n + "_a")
        bankA, bankB, bankO = ps("bankA", [P, 3, BANK]), ps("bankB", [P, 4, BANK]), ps("bankO", [P, 1, BANK])
        gsb = lambda n, sh, d: ctx.enter_context(nc.sbuf_tensor(n, sh, d))
        m1 = Moments(s, gsb, c.sem, "_x1")
        g_ = Gate(s, gsb, c.sem, None, None, "_a")
        xin = sb("xin", [P, TT, C], F32)
        xres = sb("xres", [P, TT, C], F32)
        att = sb("att", [P, TT, C], F32)
        xT_hi, xT_lo = sb("aT_hi", [P, KC, T], F32R), sb("aT_lo", [P, KC, T], F32R)
        rT_hi, rT_lo = sb("rT_hi", [P, KC, T], F32R), sb("rT_lo", [P, KC, T], F32R)
        wqk_hi, wqk_lo = (sb(n, [P, KC, HG, P], F32R) for n in ("wqk_hi", "wqk_lo"))
        wv_hi, wv_lo = (sb(n, [P, KC, NH, D], F32R) for n in ("wv_hi", "wv_lo"))
        wp_hi, wp_lo = (sb(n, [P, KC, C], F32R) for n in ("wp_hi", "wp_lo"))
        bqk = sb("bqk", [P, HG], F32)
        bv = sb("bv", [P, NH, D], F32)
        bo = sb("bo", [P, C], F32)
        qk_hi, qk_lo = (sb(n, [P, T], F32R) for n in ("qk_hi", "qk_lo"))
        sq, sk = (sb(n, [P, NS, G, T], F32R) for n in ("sq", "sk"))
        val = sb("val", [P, TT, NH * VW + 16], F32)
        ex = sb("expo", [P, NX, G, BANK], F32)
        oT = sb("oT", [P, T], F32)
        tops = sb("tops", [P, G, TT, 2], F32)
        ntop = sb("ntop", [P, G * TT], F32)
        ntopT = sb("ntopT", [G * TT, P], F32R)
        inv = sb("invs", [P, 2, HT, G], F32)
        q_rows = nc.dram_tensor("q_rows", (NS, 2 * D + 1, G, T), F32).ap()
        k_rows = nc.dram_tensor("k_rows", (NS, 3 * D, G, T), F32).ap()

        A_filled, B_filled, O_filled = sem("A_filled"), sem("B_filled"), sem("O_filled")
        ringA, ringB, ringO = Ring(sem("A_free"), 3), Ring(sem("B_free"), 4), Ring(sem("O_free"), 1)
        w_loaded, w_hi_ready, w_ready, b_loaded, filled, padded, zero_out = (
            sem(n) for n in ("w_loaded", "w_hi_ready", "w_ready", "b_loaded", "filled", "padded", "zero_out"))
        x_loaded, res_loaded, an_ready, hi_ready = (sem(n) for n in ("x_loaded", "res_loaded", "an_ready", "hi_ready"))
        stacked = [[sem(f"stacked{k}{half}") for half in range(2)] for k in range(NS)]
        spilled, top_in = sem("spilled"), [sem(f"top_in{k}") for k in range(NS)]
        ntop_ready, masked, ex_used = (sem(n) for n in ("ntop_ready", "masked", "ex_used"))
        att_dve, sp_steps, pool_steps, biased, x2_ready, x2_out = (
            sem(n) for n in ("att_dve", "sp_steps", "pool_steps", "biased", "x2_ready", "x2_out"))
        DIAG = 2 * HT
        x1_v = x1.rearrange("(b t p) c -> b p t c", b=B, p=P)
        x2_v = x2.rearrange("(b t p) c -> b p t c", b=B, p=P)

        def banks(seg, b):
            return Banks(seg, ringA, A_filled, hi_ready, (LOOP.fills, LOOP.highs), b)

        def nth(g, b):
            return HG * b + g

        def turn_of(g, b):
            return (HG // NS) * b + g // NS + 1

        def cols(i):
            half, kt = SETS[i]
            return max(kt - HT * half, 0) * P

        def crosses(i):
            half, kt = SETS[i]
            return kt + 1 if kt >= HT * half else 0

        def score_bank(g, b, i, h):
            return G * (N * nth(g, b) + i) + h

        def bank_of(i, h):
            return (G * i + h) % 4

        flat = g_.row[:].rearrange("p t r -> p (t r)")
        W1_in = flat[:, 0:KC * PART * NH].rearrange("p (k h r) -> p k h r", k=KC, r=PART)
        Wp_in = flat[:, KC * PART * NH:KC * (PART * NH + C)].rearrange("p (k n) -> p k n", k=KC)
        SPLITS = [(W1_in[:, k, :, part * D:(part + 1) * D].rearrange("p (a g) r -> p a g r", g=G),
                   *(w[:, k, :, part * G * D:(part + 1) * G * D].rearrange("p a (g r) -> p a g r", g=G)
                     for w in (wqk_hi, wqk_lo)))
                  for k in range(KC) for part in range(2)]
        SPLITS += [(W1_in[:, k, :, 2 * D:PART], wv_hi[:, k], wv_lo[:, k]) for k in range(KC)]
        SPLITS += [(Wp_in[:, k], wp_hi[:, k], wp_lo[:, k]) for k in range(KC)]
        BIASES = 2 * HG + 2
        block = ctx.enter_context(nc.Block())

        @block.sync
        def _(sp):
            def walk(seg, b):
                A = banks(seg, b)
                for step in seg.steps:
                    kind, a = step[0], step[1:]
                    if kind == "load":
                        sp.dma_start(xin[:], x1_v[b + 1]).then_inc(x_loaded, 16)
                    elif kind == "weights":
                        sp.dma_start(W1_in.rearrange("p k h r -> p k (h r)"), W1.rearrange("(k p) n -> p k n", p=P)).then_inc(w_loaded, 16)
                        sp.dma_start(Wp_in, Wp.rearrange("(k p) n -> p k n", p=P)).then_inc(w_loaded, 16)
                        with nc.allow_non_contiguous_dma(reason="biases, a few hundred bytes each"):
                            for a in range(HG):
                                for part in range(2):
                                    sp.dma_start(bqk[part * G * D:(part + 1) * G * D, a:a + 1],
                                                 b1.rearrange("(a g s r) -> a s g r", a=HG, g=G, r=D)[a, part].unsqueeze(2)).then_inc(b_loaded, 16)
                            sp.dma_start(bv[:], b1.rearrange("(h r) -> h r", h=NH)[:, 2 * D:PART].unsqueeze(0).to_broadcast([P, NH, D])
                                         ).then_inc(b_loaded, 16)
                            sp.dma_start(bo[:], bp.unsqueeze(0).to_broadcast([P, C])).then_inc(b_loaded, 16)
                    elif kind == "ready":
                        sp.wait_ge(filled, 1)
                        for k in range(NS):
                            sp.dma_start(q_rows[k, 2 * D:2 * D + 1], sq[ROWS:ROWS + 1, k, :, :].bitcast(F32)).then_inc(zero_out, 16)
                        sp.wait_ge(zero_out, 16 * NS)
                    elif kind == "residual":
                        sp.wait_ge(x2_out, 16 * (b + 1))
                        sp.sem_inc(sp_steps, 1)
                        sp.dma_start(xres[:], x1_v[b]).then_inc(res_loaded, 16)
                    elif kind == "spill":
                        g, k = a[0], a[0] % NS
                        A.wait_emptied(sp, ("qk", g, 1))
                        sp.sem_inc(sp_steps, 1)
                        if seg is not HEAD or g > 5:
                            for half in range(2):
                                sp.wait_ge(stacked[k][half], STACKING * turn_of(g - 2, b))
                                sp.sem_inc(sp_steps, 1)
                        for row, rows, part, first in ((0, q_rows, qk_hi, 0), (D, q_rows, qk_lo, 0), (0, k_rows, qk_hi, G * D),
                                                       (D, k_rows, qk_lo, G * D), (2 * D, k_rows, qk_hi, G * D)):
                            sp.dma_start(rows[k, row:row + D].rearrange("r h t -> h r t"),
                                         part[first:first + G * D, :].bitcast(F32)).then_inc(spilled, 16)
                    elif kind == "stack":
                        g, half = a
                        k, cut = g % NS, slice(half * HALF, (half + 1) * HALF)
                        sp.wait_ge(spilled, SPILLING * (nth(g, b) + 1))
                        sp.sem_inc(sp_steps, 1)
                        if (seg is not HEAD) or g > 5:
                            sp.wait_ge(ex_used, N * nth(g - 2, b) + (2 * HT if half == 0 else N))
                        for row, stack, rows, first, n in ((0, sq, q_rows, 0, 2 * D), (2 * D, sq, q_rows, 0, 2 * D + 1),
                                                           (0, sk, k_rows, 0, 2 * D), (2 * D, sk, k_rows, D, 2 * D)):
                            sp.dma_start(stack[row:row + n, k, :, cut].bitcast(F32),
                                         rows[k, first:first + n, :, cut]).then_inc(stacked[k][half], 16)
                    elif kind == "top":
                        g, k = a[0], a[0] % NS
                        A.wait_emptied(sp, step)
                        sp.dma_start(sq[ROWS:ROWS + 1, k, :, :].bitcast(F32).rearrange("p g (t q) -> p (g t) q", q=P),
                                     ntopT[:].bitcast(F32)).then_inc(top_in[k], 16)
                    elif kind == "send":
                        sp.wait_ge(x2_ready, b + 1)
                        sp.dma_start(x2_v[b], xres[:]).then_inc(x2_out, 16)
                    elif kind == "gate":
                        gate_table(g_, sp, b, table, b)

            for r in (ringA, ringB, ringO):
                r.start(sp)
            sp.sem_inc(g_.table_out, 16)
            sp.sem_inc(x2_out, 16)
            walk(HEAD, -1)
            with sp.Fori(0, B - 1) as b:
                walk(LOOP, b)
            walk(END, B - 1)
            sp.wait_ge(x2_out, 16 * (B + 1))
            sp.wait_ge(g_.table_out, 16 * (B + 1))

        @block.gpsimd
        def _(pool):
            def walk(seg, b):
                for step in seg.steps:
                    kind, a = step[0], step[1:]
                    if kind == "stats":
                        gate_rstd(m1, pool, b + 1, c.power)
                    elif kind == "split":
                        pool.wait_ge(m1.rstd_ready, 1)
                        pool.memset(sq[ROWS:P, :, :, :].bitcast(F32), 0.0).then_inc(filled, 1)
                        pool.wait_ge(filled, 1)
                        pool.memset(sk[ROWS:P, :, :, :].bitcast(F32), 1.0).then_inc(filled, 1)
                        pool.wait_ge(filled, 2)
                        pool.wait_ge(b_loaded, 16 * BIASES)
                    elif kind == "gate_stats":
                        gate_rstd(g_, pool, b, c.power)
                    elif kind == "bias":
                        pool.wait_ge(res_loaded, 16 * (b + 1))
                        pool.tensor_tensor(xres[:], xres[:], bo[:].unsqueeze(1).to_broadcast([P, TT, C]), ALU.add).then_inc(biased, 1)
                    elif kind == "weigh" and crosses(a[1]):
                        g, i = a
                        ringB.wait_emptied(pool, score_bank(g, b, i, G - 1))
                        pool.sem_inc(pool_steps, 1)
                        pool.affine_select(out=ex[:, i % NX, :, 0:P], in_=ex[:, i % NX, :, 0:P], compare_op=ALU.is_ge,
                                           fill=0.0, base=0, pattern=[[0, G], [1, P]],
                                           channel_multiplier=-1).then_inc(masked, 1)

            walk(HEAD, -1)
            with pool.Fori(0, B - 1) as b:
                walk(LOOP, b)
            walk(END, B - 1)

        @block.tensor
        def _(pe):
            def split3(out, lhs, rhs, n, last):
                pe.matmul(out, lhs[0], rhs[0], start=(n == 0), stop=False)
                pe.matmul(out, lhs[0], rhs[1], start=False, stop=False)
                return pe.matmul(out, lhs[1], rhs[0], start=False, stop=last)

            def rows_by(bank, xs, ws, t):
                for ch in range(KC):
                    cut = slice(t * P, (t + 1) * P)
                    last = split3(bank, (xs[0][:, ch, cut], xs[1][:, ch, cut]), (ws[0][:, ch], ws[1][:, ch]), ch, ch == KC - 1)
                return last

            def walk(seg, b):
                A = banks(seg, b)
                for step in seg.steps:
                    kind, a = step[0], step[1:]
                    if kind in ("x", "att", "row"):
                        src = {"x": xin, "att": att, "row": g_.row}[kind]
                        ch, half = a
                        if a == TURNS[0]:
                            if kind == "x":
                                pe.wait_ge(an_ready, b + 2)
                            elif kind == "att":
                                A.wait_emptied(pe, ("out", 3, 1))
                            else:
                                pe.wait_ge(g_.row_ready, b + 1)
                        k = A.fill(pe, step)
                        for t in range(HT):
                            last = pe.transpose(bankA[:, k, t * P:(t + 1) * P],
                                                src[:, HT * half + t, ch * P:(ch + 1) * P], c.ident[:])
                        last.then_inc(A_filled, 1)
                    elif kind == "ready":
                        pe.wait_ge(w_ready, len(SPLITS))
                    elif kind == "qk":
                        g, half = a
                        if seg is HEAD and g == 4:
                            A.wait_emptied(pe, X[-1])
                        k = A.fill(pe, step)
                        for ch in range(KC):
                            cut = slice(half * HALF, (half + 1) * HALF)
                            last = split3(bankA[:, k, :], (wqk_hi[:, ch, g % HG, :], wqk_lo[:, ch, g % HG, :]),
                                          (xT_hi[:, ch, cut], xT_lo[:, ch, cut]), ch, ch == KC - 1)
                        last.then_inc(A_filled, 1)
                    elif kind == "v":
                        k = A.fill(pe, step)
                        for n in range(2):
                            last = rows_by(bankA[:, k, n * C:(n + 1) * C], (xT_hi, xT_lo), (wv_hi, wv_lo), 2 * a[0] + n)
                        last.then_inc(A_filled, 1)
                    elif kind == "proj":
                        if a[0] == 0:
                            A.wait_emptied(pe, ATT[-1])
                        k = A.fill(pe, step)
                        rows_by(bankA[:, k, 0:C], (rT_hi, rT_lo), (wp_hi, wp_lo), a[0]).then_inc(A_filled, 1)
                    elif kind == "max":
                        g, h, qt, k0, k1 = a
                        for half, first in ((0, EARLY[0]), (1, LATE[0])):
                            if a[1:] == first:
                                pe.wait_ge(stacked[g % NS][half], STACKING * turn_of(g, b))
                        if seg is HEAD and a == (4,) + EARLY[0]:
                            pe.wait_ge(filled, 2)
                            pe.wait_ge(padded, 2)
                        k = A.fill(pe, step)
                        crossing = k1 == (qt + 1) * P
                        last = pe.matmul(bankA[:, k, 0:k1 - k0], sq[:, g % NS, h, qt * P:(qt + 1) * P],
                                         sk[:, g % NS, h, k0:k1], start=True, stop=not crossing)
                        if crossing:
                            last = pe.matmul(bankA[:, k, k1 - k0 - P:k1 - k0], c.identb[:], c.later[:], start=False, stop=True)
                        last.then_inc(A_filled, 1)
                    elif kind == "top":
                        pe.wait_ge(ntop_ready, nth(a[0], b) + 1)
                        k = A.fill(pe, step)
                        pe.transpose(bankA[0:G * TT, k, 0:P], ntop[:], c.ident[:]).then_inc(A_filled, 1)
                    elif kind == "scores":
                        g, i, h = a
                        if i == 0 and h == 0:
                            pe.wait_ge(top_in[g % NS], 16 * turn_of(g, b))
                        half, kt = SETS[i]
                        q0 = half * HALF + cols(i)
                        ringB.wait_free(pe, score_bank(g, b, i, h))
                        pe.matmul(bankB[:, bank_of(i, h), 0:HALF - cols(i)], sk[:, g % NS, h, kt * P:(kt + 1) * P],
                                  sq[:, g % NS, h, q0:(half + 1) * HALF], start=True, stop=True).then_inc(B_filled, 1)
                    elif kind == "weigh":
                        g, i = a
                        half, kt = SETS[i]
                        ringB.wait_emptied(pe, score_bank(g, b, i, G - 1))
                        if crosses(i):
                            pe.wait_ge(masked, DIAG * nth(g, b) + crosses(i))
                        if kt == 0:
                            ringO.wait_free(pe, 2 * nth(g, b) + half)
                        for h in range(G):
                            v0 = VW * (g % HG * G + h)
                            last = pe.matmul(bankO[32 * h:32 * (h + 1), 0, cols(i):HALF], val[:, kt, v0:v0 + 32],
                                             ex[:, i % NX, h, 0:HALF - cols(i)], start=(kt == 0), stop=(i == LAST[half]))
                        last.then_inc(ex_used, 1)
                    elif kind == "out":
                        g, half = a
                        ringO.wait_emptied(pe, 2 * nth(g, b) + half)
                        k = A.fill(pe, step)
                        for t in range(HT):
                            q0 = half * HALF + t * P
                            last = pe.transpose(bankA[:, k, t * P:(t + 1) * P], oT[:, q0:q0 + P], c.ident[:])
                        last.then_inc(A_filled, 1)
                    elif kind == "gate":
                        A.wait_emptied(pe, ROW[-1])
                        k = A.fill(pe, step)
                        gate_score(g_, pe, c.gate, bankA[:, k, 0:2 * P])
                        gate_score_turn(g_, pe, b, bankA[:, k, 2 * P:4 * P], c.ident).then_inc(A_filled, 1)

            walk(HEAD, -1)
            with pe.Fori(0, B - 1) as b:
                walk(LOOP, b)
            walk(END, B - 1)

        @block.scalar
        def _(act):
            def walk(seg, b):
                A = banks(seg, b)
                for step in seg.steps:
                    kind, a = step[0], step[1:]
                    if kind == "weights":
                        act.wait_ge(w_loaded, 32)
                        for whole, hi, _ in SPLITS:
                            act.activation(hi, whole, ACT.Copy).then_inc(w_hi_ready, 1)
                        act.wait_ge(b_loaded, 16 * BIASES)
                    elif kind in ("x", "att"):
                        k = A.take(act, step)
                        ch, half = a
                        to = xT_hi if kind == "x" else rT_hi
                        act.activation(to[:, ch, half * HALF:(half + 1) * HALF], bankA[:, k, :], ACT.Copy).then_inc(hi_ready, 1)
                    elif kind == "qk":
                        g, half = a
                        k = A.take(act, step)
                        if half == 0 and not (seg is HEAD and g == 4):
                            act.wait_ge(spilled, SPILLING * nth(g, b))
                        act.activation(qk_hi[:, half * HALF:(half + 1) * HALF], bankA[:, k, :], ACT.Identity,
                                       bias=bqk[:, g % HG:g % HG + 1]).then_inc(hi_ready, 1)
                    elif kind == "scores":
                        g, i, h = a
                        act.wait_ge(B_filled, score_bank(g, b, i, h) + 1)
                        if h == 0 and not (seg is HEAD and i < NX):
                            act.wait_ge(ex_used, N * nth(g, b) + i - NX + 1)
                        ringB.emptied(act.activation(ex[:, i % NX, h, 0:HALF - cols(i)],
                                                     bankB[:, bank_of(i, h), 0:HALF - cols(i)], ACT.Exp, scale=SCALE))
                    elif kind == "sums":
                        g, half = a
                        act.wait_ge(ex_used, N * nth(g, b) + LAST[half] + 1)
                        ringO.emptied(act.activation(oT[:, half * HALF:(half + 1) * HALF], bankO[:, 0, :], ACT.Copy))
                    elif kind == "gate":
                        A.wait_emptied(act, step)
                        act.activation(g_.ex[:], g_.sub[:], ACT.Exp).then_inc(g_.ex_ready, 1)

            walk(HEAD, -1)
            with act.Fori(0, B - 1) as b:
                walk(LOOP, b)
            walk(END, B - 1)

        @block.vector
        def _(dve):
            def walk(seg, b):
                A = banks(seg, b)
                norm = Chain(dve, m1.dve, Moments.DVE_STEPS * (b + 1))
                gate = Chain(dve, g_.dve, Gate.DVE_STEPS * b)
                for step in seg.steps:
                    kind, a = step[0], step[1:]
                    if kind == "split":
                        for n, (whole, hi, lo) in enumerate(SPLITS):
                            dve.wait_ge(w_hi_ready, n + 1)
                            dve.tensor_tensor(lo, whole, hi.bitcast(F32), ALU.subtract).then_inc(w_ready, 1)
                        dve.memset(tops[:], -3e38).then_inc(padded, 1)
                        dve.memset(val[:], 1.0).then_inc(padded, 1)
                        dve.wait_ge(padded, 2)
                        dve.wait_ge(w_ready, len(SPLITS))
                    elif kind == "stats":
                        dve.wait_ge(x_loaded, 16 * (b + 2))
                        gate_stats(m1, dve, norm, xin)
                    elif kind == "norm":
                        dve.wait_ge(m1.rstd_ready, b + 2)
                        for t in range(TT):
                            last = dve.tensor_scalar(xin[:, t, :], xin[:, t, :], m1.mv[:, t, 0:1], m1.rstd[:, t:t + 1],
                                                     ALU.subtract, ALU.mult)
                        last.then_inc(an_ready, 1)
                    elif kind in ("x", "att"):
                        ch, half = a
                        hi, lo = (xT_hi, xT_lo) if kind == "x" else (rT_hi, rT_lo)
                        cut = slice(half * HALF, (half + 1) * HALF)
                        A.wait_high(dve, step)
                        ringA.emptied(dve.tensor_tensor(lo[:, ch, cut], bankA[:, A.bank(step), :], hi[:, ch, cut].bitcast(F32),
                                                        ALU.subtract))
                    elif kind == "qk":
                        g, half = a
                        cut = slice(half * HALF, (half + 1) * HALF)
                        A.wait_high(dve, step)
                        ringA.emptied(dve.scalar_tensor_tensor(qk_lo[:, cut], bankA[:, A.bank(step), :], bqk[:, g % HG:g % HG + 1],
                                                               qk_hi[:, cut].bitcast(F32), ALU.add, ALU.subtract))
                    elif kind == "v":
                        k = A.take(dve, step)
                        ringA.emptied(dve.tensor_tensor(
                            val[:, 2 * a[0]:2 * a[0] + 2, 0:NH * VW].rearrange("p n (h w) -> p n h w", w=VW)[:, :, :, 0:D],
                            bankA[:, k, :].rearrange("p (n h d) -> p n h d", n=2, d=D),
                            bv[:].unsqueeze(1).to_broadcast([P, 2, NH, D]), ALU.add))
                    elif kind == "max":
                        g, h, qt, k0, k1 = a
                        k = A.take(dve, step)
                        ringA.emptied(dve.tensor_reduce(tops[:, h, qt, k0 // BANK:k0 // BANK + 1], bankA[:, k, 0:k1 - k0],
                                                        AX.X, ALU.max))
                        if a[1:] == LATE[-1]:
                            A.wait_emptied(dve, step)
                            dve.tensor_reduce(ntop[:].rearrange("p (g t) -> p g t", g=G), tops[:], AX.X, ALU.max,
                                              negate=True).then_inc(ntop_ready, 1)
                    elif kind == "top":
                        k = A.take(dve, step)
                        g = a[0]
                        if not (seg is HEAD and g == 4):
                            dve.wait_ge(top_in[(g - 1) % NS], 16 * turn_of(g - 1, b))
                        ringA.emptied(dve.tensor_copy(ntopT[:], bankA[0:G * TT, k, 0:P]))
                    elif kind == "out":
                        g, half = a
                        k = A.take(dve, step)
                        sums = bankA[:, k, :].rearrange("p (t g d) -> p t g d", t=HT, g=G)
                        dve.reciprocal(inv[:, half].unsqueeze(3), sums[:, :, :, D:D + 1]).then_inc(att_dve, 1)
                        dve.wait_ge(att_dve, 2 * nth(g, b) + half + 1)
                        to = att[:, HT * half:HT * (half + 1), g % HG * G * D:(g % HG + 1) * G * D]
                        ringA.emptied(dve.tensor_tensor(to.rearrange("p t (g d) -> p t g d", g=G), sums[:, :, :, 0:D],
                                                        inv[:, half].unsqueeze(3).to_broadcast([P, HT, G, D]), ALU.mult))
                    elif kind == "proj":
                        if a[0] == 0:
                            dve.wait_ge(biased, b + 1)
                        k = A.take(dve, step)
                        ringA.emptied(dve.tensor_tensor(xres[:, a[0], :], bankA[:, k, 0:C], xres[:, a[0], :], ALU.add))
                    elif kind == "send":
                        A.wait_emptied(dve, PROJ[-1])
                        dve.sem_inc(x2_ready, 1)
                    elif kind == "gate_stats":
                        gate_stats(g_, dve, gate, xres)
                    elif kind == "rows":
                        gate_rows(g_, dve, b, xres)
                    elif kind == "row":
                        k = A.take(dve, step)
                        ringA.emptied(dve.tensor_copy(g_.xT[:, a[0], a[1] * HALF:(a[1] + 1) * HALF], bankA[:, k, :]))
                    elif kind == "gate":
                        k = A.bank(step)
                        gate_score_copy(g_, dve, b, bankA[:, k, 0:2 * P])
                        A.take(dve, step)
                        ringA.emptied(gate_softmax_front(g_, dve, gate, bankA[:, k, 2 * P:4 * P]))
                        gate_softmax_back(g_, dve, gate, b, prob, b)
                assert norm.n in (0, Moments.DVE_STEPS) and gate.n in (0, Gate.DVE_STEPS)

            walk(HEAD, -1)
            with dve.Fori(0, B - 1) as b:
                walk(LOOP, b)
            walk(END, B - 1)



def macaron_layer(nc, x, W1, b1, Wp, bp, gate_w, w1, w2, out):
    s = Shapes(x, gate_w, w1)
    with ExitStack() as ctx:
        c = Constants(nc, ctx, s, gate_w)
        prob = ctx.enter_context(nc.sbuf_tensor("prob", [P, s.BE * s.TT], F32))
        index = ctx.enter_context(nc.sbuf_tensor("index", [P, s.E * s.ST], U32))
        table = nc.dram_tensor("table", (s.B * s.T, s.ROW), F32).ap()
        x1 = nc.dram_tensor("x1", (s.B * s.T, s.C), F32).ap()
        x2 = out.rearrange("b t c -> (b t) c")
        norm_block(nc, s, c, x, table, x1, prob)
        experts_block(nc, s, c, w1, w2, table, x1, prob, index, "_1")
        attention_block(nc, s, c, x1, W1, b1, Wp, bp, x2, table, prob)
        experts_block(nc, s, c, w1, w2, table, x2, prob, index, "_2")


_INS = ["L0_attn_x", "L0_attn_W1", "L0_attn_b1", "L0_attn_Wp", "L0_attn_bp", "L0_ffn_gate_w", "L0_ffn_w1", "L0_ffn_w2"]
_OUTS = [((4, 1024, 256), "float32")]


def kernel(**inputs):
    import numpy as _np
    import concourse.bacc as _bacc
    from concourse import mybir as _mybir
    from concourse.bass_utils import run_bass_kernel_spmd as _run

    nc = _bacc.Bacc("TRN2", target_bir_lowering=False, num_devices=1)
    arrays, args = {}, []
    for name in _INS:
        a = _np.ascontiguousarray(inputs[name])
        arrays[f"in_{name}_dram"] = a
        args.append(nc.dram_tensor(f"in_{name}_dram", a.shape, _mybir.dt.from_np(a.dtype), kind="ExternalInput").ap())
    for i, (shape, dtype) in enumerate(_OUTS):
        dt = _mybir.dt.from_np(_np.dtype(dtype))
        args.append(nc.dram_tensor(f"out_{i}_dram", shape, dt, kind="ExternalOutput").ap())
    macaron_layer(nc, *args)
    r = _run(nc, [arrays], core_ids=[0])
    got = tuple(r.results[0][f"out_{i}_dram"] for i in range(len(_OUTS)))
    return got[0]
```
